# Optimizing a Trainium2 kernel written in Bass

```python
import numpy as np
import jax
import jax.numpy as jnp

def _softmax(x, axis=-1):
    return jax.nn.softmax(x, axis=axis)

def _gelu(x):
    return jax.nn.gelu(x, approximate=True)

def _silu(x):
    return jax.nn.silu(x)

def _sigmoid(x):
    return jax.nn.sigmoid(x)

def _layernorm(x, axis=-1, eps=1e-05):
    m = jnp.mean(x, axis=axis, keepdims=True)
    v = jnp.var(x, axis=axis, keepdims=True)
    return (x - m) / jnp.sqrt(v + eps)

def _scatter_add(tgt, idx, src, axis=0):
    return tgt.at[idx].add(src)

def _segment_sum(src, seg, n):
    return jax.ops.segment_sum(src, seg, n)
kernel_name = 'mk_recurrent_d4_jaxref_r8_d4bd1c'

def setup_inputs(seed: int=0):
    np.random.seed(seed)
    _w = jnp.asarray

    def _L0_attn_setup():
        import jax, jax.numpy as jnp
        import numpy as np
        N_HEAD = 16
        CHUNK = 128

        def _phi(x):
            return jax.nn.elu(x) + 1.0

        def _causal_linear_attn(qp, kp, v):
            B, H, T, D = qp.shape
            NC = T // CHUNK

            def to_chunks(a):
                return a.reshape(B, H, NC, CHUNK, D).transpose(2, 0, 1, 3, 4)
            qc, kc, vc = (to_chunks(qp), to_chunks(kp), to_chunks(v))
            mask = jnp.tril(jnp.ones((CHUNK, CHUNK), dtype=bool))

            def step(carry, blk):
                S, z = carry
                q_c, k_c, v_c = blk
                scores = jnp.einsum('bhcd,bhkd->bhck', q_c, k_c)
                scores = jnp.where(mask, scores, 0.0)
                num = jnp.einsum('bhck,bhke->bhce', scores, v_c) + jnp.einsum('bhcd,bhde->bhce', q_c, S)
                den = scores.sum(-1) + jnp.einsum('bhcd,bhd->bhc', q_c, z)
                S = S + jnp.einsum('bhkd,bhke->bhde', k_c, v_c)
                z = z + k_c.sum(axis=2)
                return ((S, z), (num, den))
            S0 = jnp.zeros((B, H, D, D), dtype=qp.dtype)
            z0 = jnp.zeros((B, H, D), dtype=qp.dtype)
            _, (num, den) = jax.lax.scan(step, (S0, z0), (qc, kc, vc))
            y = num / (den[..., None] + 1e-06)
            y = y.transpose(1, 2, 0, 3, 4).reshape(B, H, T, D)
            return y
        key = jax.random.key(seed)
        k1, k2, k3 = jax.random.split(key, 3)
        B, T, E = (4, 256, 128)
        x = jax.random.normal(k1, (B, T, E), dtype=jnp.float32)
        w_attn = jax.random.normal(k2, (3 * E, E), dtype=jnp.float32) * 0.02
        w_proj = jax.random.normal(k3, (E, E), dtype=jnp.float32) * 0.02
        return {'x': x, 'w_attn': w_attn, 'w_proj': w_proj}
    _L0_attn_in = _L0_attn_setup()

    def _L0_ffn_setup():
        import jax, jax.numpy as jnp
        import numpy as np
        B, S, D = (2, 64, 128)
        E, K, I = (16, 8, 128)
        I_SH = 128
        ROUTE_SCALE = 2.826
        key = jax.random.key(seed)
        ks = jax.random.split(key, 8)
        s = 0.02
        return {'x': jax.random.normal(ks[0], (B, S, D), dtype=jnp.float32), 'gate_w': jax.random.normal(ks[1], (E, D), dtype=jnp.float32) * s, 'expert_bias': jnp.zeros((E,), dtype=jnp.float32), 'w_gate': jax.random.normal(ks[2], (E, I, D), dtype=jnp.float32) * s, 'w_up': jax.random.normal(ks[3], (E, I, D), dtype=jnp.float32) * s, 'w_down': jax.random.normal(ks[4], (E, D, I), dtype=jnp.float32) * s, 'shared_gate_w': jax.random.normal(ks[5], (I_SH, D), dtype=jnp.float32) * s, 'shared_up_w': jax.random.normal(ks[6], (I_SH, D), dtype=jnp.float32) * s, 'shared_down_w': jax.random.normal(ks[7], (D, I_SH), dtype=jnp.float32) * s}
    _L0_ffn_in = _L0_ffn_setup()

    def _L1_attn_setup():
        import jax, jax.numpy as jnp
        import numpy as np
        B, S, D, H = (2, 256, 128, 16)
        HD = D // H
        key = jax.random.key(seed)
        k0, k1, k2 = jax.random.split(key, 3)
        return {'x': jax.random.normal(k0, (B, S, D), jnp.float32), 'qkv_w': jax.random.normal(k1, (D, 3 * D), jnp.float32) / np.sqrt(D).astype(np.float32), 'qkv_b': jnp.zeros((3 * D,), jnp.float32), 'out_w': jax.random.normal(k2, (D, D), jnp.float32) / np.sqrt(D).astype(np.float32), 'out_b': jnp.zeros((D,), jnp.float32)}
    _L1_attn_in = _L1_attn_setup()

    def _L1_ffn_setup():
        import jax, jax.numpy as jnp
        import numpy as np
        B, T, D = (2, 256, 128)
        F = 512
        E = 8
        key = jax.random.key(seed)
        k0, k1, k2, k3 = jax.random.split(key, 4)
        x = jax.random.normal(k0, (B, T, D), dtype=jnp.float32)
        Wg = jax.random.normal(k1, (E, D), dtype=jnp.float32) * 0.02
        W1 = jax.random.normal(k2, (E, D, F), dtype=jnp.float32) * 0.02
        W2 = jax.random.normal(k3, (E, F, D), dtype=jnp.float32) * 0.02
        return {'x': x, 'Wg': Wg, 'W1': W1, 'W2': W2}
    _L1_ffn_in = _L1_ffn_setup()

    def _L2_attn_setup():
        import jax, jax.numpy as jnp
        import numpy as np
        NUM_HEADS = 16
        EPS = 1e-05
        CHUNK = 128

        def _linear_attention(x, Wq, Wk, Wv, Wo, bo):
            B, T, E = x.shape
            H = NUM_HEADS
            d = E // H

            def proj(W):
                return (x @ W.T).reshape(B, T, H, d).transpose(0, 2, 1, 3)
            phi_q = jax.nn.elu(proj(Wq)) + 1.0
            phi_k = jax.nn.elu(proj(Wk)) + 1.0
            V = proj(Wv)
            nC = T // CHUNK

            def to_chunks(a):
                return a.reshape(B, H, nC, CHUNK, d).transpose(2, 0, 1, 3, 4)
            qc, kc, vc = (to_chunks(phi_q), to_chunks(phi_k), to_chunks(V))
            mask = jnp.tril(jnp.ones((CHUNK, CHUNK), x.dtype))
            S0 = jnp.zeros((B, H, d, d), x.dtype)
            z0 = jnp.zeros((B, H, d), x.dtype)

            def step(carry, inp):
                S, z = carry
                q, k, v = inp
                A = jnp.einsum('bhid,bhjd->bhij', q, k) * mask
                num = jnp.einsum('bhij,bhjd->bhid', A, v) + jnp.einsum('bhid,bhde->bhie', q, S)
                den = jnp.sum(A, axis=-1) + jnp.einsum('bhid,bhd->bhi', q, z) + EPS
                out = num / den[..., None]
                S = S + jnp.einsum('bhjd,bhje->bhde', k, v)
                z = z + jnp.sum(k, axis=2)
                return ((S, z), out)
            _, outs = jax.lax.scan(step, (S0, z0), (qc, kc, vc))
            out = outs.transpose(1, 2, 0, 3, 4).reshape(B, H, T, d)
            out = out.transpose(0, 2, 1, 3).reshape(B, T, E)
            return out @ Wo.T + bo
        key = jax.random.key(seed)
        ks = jax.random.split(key, 6)
        B, T, E = (2, 256, 128)
        s = 1.0 / np.sqrt(E)
        return {'x': jax.random.normal(ks[0], (B, T, E), jnp.float32), 'Wq': jax.random.normal(ks[1], (E, E), jnp.float32) * s, 'Wk': jax.random.normal(ks[2], (E, E), jnp.float32) * s, 'Wv': jax.random.normal(ks[3], (E, E), jnp.float32) * s, 'Wo': jax.random.normal(ks[4], (E, E), jnp.float32) * s, 'bo': jnp.zeros((E,), jnp.float32)}
    _L2_attn_in = _L2_attn_setup()

    def _L2_ffn_setup():
        import jax, jax.numpy as jnp
        import numpy as np
        EPS = 1e-06
        LN_EPS = 1e-05

        def _absmean_core(W):
            gamma = jnp.mean(jnp.abs(W)) + EPS
            Ws = W / gamma
            Wq = jnp.sign(Ws) * jnp.minimum(jnp.round(jnp.abs(Ws)), 1.0)
            return (Wq, gamma)

        @jax.custom_vjp
        def absmean(W):
            return _absmean_core(W)[0]

        def _absmean_fwd(W):
            Wq, gamma = _absmean_core(W)
            return (Wq, gamma)

        def _absmean_bwd(gamma, g):
            return (g / gamma,)
        absmean.defvjp(_absmean_fwd, _absmean_bwd)

        def layernorm(x, w, b, eps=LN_EPS):
            mu = jnp.mean(x, axis=-1, keepdims=True)
            var = jnp.mean((x - mu) ** 2, axis=-1, keepdims=True)
            return (x - mu) * jax.lax.rsqrt(var + eps) * w + b
        key = jax.random.key(seed)
        k1, k2, k3 = jax.random.split(key, 3)
        d, h = (128, 512)
        B, T = (8, 256)
        return {'x': jax.random.normal(k1, (B, T, d), jnp.float32), 'W_fc': jax.random.normal(k2, (h, d), jnp.float32), 'ln_w': jnp.ones((h,), jnp.float32), 'ln_b': jnp.zeros((h,), jnp.float32), 'W_proj': jax.random.normal(k3, (d, h), jnp.float32)}
    _L2_ffn_in = _L2_ffn_setup()

    def _L3_attn_setup():
        import jax, jax.numpy as jnp
        import numpy as np
        import math
        D_MODEL = 128
        N_HEADS = 16
        DECAY_SCALE = 0.25

        def power_law_mask(n, decay_scale):
            i = jnp.arange(n)[:, None]
            j = jnp.arange(n)[None, :]
            delta = (i - j).astype(jnp.float32)
            decay = jnp.where(delta > 0, -decay_scale * jnp.log(jnp.maximum(delta, 1.0)), 0.0)
            return jnp.where(j > i, -jnp.inf, decay)
        key = jax.random.key(seed)
        ks = jax.random.split(key, 9)
        B, N, D = (2, 256, D_MODEL)
        s = 1.0 / math.sqrt(D)
        return {'x': jax.random.normal(ks[0], (B, N, D), dtype=jnp.float32), 'Wq': jax.random.normal(ks[1], (D, D), dtype=jnp.float32) * s, 'bq': jnp.zeros((D,), dtype=jnp.float32), 'Wk': jax.random.normal(ks[2], (D, D), dtype=jnp.float32) * s, 'bk': jnp.zeros((D,), dtype=jnp.float32), 'Wv': jax.random.normal(ks[3], (D, D), dtype=jnp.float32) * s, 'bv': jnp.zeros((D,), dtype=jnp.float32), 'Wo': jax.random.normal(ks[4], (D, D), dtype=jnp.float32) * s, 'bo': jnp.zeros((D,), dtype=jnp.float32)}
    _L3_attn_in = _L3_attn_setup()

    def _L3_ffn_setup():
        import jax, jax.numpy as jnp
        import numpy as np
        H = 128
        E = 8
        FFN = 512
        TOP_K = 2
        key = jax.random.key(seed)
        ks = jax.random.split(key, 6)
        s_h = 1.0 / np.sqrt(H)
        s_f = 1.0 / np.sqrt(FFN)
        return {'hidden_states': jax.random.normal(ks[0], (4, 128, H), dtype=jnp.float32), 'router_w': jax.random.uniform(ks[1], (E, H), jnp.float32, -s_h, s_h), 'w1': jax.random.uniform(ks[2], (E, FFN, H), jnp.float32, -s_h, s_h), 'b1': jax.random.uniform(ks[3], (E, FFN), jnp.float32, -s_h, s_h), 'w2': jax.random.uniform(ks[4], (E, H, FFN), jnp.float32, -s_f, s_f), 'b2': jax.random.uniform(ks[5], (E, H), jnp.float32, -s_f, s_f)}
    _L3_ffn_in = _L3_ffn_setup()
    _d = {'L0_attn_x': _L0_attn_in['x'], 'L0_attn_w_attn': _L0_attn_in['w_attn'], 'L0_attn_w_proj': _L0_attn_in['w_proj'], 'L0_ffn_gate_w': _L0_ffn_in['gate_w'], 'L0_ffn_expert_bias': _L0_ffn_in['expert_bias'], 'L0_ffn_w_gate': _L0_ffn_in['w_gate'], 'L0_ffn_w_up': _L0_ffn_in['w_up'], 'L0_ffn_w_down': _L0_ffn_in['w_down'], 'L0_ffn_shared_gate_w': _L0_ffn_in['shared_gate_w'], 'L0_ffn_shared_up_w': _L0_ffn_in['shared_up_w'], 'L0_ffn_shared_down_w': _L0_ffn_in['shared_down_w'], 'L1_attn_qkv_w': _L1_attn_in['qkv_w'], 'L1_attn_qkv_b': _L1_attn_in['qkv_b'], 'L1_attn_out_w': _L1_attn_in['out_w'], 'L1_attn_out_b': _L1_attn_in['out_b'], 'L1_ffn_Wg': _L1_ffn_in['Wg'], 'L1_ffn_W1': _L1_ffn_in['W1'], 'L1_ffn_W2': _L1_ffn_in['W2'], 'L2_attn_Wq': _L2_attn_in['Wq'], 'L2_attn_Wk': _L2_attn_in['Wk'], 'L2_attn_Wv': _L2_attn_in['Wv'], 'L2_attn_Wo': _L2_attn_in['Wo'], 'L2_attn_bo': _L2_attn_in['bo'], 'L2_ffn_W_fc': _L2_ffn_in['W_fc'], 'L2_ffn_ln_w': _L2_ffn_in['ln_w'], 'L2_ffn_ln_b': _L2_ffn_in['ln_b'], 'L2_ffn_W_proj': _L2_ffn_in['W_proj'], 'L3_attn_Wq': _L3_attn_in['Wq'], 'L3_attn_bq': _L3_attn_in['bq'], 'L3_attn_Wk': _L3_attn_in['Wk'], 'L3_attn_bk': _L3_attn_in['bk'], 'L3_attn_Wv': _L3_attn_in['Wv'], 'L3_attn_bv': _L3_attn_in['bv'], 'L3_attn_Wo': _L3_attn_in['Wo'], 'L3_attn_bo': _L3_attn_in['bo'], 'L3_ffn_router_w': _L3_ffn_in['router_w'], 'L3_ffn_w1': _L3_ffn_in['w1'], 'L3_ffn_b1': _L3_ffn_in['b1'], 'L3_ffn_w2': _L3_ffn_in['w2'], 'L3_ffn_b2': _L3_ffn_in['b2']}
    _x0 = _d['L0_attn_x']
    _d['L0_attn_x'] = jax.random.normal(jax.random.fold_in(jax.random.key(seed), 1), (8, 512, 128), dtype=_x0.dtype)
    del _x0
    return _d

def reference(L0_attn_x, L0_attn_w_attn, L0_attn_w_proj, L0_ffn_gate_w, L0_ffn_expert_bias, L0_ffn_w_gate, L0_ffn_w_up, L0_ffn_w_down, L0_ffn_shared_gate_w, L0_ffn_shared_up_w, L0_ffn_shared_down_w, L1_attn_qkv_w, L1_attn_qkv_b, L1_attn_out_w, L1_attn_out_b, L1_ffn_Wg, L1_ffn_W1, L1_ffn_W2, L2_attn_Wq, L2_attn_Wk, L2_attn_Wv, L2_attn_Wo, L2_attn_bo, L2_ffn_W_fc, L2_ffn_ln_w, L2_ffn_ln_b, L2_ffn_W_proj, L3_attn_Wq, L3_attn_bq, L3_attn_Wk, L3_attn_bk, L3_attn_Wv, L3_attn_bv, L3_attn_Wo, L3_attn_bo, L3_ffn_router_w, L3_ffn_w1, L3_ffn_b1, L3_ffn_w2, L3_ffn_b2):

    def _L0_attn_ref(x, w_attn, w_proj):
        import jax, jax.numpy as jnp
        import numpy as np
        N_HEAD = 16
        CHUNK = 128

        def _phi(x):
            return jax.nn.elu(x) + 1.0

        def _causal_linear_attn(qp, kp, v):
            B, H, T, D = qp.shape
            NC = T // CHUNK

            def to_chunks(a):
                return a.reshape(B, H, NC, CHUNK, D).transpose(2, 0, 1, 3, 4)
            qc, kc, vc = (to_chunks(qp), to_chunks(kp), to_chunks(v))
            mask = jnp.tril(jnp.ones((CHUNK, CHUNK), dtype=bool))

            def step(carry, blk):
                S, z = carry
                q_c, k_c, v_c = blk
                scores = jnp.einsum('bhcd,bhkd->bhck', q_c, k_c)
                scores = jnp.where(mask, scores, 0.0)
                num = jnp.einsum('bhck,bhke->bhce', scores, v_c) + jnp.einsum('bhcd,bhde->bhce', q_c, S)
                den = scores.sum(-1) + jnp.einsum('bhcd,bhd->bhc', q_c, z)
                S = S + jnp.einsum('bhkd,bhke->bhde', k_c, v_c)
                z = z + k_c.sum(axis=2)
                return ((S, z), (num, den))
            S0 = jnp.zeros((B, H, D, D), dtype=qp.dtype)
            z0 = jnp.zeros((B, H, D), dtype=qp.dtype)
            _, (num, den) = jax.lax.scan(step, (S0, z0), (qc, kc, vc))
            y = num / (den[..., None] + 1e-06)
            y = y.transpose(1, 2, 0, 3, 4).reshape(B, H, T, D)
            return y
        B, T, E = x.shape
        H = N_HEAD
        D = E // H
        qkv = x @ w_attn.T
        q, k, v = jnp.split(qkv, 3, axis=2)

        def heads(a):
            return a.reshape(B, T, H, D).transpose(0, 2, 1, 3)
        y = _causal_linear_attn(_phi(heads(q)), _phi(heads(k)), heads(v))
        y = y.transpose(0, 2, 1, 3).reshape(B, T, E)
        return y @ w_proj.T

    def _L0_ffn_ref(x, gate_w, expert_bias, w_gate, w_up, w_down, shared_gate_w, shared_up_w, shared_down_w):
        import jax, jax.numpy as jnp
        import numpy as np
        B, S, D = (2, 64, 128)
        E, K, I = (16, 8, 128)
        I_SH = 128
        ROUTE_SCALE = 2.826
        gates = jnp.einsum('bsd,ed->bse', x, gate_w)
        scores = jax.nn.sigmoid(gates.astype(jnp.float32))
        sel_scores = scores + expert_bias
        _, inds = jax.lax.top_k(sel_scores, K)
        selected = jnp.take_along_axis(scores, inds, axis=-1)
        selected = selected / selected.sum(axis=-1, keepdims=True)
        selected = selected * ROUTE_SCALE
        onehot = jax.nn.one_hot(inds, E, dtype=selected.dtype)
        combine = jnp.einsum('bske,bsk->bse', onehot, selected)
        hg = jnp.einsum('bsd,eid->bsei', x, w_gate)
        hu = jnp.einsum('bsd,eid->bsei', x, w_up)
        h = jax.nn.silu(hg) * hu
        ye = jnp.einsum('bsei,edi->bsed', h, w_down)
        y = jnp.einsum('bsed,bse->bsd', ye, combine).astype(x.dtype)
        g = jnp.einsum('bsd,id->bsi', x, shared_gate_w)
        u = jnp.einsum('bsd,id->bsi', x, shared_up_w)
        y = y + jnp.einsum('bsi,di->bsd', jax.nn.silu(g) * u, shared_down_w)
        return y

    def _L1_attn_ref(x, qkv_w, qkv_b, out_w, out_b):
        import jax, jax.numpy as jnp
        import numpy as np
        B, S, D, H = (2, 256, 128, 16)
        HD = D // H
        b, s, d = x.shape
        h, hd = (H, d // H)
        scale = 1.0 / np.sqrt(hd).astype(np.float32)
        qkv = (x @ qkv_w + qkv_b).reshape(b, s, 3, h, hd)
        q, k, v = (qkv[:, :, 0], qkv[:, :, 1], qkv[:, :, 2])
        logits = jnp.einsum('bqhd,bkhd->bhqk', q, k)
        causal_mask = jnp.triu(jnp.ones((s, s), bool), 1)
        logits = jnp.where(causal_mask, -jnp.inf, logits) * scale
        att = jax.nn.softmax(logits, axis=-1)
        out = jnp.einsum('bhqk,bkhd->bqhd', att, v).reshape(b, s, d)
        return out @ out_w + out_b

    def _L1_ffn_ref(x, Wg, W1, W2):
        import jax, jax.numpy as jnp
        import numpy as np
        B, T, D = (2, 256, 128)
        F = 512
        E = 8
        b, t, d = x.shape
        h = x.reshape(-1, d)
        logits = h @ Wg.T
        scores, idx = jax.lax.top_k(logits, 2)
        scores = jax.nn.softmax(scores.astype(jnp.float32), axis=-1).astype(x.dtype)
        up = jnp.einsum('nd,edf->enf', h, W1)
        act = jax.nn.silu(up)
        out = jnp.einsum('enf,efd->ned', act, W2)
        sel = jnp.take_along_axis(out, idx[:, :, None], axis=1)
        y = jnp.sum(scores[:, :, None] * sel, axis=1)
        return y.reshape(b, t, d)

    def _L2_attn_ref(x, Wq, Wk, Wv, Wo, bo):
        import jax, jax.numpy as jnp
        import numpy as np
        NUM_HEADS = 16
        EPS = 1e-05
        CHUNK = 128

        def _linear_attention(x, Wq, Wk, Wv, Wo, bo):
            B, T, E = x.shape
            H = NUM_HEADS
            d = E // H

            def proj(W):
                return (x @ W.T).reshape(B, T, H, d).transpose(0, 2, 1, 3)
            phi_q = jax.nn.elu(proj(Wq)) + 1.0
            phi_k = jax.nn.elu(proj(Wk)) + 1.0
            V = proj(Wv)
            nC = T // CHUNK

            def to_chunks(a):
                return a.reshape(B, H, nC, CHUNK, d).transpose(2, 0, 1, 3, 4)
            qc, kc, vc = (to_chunks(phi_q), to_chunks(phi_k), to_chunks(V))
            mask = jnp.tril(jnp.ones((CHUNK, CHUNK), x.dtype))
            S0 = jnp.zeros((B, H, d, d), x.dtype)
            z0 = jnp.zeros((B, H, d), x.dtype)

            def step(carry, inp):
                S, z = carry
                q, k, v = inp
                A = jnp.einsum('bhid,bhjd->bhij', q, k) * mask
                num = jnp.einsum('bhij,bhjd->bhid', A, v) + jnp.einsum('bhid,bhde->bhie', q, S)
                den = jnp.sum(A, axis=-1) + jnp.einsum('bhid,bhd->bhi', q, z) + EPS
                out = num / den[..., None]
                S = S + jnp.einsum('bhjd,bhje->bhde', k, v)
                z = z + jnp.sum(k, axis=2)
                return ((S, z), out)
            _, outs = jax.lax.scan(step, (S0, z0), (qc, kc, vc))
            out = outs.transpose(1, 2, 0, 3, 4).reshape(B, H, T, d)
            out = out.transpose(0, 2, 1, 3).reshape(B, T, E)
            return out @ Wo.T + bo
        return _linear_attention(x, Wq, Wk, Wv, Wo, bo)

    def _L2_ffn_ref(x, W_fc, ln_w, ln_b, W_proj):
        import jax, jax.numpy as jnp
        import numpy as np
        EPS = 1e-06
        LN_EPS = 1e-05

        def _absmean_core(W):
            gamma = jnp.mean(jnp.abs(W)) + EPS
            Ws = W / gamma
            Wq = jnp.sign(Ws) * jnp.minimum(jnp.round(jnp.abs(Ws)), 1.0)
            return (Wq, gamma)

        @jax.custom_vjp
        def absmean(W):
            return _absmean_core(W)[0]

        def _absmean_fwd(W):
            Wq, gamma = _absmean_core(W)
            return (Wq, gamma)

        def _absmean_bwd(gamma, g):
            return (g / gamma,)
        absmean.defvjp(_absmean_fwd, _absmean_bwd)

        def layernorm(x, w, b, eps=LN_EPS):
            mu = jnp.mean(x, axis=-1, keepdims=True)
            var = jnp.mean((x - mu) ** 2, axis=-1, keepdims=True)
            return (x - mu) * jax.lax.rsqrt(var + eps) * w + b
        h = jnp.einsum('btd,hd->bth', x, absmean(W_fc))
        h = jax.nn.gelu(h, approximate=False)
        h = layernorm(h, ln_w, ln_b)
        return jnp.einsum('bth,dh->btd', h, absmean(W_proj))

    def _L3_attn_ref(x, Wq, bq, Wk, bk, Wv, bv, Wo, bo):
        import jax, jax.numpy as jnp
        import numpy as np
        import math
        D_MODEL = 128
        N_HEADS = 16
        DECAY_SCALE = 0.25

        def power_law_mask(n, decay_scale):
            i = jnp.arange(n)[:, None]
            j = jnp.arange(n)[None, :]
            delta = (i - j).astype(jnp.float32)
            decay = jnp.where(delta > 0, -decay_scale * jnp.log(jnp.maximum(delta, 1.0)), 0.0)
            return jnp.where(j > i, -jnp.inf, decay)
        B, N, D = x.shape
        H = N_HEADS
        dk = D // H

        def proj(W, b):
            return (x @ W + b).reshape(B, N, H, dk).transpose(0, 2, 1, 3)
        Q, K, V = (proj(Wq, bq), proj(Wk, bk), proj(Wv, bv))
        scores = jnp.einsum('bhnd,bhmd->bhnm', Q, K) / jnp.sqrt(jnp.float32(dk))
        scores = scores + power_law_mask(N, DECAY_SCALE)[None, None]
        attn = jax.nn.softmax(scores, axis=-1)
        out = jnp.einsum('bhnm,bhmd->bhnd', attn, V)
        out = out.transpose(0, 2, 1, 3).reshape(B, N, D)
        return out @ Wo + bo

    def _L3_ffn_ref(hidden_states, router_w, w1, b1, w2, b2):
        import jax, jax.numpy as jnp
        import numpy as np
        H = 128
        E = 8
        FFN = 512
        TOP_K = 2
        B, S, _ = hidden_states.shape
        x = hidden_states.reshape(-1, H)
        T = x.shape[0]
        logits = x @ router_w.T
        top_v, top_i = jax.lax.top_k(logits, TOP_K)
        rw = jax.nn.softmax(top_v, axis=-1)
        combine = jnp.zeros((T, E), x.dtype).at[jnp.arange(T)[:, None], top_i].add(rw)
        h = jax.nn.gelu(jnp.einsum('th,efh->etf', x, w1) + b1[:, None, :], approximate=False)
        y = jnp.einsum('etf,ehf->eth', h, w2) + b2[:, None, :]
        out = jnp.einsum('eth,te->th', y, combine)
        return out.reshape(B, S, H)
    x = L0_attn_x
    xn = _layernorm(x, axis=-1)
    s = _L0_attn_ref(xn, L0_attn_w_attn, L0_attn_w_proj)
    g = _silu(_L0_ffn_ref(xn, L0_ffn_gate_w, L0_ffn_expert_bias, L0_ffn_w_gate, L0_ffn_w_up, L0_ffn_w_down, L0_ffn_shared_gate_w, L0_ffn_shared_up_w, L0_ffn_shared_down_w))
    x = x + s * g
    xn = _layernorm(x, axis=-1)
    s = _L1_attn_ref(xn, L1_attn_qkv_w, L1_attn_qkv_b, L1_attn_out_w, L1_attn_out_b)
    g = _silu(_L1_ffn_ref(xn, L1_ffn_Wg, L1_ffn_W1, L1_ffn_W2))
    x = x + s * g
    xn = _layernorm(x, axis=-1)
    s = _L2_attn_ref(xn, L2_attn_Wq, L2_attn_Wk, L2_attn_Wv, L2_attn_Wo, L2_attn_bo)
    g = _silu(_L2_ffn_ref(xn, L2_ffn_W_fc, L2_ffn_ln_w, L2_ffn_ln_b, L2_ffn_W_proj))
    x = x + s * g
    xn = _layernorm(x, axis=-1)
    s = _L3_attn_ref(xn, L3_attn_Wq, L3_attn_bq, L3_attn_Wk, L3_attn_bk, L3_attn_Wv, L3_attn_bv, L3_attn_Wo, L3_attn_bo)
    g = _silu(_L3_ffn_ref(xn, L3_ffn_router_w, L3_ffn_w1, L3_ffn_b1, L3_ffn_w2, L3_ffn_b2))
    x = x + s * g
    return x

_drawn_inputs = setup_inputs


def setup_inputs(seed=0):
    import zlib

    import numpy as np

    out = dict(_drawn_inputs(seed))
    spreads = {'L0_ffn_expert_bias': (0.0, 0.8),
     'L1_attn_qkv_b': (0.0, 0.8),
     'L1_attn_out_b': (0.0, 0.8),
     'L2_attn_bo': (0.0, 0.1),
     'L2_ffn_ln_w': (1.0, 0.2),
     'L2_ffn_ln_b': (0.0, 0.1),
     'L3_attn_bq': (0.0, 0.8),
     'L3_attn_bk': (0.0, 0.8),
     'L3_attn_bv': (0.0, 0.8),
     'L3_attn_bo': (0.0, 0.8)}
    factors = {'L0_attn_w_attn': 8.0,
     'L0_attn_w_proj': 8.0,
     'L0_ffn_gate_w': 8.0,
     'L0_ffn_w_gate': 8.0,
     'L0_ffn_w_up': 8.0,
     'L0_ffn_w_down': 8.0,
     'L0_ffn_shared_gate_w': 8.0,
     'L0_ffn_shared_up_w': 8.0,
     'L0_ffn_shared_down_w': 8.0,
     'L1_attn_qkv_w': 4.517,
     'L1_attn_out_w': 4.568,
     'L1_ffn_Wg': 5.404,
     'L1_ffn_W1': 4.421,
     'L1_ffn_W2': 4.597,
     'L3_attn_Wq': 8.0,
     'L3_attn_Wk': 8.0,
     'L3_attn_Wv': 4.362,
     'L3_attn_Wo': 3.945,
     'L3_ffn_router_w': 4.424,
     'L3_ffn_w1': 4.302,
     'L3_ffn_b1': 8.0,
     'L3_ffn_w2': 4.112,
     'L3_ffn_b2': 8.0}
    for name, (base, spread) in spreads.items():
        noise = np.random.default_rng([zlib.crc32(name.encode()), seed]).standard_normal(out[name].shape)
        drawn = base * np.exp(spread * noise) if base else spread * noise
        out[name] = jnp.asarray(drawn.astype(out[name].dtype))
    for name, factor in factors.items():
        out[name] = (out[name] * factor).astype(out[name].dtype)
    return out
```

```python
from contextlib import ExitStack

import numpy as np

import concourse.bass as bass
from concourse import mybir

F32 = mybir.dt.float32
F32R = mybir.dt.float32r
BF16 = mybir.dt.bfloat16
ALU = mybir.AluOpType
ACT = mybir.ActivationFunctionType
AX = mybir.AxisListType

P = 128
D = 128
B, T = 8, 512
NB = T // P
H, HD = 16, 8
LN_EPS = 1e-5
EXP_LN = "natural_log_exp_and_others"
NEG = -1e30




class Semaphores:

    def __init__(self, nc, ctx):
        self.nc, self.made = nc, []
        ctx.callback(self.clear)

    def new(self, name):
        self.made.append(self.nc.alloc_semaphore(name=name))
        return self.made[-1]

    def clear(self):
        self.nc.clear_and_free_semaphores(self.made)
        self.nc.all_engine_barrier()


class Signal:

    def __init__(self, sems, name, per):
        self.sem, self.per = sems.new(name), per

    def now(self, b, n):
        return (b + 1) * self.per + n

    def before(self, b, n):
        return b * self.per + n


def signals(sems, layer, **per):
    return {k: Signal(sems, f"{k}_{layer}", n) for k, n in per.items()}


def block_of(x_res, b, i):
    return x_res[:, bass.ds(b * NB + i, 1), :].rearrange("p a d -> p (a d)")




def prep_vector(dve, s, m, k):
    for i in range(NB):
        dve.bn_stats(m["stats"][:, i, :], block_of(m["x"], k, i)).then_inc(s["stats"].sem, 1)
    for i in range(NB):
        dve.wait_ge(s["stats"].sem, s["stats"].now(k, i + 1))
        dve.sem_inc(m["passed"], 1)
        dve.bn_aggr(m["mean_var"][:, i, :], m["stats"][:, i, :]).then_inc(s["mean_var"].sem, 1)
    dve.wait_ge(s["rstd"].sem, s["rstd"].now(k, 1))
    dve.wait_ge(s["xnT_ps"].sem, s["xnT_ps"].before(k, 1))
    for i in range(NB):
        dve.tensor_scalar(m["xn"][:, i, :], block_of(m["x"], k, i), m["mean_var"][:, i, 0:1],
                          m["rstd"][:, i:i + 1], ALU.subtract, ALU.mult).then_inc(s["xn"].sem, 1)


def prep_gpsimd(pool, s, m, k):
    pool.wait_ge(s["mean_var"].sem, s["mean_var"].now(k, NB))
    pool.sem_inc(m["passed"], 1)
    pool.tensor_scalar(m["var_eps"][:, :], m["mean_var"][:, :, 1], LN_EPS, 1.0, ALU.add,
                       ALU.mult).then_inc(s["var_eps"].sem, 1)
    pool.wait_ge(s["var_eps"].sem, s["var_eps"].now(k, 1))
    pool.tensor_tensor(m["rstd"][:, :], m["var_eps"][:, :], m["minus_half"][:, :],
                       ALU.pow).then_inc(s["rstd"].sem, 1)


def prep_tensor(pe, s, m, k, bank):
    pe.wait_ge(s["xn"].sem, s["xn"].now(k, NB))
    for i in range(NB):
        last = pe.transpose(bank[:, i * P:(i + 1) * P], m["xn"][:, i, :], m["ident"][:, :])
    last.then_inc(s["xnT_ps"].sem, 1)


def prep_scalar(act, s, m, k, bank):
    act.wait_ge(s["xnT_ps"].sem, s["xnT_ps"].now(k, 1))
    act.activation(m["xnT"][:, :], bank[:, :], ACT.Copy).then_inc(s["xnT"].sem, 1)
    act.activation(m["xnT_hi"][:, :], bank[:, :], ACT.Copy).then_inc(s["xnT_hi"].sem, 1)


def prep_vector_lo(dve, s, m, k, bank):
    dve.wait_ge(s["xnT_hi"].sem, s["xnT_hi"].now(k, 1))
    dve.tensor_tensor(m["xnT_lo"][:, :], bank[:, :], m["xnT_hi"][:, :].bitcast(F32),
                      ALU.subtract).then_inc(s["xnT_lo"].sem, 1)


PREP = dict(stats=NB, mean_var=NB, var_eps=1, rstd=1, xn=NB, xnT_ps=1, xnT=1, xnT_hi=1, xnT_lo=1)


def prep_tiles(m, sb):
    m["stats"] = sb("stats", [P, NB, 6], F32)
    m["mean_var"] = sb("mean_var", [P, NB, 2], F32)
    m["var_eps"] = sb("var_eps", [P, NB], F32)
    m["rstd"] = sb("rstd", [P, NB], F32)
    m["xn"] = sb("xn", [P, NB, D], F32)
    m["xnT"] = sb("xnT", [P, T], F32)
    m["xnT_hi"] = sb("xnT_hi", [P, T], F32R)
    m["xnT_lo"] = sb("xnT_lo", [P, T], F32R)


def product3(pe, out, w_hi, w_lo, m):
    pe.matmul(out, w_hi, m["xnT_hi"][:, :], start=True, stop=False)
    pe.matmul(out, w_lo, m["xnT_hi"][:, :], start=False, stop=False)
    return pe.matmul(out, w_hi, m["xnT_lo"][:, :], start=False, stop=True)




def split_gpsimd(pool, done, hi, lo, stage, n0):
    pool.tensor_scalar(hi, stage, 1.0, 1.0, ALU.mult, ALU.mult).then_inc(done, 1)
    pool.wait_ge(done, 2 * n0 + 1)
    pool.tensor_tensor(lo, stage, hi.bitcast(F32), ALU.subtract).then_inc(done, 1)





E8, FC = 8, 4
CHUNKS = [(0, 512, 0), (0, 384, 512), (128, 384, 896)]
MAX_AT = [(5, 256, 128), (5, 0, 256), (4, 0, 384), (3, 0, 512)]


def softmax_layer(nc, layer, g, d):
    power_law = layer == 3
    with ExitStack() as ctx:
        sems = Semaphores(nc, ctx)

        def sb(name, shape, dt):
            return ctx.enter_context(nc.sbuf_tensor(f"{name}_{layer}", shape, dt))

        m = dict(g)
        prep_tiles(m, sb)
        NPIECE = E8 * FC * P // 512
        wup_hi = sb("wup_hi", [P, E8 * FC * P], F32R)
        wup_lo = sb("wup_lo", [P, E8 * FC * P], F32R)
        wdn = sb("wdn", [P, E8, FC, D], F32)
        stage = sb("stage", [P, 2, 512], F32)
        wqk_hi = sb("wqk_hi", [P, 2, 4, P], F32R)
        wqk_lo = sb("wqk_lo", [P, 2, 4, P], F32R)
        wv = sb("wv", [P, D], F32)
        wo = sb("wo", [P, D], F32)
        wr = sb("wr", [P, E8], F32)
        bqk = sb("bqk", [P, 2, 4], F32)
        bv = sb("bv", [P, D], F32)
        bo = sb("bo", [P, 1], F32)
        b1 = sb("b1", [P, E8, FC], F32)
        b2 = sb("b2", [P, E8], F32)
        q4 = sb("q4", [P, 4, T], F32R)
        k4 = sb("k4", [P, 4, T], F32R)
        qm = sb("qm", [P, 8, T], F32R)
        vs = sb("vs", [P, NB, H, P], F32)
        probs = sb("probs", [P, 2, 1280], F32)
        neg_max = sb("neg_max", [P, NB, 112], F32)
        den_inv = sb("den_inv", [P, T], F32)
        o_t = sb("o_t", [P, T], F32)
        s_t = sb("s_t", [P, T], F32)
        lg = sb("lg", [P, NB, 16], F32)
        top = sb("top", [P, NB, 8], F32)
        two = sb("two", [P, NB, 8], F32)
        rest = sb("rest", [P, NB, 16], F32)
        chosen = sb("chosen", [P, NB, E8], F32)
        lg_rel = sb("lg_rel", [P, NB, E8], F32)
        lg_exp = sb("lg_exp", [P, NB, E8], F32)
        c_raw = sb("c_raw", [P, NB, E8], F32)
        c_sum = sb("c_sum", [P, NB], F32)
        c_inv = sb("c_inv", [P, NB], F32)
        c_tok = sb("c_tok", [P, NB, E8], F32)
        c_t = sb("c_t", [64, T], F32R)
        hid = sb("hid", [P, 3, T], F32)
        c_all = sb("c_all", [P, T], F32)
        y_one = sb("y_one", [P, T], F32)
        acc = sb("acc", [P, T], F32)
        gate = y_one
        upd = sb("upd", [P, T], F32)

        NH = len(range(E8 * FC))
        s = signals(sems, layer, **PREP, qk_ps=8, qk_hi=8, qk_lo=8, qm=16, v_ps=1,
                    vs=4, max_ps=16, neg_max=16, maxT=4, qm_max=16, s_ps=48, probs=48, pv=16,
                    den_ln=2, den_inv=2, o_t=2, s_ps_out=1, s_t=1,
                    lg_ps=1, route=16, lg_exp=1, cT_ps=1, c_hi=1, c_lo=1, c_ps=E8, c_all=E8,
                    up=NH, hid=NH, dn=NH, y_mul=E8, y=E8 - 1, gate=1, upd=1, updT=1, x_new=1)
        setup = sems.new(f"setup_{layer}")
        m["passed"] = sems.new(f"passed_{layer}")
        w_small = sems.new(f"w_small_{layer}")
        w_stage = [sems.new(f"w_stage{i}_{layer}") for i in range(2)]
        w_split = sems.new(f"w_split_{layer}")
        w_down = sems.new(f"w_down_{layer}")
        block = ctx.enter_context(nc.Block())
        bank = g["bank"]
        QK_SPLITS = 4
        small = [(wv, d["wv"]), (wo, d["wo"]), (wr, d["wr"]), (bqk, d["bqk"]), (bv, d["bv"]),
                 (bo, d["bo"])]
        if power_law:
            small += [(b1, d["b1"]), (b2, d["b2"])]
        N_SMALL = 16 * len(small)
        N_PIECES = QK_SPLITS + NPIECE

        def piece(n):
            if n < QK_SPLITS:
                c = slice(n * 2 * P, (n + 1) * 2 * P)
                flat = [w[:, :, :, :].rearrange("p a g c -> p (a g c)") for w in (wqk_hi, wqk_lo)]
                return flat[0][:, c], flat[1][:, c], d["wqk"][:, c]
            c = slice((n - QK_SPLITS) * 512, (n - QK_SPLITS + 1) * 512)
            return wup_hi[:, c], wup_lo[:, c], d["wup"][:, c]

        @block.sync
        def _(sync):
            for x in s.values():
                sync.sem_inc(x.sem, x.per)
            for tile, src in small:
                sync.dma_start(tile[:], src).then_inc(w_small, 16)
            for n in range(N_PIECES):
                if n >= 2:
                    sync.wait_ge(w_split, 2 * (n - 1))
                hi, _, src = piece(n)
                sync.dma_start(stage[:, n % 2, 0:src.shape[1]], src).then_inc(w_stage[n % 2], 16)
                if n == QK_SPLITS:
                    sync.dma_start(wdn[:], d["wdn"]).then_inc(w_down, 16)

        @block.gpsimd
        def _(pool):
            fills = [(k4[96:P, :, :].bitcast(F32), 1.0), (qm[96:P, :, :].bitcast(F32), 0.0),
                     (neg_max[:, :, :], 0.0), (vs[:, :, :, :], 0.0), (c_t[:, :].bitcast(F32), 0.0),
                     (lg[:, :, :], -3e38), (two[:, :, :], -3e38)]
            for h in range(H):
                c = 64 * (1 - h // 8) + 8 * (h % 8)
                fills.append((vs[:, :, h, c:c + HD], 1.0))
            for n, (tile, value) in enumerate(fills):
                if n:
                    pool.wait_ge(setup, n)
                pool.memset(tile, value).then_inc(setup, 1)
            prep_gpsimd(pool, s, m, 0)

            def split(n):
                hi, lo, src = piece(n)
                pool.wait_ge(w_stage[n % 2], 16 * (n // 2 + 1))
                split_gpsimd(pool, w_split, hi, lo, stage[:, n % 2, 0:src.shape[1]], n)

            for n in range(N_PIECES):
                split(n)

            with pool.Fori(0, B) as b:
                for gr in range(4):
                    pool.wait_ge(s["qk_lo"].sem, s["qk_lo"].now(b, 2 * gr + 1))
                    for j in range(4):
                        h = 4 * gr + j
                        if h < 8:
                            pool.wait_ge(s["s_ps"].sem, s["s_ps"].before(b, 3 * (h + 8) + 3))
                        else:
                            pool.wait_ge(s["s_ps"].sem, s["s_ps"].now(b, 3 * (h - 8) + 3))
                        pool.sem_inc(m["passed"], 1)
                        pool.tensor_scalar(qm[0:96, h % 8, :], q4[0:96, gr, :].bitcast(F32),
                                           g["head_mask"][0:96, h:h + 1], 1.0, ALU.mult,
                                           ALU.mult).then_inc(s["qm"].sem, 1)
                prep_gpsimd(pool, s, m, b + 1)
                pool.wait_ge(s["gate"].sem, s["gate"].now(b, 1))
                pool.wait_ge(s["updT"].sem, s["updT"].before(b, 1))
                pool.tensor_tensor(upd[:, :], gate[:, :], s_t[:, :], ALU.mult)\
                    .then_inc(s["upd"].sem, 1)

        @block.scalar
        def _(act):
            act.preload_act_table_set(EXP_LN)
            prep_scalar(act, s, m, 0, bank[7])
            act.wait_ge(w_small, N_SMALL)
            with act.Fori(0, B) as b:
                act.preload_act_table_set(EXP_LN)
                for n in range(8):
                    a, gr = n % 2, n // 2
                    act.wait_ge(s["qk_ps"].sem, s["qk_ps"].now(b, n + 1))
                    if n == 0:
                        act.wait_ge(s["qm"].sem, s["qm"].before(b, 16))
                        act.wait_ge(s["s_ps"].sem, s["s_ps"].before(b, 48))
                    out = (k4 if a else q4)[0:96, gr, :]
                    act.activation(out, bank[3 + n % 4][0:96, :], ACT.Identity,
                                   bias=bqk[0:96, a, gr:gr + 1]).then_inc(s["qk_hi"].sem, 1)

                def router_exp():
                    act.wait_ge(s["route"].sem, s["route"].now(b, 12))
                    act.activation(lg_exp[:, :, :], lg_rel[:, :, :], ACT.Exp)\
                        .then_inc(s["lg_exp"].sem, 1)

                def add_max(gr):
                    act.wait_ge(s["maxT"].sem, s["maxT"].now(b, gr + 1))
                    for h in range(4 * gr, 4 * gr + 4):
                        act.activation(qm[96:112, h % 8, :], bank[5][96:112, :], ACT.Copy,
                                       scale=g["head_mask"][96:112, h:h + 1])\
                            .then_inc(s["qm_max"].sem, 1)

                def exps(h):
                    for c, (lo, n, at) in enumerate(CHUNKS):
                        act.wait_ge(s["s_ps"].sem, s["s_ps"].now(b, 3 * h + c + 1))
                        if c == 0:
                            if h >= 2:
                                act.wait_ge(s["pv"].sem, s["pv"].now(b, h - 1))
                            else:
                                act.wait_ge(s["pv"].sem, s["pv"].before(b, 15 + h))
                        act.activation(probs[:, h % 2, at:at + n], bank[c][:, lo:lo + n], ACT.Exp,
                                       scale=float(HD) ** -0.5).then_inc(s["probs"].sem, 1)

                def denominator(half):
                    rows = slice(64, 128) if half == 0 else slice(0, 64)
                    act.wait_ge(s["pv"].sem, s["pv"].now(b, 8 * half + 8))
                    if half == 0:
                        act.wait_ge(s["o_t"].sem, s["o_t"].before(b, 2))
                    act.activation(den_inv[rows, :], bank[6 + half][rows, :], ACT.Ln)\
                        .then_inc(s["den_ln"].sem, 1)
                    act.wait_ge(s["den_ln"].sem, s["den_ln"].now(b, half + 1))
                    act.activation(den_inv[rows, :], den_inv[rows, :], ACT.Exp, scale=-1.0)\
                        .then_inc(s["den_inv"].sem, 1)

                add_max(0)
                router_exp()
                for h in range(H):
                    exps(h)
                    if h % 4 == 3 and h < H - 1:
                        add_max(h // 4 + 1)
                    if h == 8:
                        denominator(0)
                denominator(1)
                act.wait_ge(s["s_ps_out"].sem, s["s_ps_out"].now(b, 1))
                act.wait_ge(s["upd"].sem, s["upd"].before(b, 1))
                act.activation(s_t[:, :], bank[6][:, :], ACT.Identity, bias=bo[:, 0:1])\
                    .then_inc(s["s_t"].sem, 1)
                act.wait_ge(s["cT_ps"].sem, s["cT_ps"].now(b, 1))
                act.wait_ge(s["c_ps"].sem, s["c_ps"].before(b, E8))
                act.activation(c_t[0:E8, :], bank[7][0:E8, :], ACT.Copy).then_inc(s["c_hi"].sem, 1)
                for e in range(E8):
                    for f in range(FC):
                        n = e * FC + f
                        act.wait_ge(s["up"].sem, s["up"].now(b, n + 1))
                        if n >= 3:
                            act.wait_ge(s["dn"].sem, s["dn"].now(b, n - 2))
                        else:
                            act.wait_ge(s["dn"].sem, s["dn"].before(b, NH - 2 + n))
                        act.activation(hid[:, n % 3, :], bank[n % 3][:, :],
                                       ACT.Gelu if power_law else ACT.Silu,
                                       bias=b1[:, e, f:f + 1] if power_law else 0.0)\
                            .then_inc(s["hid"].sem, 1)
                    act.wait_ge(s["c_ps"].sem, s["c_ps"].now(b, e + 1))
                    if e:
                        act.wait_ge(s["y_mul"].sem, s["y_mul"].now(b, e))
                    else:
                        act.wait_ge(s["y_mul"].sem, s["y_mul"].before(b, E8))
                    act.activation(c_all[:, :], bank[5][:, :], ACT.Copy).then_inc(s["c_all"].sem, 1)
                prep_scalar(act, s, m, b + 1, bank[7])
                act.wait_ge(s["y"].sem, s["y"].now(b, E8 - 1))
                act.activation(gate[:, :], acc[:, :], ACT.Silu).then_inc(s["gate"].sem, 1)

        @block.vector
        def _(dve):
            prep_vector(dve, s, m, 0)
            prep_vector_lo(dve, s, m, 0, bank[7])
            dve.wait_ge(w_small, N_SMALL)
            dve.wait_ge(setup, 7 + H)
            with dve.Fori(0, B) as b:
                def values():
                    dve.wait_ge(s["v_ps"].sem, s["v_ps"].now(b, 1))
                    dve.wait_ge(s["pv"].sem, s["pv"].before(b, 16))
                    for i in range(NB):
                        t0 = vs[:, i, 0, 0:HD]
                        out = bass.AP(tensor=t0.tensor, offset=t0.offset,
                                      ap=[t0.ap[0], [8 * P + 64, 2], [P + 8, 8], [1, HD]])
                        dve.tensor_tensor(
                            out, bank[7][:, i * P:(i + 1) * P].rearrange("p (g j e) -> p g j e",
                                                                         g=2, j=8),
                            bv[:, :].rearrange("p (g j e) -> p g j e", g=2, j=8), ALU.add)\
                            .then_inc(s["vs"].sem, 1)

                def route(n):
                    dve.wait_ge(s["route"].sem, s["route"].now(b, n))

                def route_top():
                    dve.wait_ge(s["lg_ps"].sem, s["lg_ps"].now(b, 1))
                    dve.tensor_copy(lg[:, :, 0:E8],
                                    bank[7][:, 0:NB * E8].rearrange("p (i e) -> p i e", i=NB))\
                        .then_inc(s["route"].sem, 1)
                    route(1)
                    dve.sem_inc(m["passed"], 1)
                    for i in range(NB):
                        dve.max(top[:, i, :], lg[:, i, :]).then_inc(s["route"].sem, 1)
                    route(5)
                    dve.tensor_copy(two[:, :, 0:2], top[:, :, 0:2]).then_inc(s["route"].sem, 1)
                    route(6)
                    dve.sem_inc(m["passed"], 1)
                    for i in range(NB):
                        dve.match_replace(rest[:, i, :], two[:, i, :], lg[:, i, :], 3e38)\
                            .then_inc(s["route"].sem, 1)
                    route(10)
                    dve.tensor_tensor(chosen[:, :, :], rest[:, :, 0:E8], lg[:, :, 0:E8],
                                      ALU.not_equal).then_inc(s["route"].sem, 1)
                    dve.tensor_tensor(lg_rel[:, :, :], lg[:, :, 0:E8],
                                      top[:, :, 0:1].to_broadcast([P, NB, E8]), ALU.subtract)\
                        .then_inc(s["route"].sem, 1)

                def route_rest():
                    dve.wait_ge(s["lg_exp"].sem, s["lg_exp"].now(b, 1))
                    dve.tensor_tensor(c_raw[:, :, :], lg_exp[:, :, :], chosen[:, :, :], ALU.mult)\
                        .then_inc(s["route"].sem, 1)
                    route(13)
                    dve.tensor_reduce(c_sum[:, :], c_raw[:, :, :], AX.X, ALU.add)\
                        .then_inc(s["route"].sem, 1)
                    route(14)
                    dve.reciprocal(c_inv[:, :], c_sum[:, :]).then_inc(s["route"].sem, 1)
                    route(15)
                    dve.wait_ge(s["cT_ps"].sem, s["cT_ps"].before(b, 1))
                    dve.tensor_tensor(c_tok[:, :, :], c_raw[:, :, :],
                                      c_inv[:, :].unsqueeze(2).to_broadcast([P, NB, E8]),
                                      ALU.mult).then_inc(s["route"].sem, 1)

                for n in range(8):
                    a, gr = n % 2, n // 2
                    rows = slice(64, 96) if a == 0 else slice(32, 64)
                    tile = (k4 if a else q4)[:, gr, :]
                    dve.wait_ge(s["qk_hi"].sem, s["qk_hi"].now(b, n + 1))
                    dve.scalar_tensor_tensor(out=tile[rows, :], in0=bank[3 + n % 4][rows, :],
                                             scalar=bqk[rows, a, gr:gr + 1],
                                             in1=tile[rows, :].bitcast(F32), op0=ALU.add,
                                             op1=ALU.subtract).then_inc(s["qk_lo"].sem, 1)
                    if n == 3:
                        values()
                route_top()

                def neg_maxima(h):
                    dve.wait_ge(s["max_ps"].sem, s["max_ps"].now(b, h + 1))
                    if h % 4 == 0:
                        if h:
                            dve.wait_ge(s["maxT"].sem, s["maxT"].now(b, h // 4))
                        else:
                            dve.wait_ge(s["maxT"].sem, s["maxT"].before(b, 4))
                    for i, (bk, lo, n) in enumerate(MAX_AT):
                        last = dve.tensor_reduce(neg_max[:, i, 96 + h:97 + h],
                                                 bank[bk][:, lo:lo + n], AX.X, ALU.max,
                                                 negate=True)
                    last.then_inc(s["neg_max"].sem, 1)

                def normalise(half):
                    num = slice(64 * half, 64 * half + 64)
                    den = slice(64 * (1 - half), 64 * (1 - half) + 64)
                    dve.wait_ge(s["den_inv"].sem, s["den_inv"].now(b, half + 1))
                    if half == 0:
                        dve.wait_ge(s["s_ps_out"].sem, s["s_ps_out"].before(b, 1))
                    dve.tensor_tensor(o_t[num, :], bank[6 + half][num, :], den_inv[den, :],
                                      ALU.mult).then_inc(s["o_t"].sem, 1)

                for h in range(4):
                    neg_maxima(h)
                route_rest()
                for h in range(H):
                    if h + 4 < H:
                        neg_maxima(h + 4)
                    if h == 10:
                        normalise(0)
                normalise(1)
                dve.wait_ge(s["c_hi"].sem, s["c_hi"].now(b, 1))
                dve.tensor_tensor(c_t[32:32 + E8, :], bank[7][0:E8, :],
                                  c_t[0:E8, :].bitcast(F32), ALU.subtract)\
                    .then_inc(s["c_lo"].sem, 1)
                for e in range(E8):
                    dve.wait_ge(s["dn"].sem, s["dn"].now(b, FC * (e + 1)))
                    dve.wait_ge(s["c_all"].sem, s["c_all"].now(b, e + 1))
                    if e == 0:
                        dve.wait_ge(s["gate"].sem, s["gate"].before(b, 1))
                    elif e > 1:
                        dve.wait_ge(s["y"].sem, s["y"].now(b, e - 1))
                    out = y_one[:, :] if e else acc[:, :]
                    if power_law:
                        dve.scalar_tensor_tensor(out=out, in0=bank[3 + e % 2][:, :],
                                                 scalar=b2[:, e:e + 1], in1=c_all[:, :],
                                                 op0=ALU.add, op1=ALU.mult)\
                            .then_inc(s["y_mul"].sem, 1)
                    else:
                        dve.tensor_tensor(out, bank[3 + e % 2][:, :], c_all[:, :], ALU.mult)\
                            .then_inc(s["y_mul"].sem, 1)
                    if e:
                        dve.wait_ge(s["y_mul"].sem, s["y_mul"].now(b, e + 1))
                        dve.tensor_tensor(acc[:, :], acc[:, :], y_one[:, :], ALU.add)\
                            .then_inc(s["y"].sem, 1)
                    if e == 2:
                        prep_vector(dve, s, m, b + 1)
                prep_vector_lo(dve, s, m, b + 1, bank[7])
                dve.wait_ge(s["updT"].sem, s["updT"].now(b, 1))
                xb = g["x"][:, bass.ds(b * NB, NB), :]
                dve.tensor_tensor(xb, xb, bank[6][:, :].rearrange("p (i d) -> p i d", i=NB),
                                  ALU.add).then_inc(s["x_new"].sem, 1)

        @block.tensor
        def _(pe):
            prep_tensor(pe, s, m, 0, bank[7])
            pe.wait_ge(w_small, N_SMALL)
            pe.wait_ge(setup, 7 + H)
            pe.wait_ge(w_split, 2 * QK_SPLITS)
            with pe.Fori(0, B) as b:
                pe.wait_ge(s["xnT"].sem, s["xnT"].now(b, 1))
                pe.wait_ge(s["xnT_hi"].sem, s["xnT_hi"].now(b, 1))
                pe.wait_ge(s["xnT_lo"].sem, s["xnT_lo"].now(b, 1))

                def queries_keys(n):
                    a, gr = n % 2, n // 2
                    if n >= 4:
                        pe.wait_ge(s["qk_lo"].sem, s["qk_lo"].now(b, n - 3))
                    elif n < 2:
                        pe.wait_ge(s["y_mul"].sem, s["y_mul"].before(b, E8 - 1 + n))
                    elif n == 2:
                        pe.wait_ge(s["c_all"].sem, s["c_all"].before(b, E8))
                    else:
                        pe.wait_ge(s["x_new"].sem, s["x_new"].before(b, 1))
                    product3(pe, bank[3 + n % 4][:, :], wqk_hi[:, a, gr, :], wqk_lo[:, a, gr, :],
                             m).then_inc(s["qk_ps"].sem, 1)

                def per_block(w, n, signal):
                    for i in range(NB):
                        last = pe.matmul(bank[7][:, i * n:(i + 1) * n],
                                         m["xnT"][:, i * P:(i + 1) * P], w, start=True, stop=True)
                    last.then_inc(s[signal].sem, 1)

                def max_scores(h):
                    gr = h // 4
                    pe.wait_ge(s["qm"].sem, s["qm"].now(b, h + 1))
                    if h == 0:
                        pe.wait_ge(s["qk_lo"].sem, s["qk_lo"].now(b, 8))
                    else:
                        pe.wait_ge(s["neg_max"].sem, s["neg_max"].now(b, h))
                    if h and h % 4 == 0:
                        pe.wait_ge(s["qm_max"].sem, s["qm_max"].now(b, h))
                    for i in reversed(range(NB)):
                        bk, lo, n = MAX_AT[i]
                        n = max(n, 256)
                        pe.matmul(bank[bk][:, lo:lo + n], qm[0:96, h % 8, i * P:(i + 1) * P],
                                  k4[0:96, gr, 0:n], start=True, stop=False)
                        last = pe.matmul(bank[bk][:, lo + i * P:lo + (i + 1) * P],
                                         g["ident_bf"][:, :], g["causal_q"][:, :],
                                         start=False, stop=True)
                    last.then_inc(s["max_ps"].sem, 1)

                def transpose_max(gr):
                    pe.wait_ge(s["neg_max"].sem, s["neg_max"].now(b, 4 * gr + 4))
                    for i in range(NB):
                        last = pe.transpose(bank[5][0:112, i * P:(i + 1) * P], neg_max[:, i, :],
                                            g["ident"][:, :])
                    last.then_inc(s["maxT"].sem, 1)

                def scores(h):
                    gr = h // 4
                    pe.wait_ge(s["qm_max"].sem, s["qm_max"].now(b, h + 1))
                    for c, blocks in enumerate([(0,), (1,), (3, 2)]):
                        if h:
                            pe.wait_ge(s["probs"].sem, s["probs"].now(b, 3 * (h - 1) + c + 1))
                        else:
                            pe.wait_ge(s["hid"].sem, s["hid"].before(b, NH))
                        for kb in blocks:
                            lo, n = (0, T - kb * P) if kb < 2 else (256 * (3 - kb), 256)
                            if kb == 3:
                                lo = 0
                            pe.matmul(bank[c][:, lo:lo + n], k4[:, gr, kb * P:(kb + 1) * P],
                                      qm[:, h % 8, T - n:T], start=True, stop=False)
                            if power_law:
                                first = 0 if kb == 3 else P
                                pe.matmul(bank[c][:, lo:lo + n], g["ident_r"][:, :],
                                          g["decay_hi"][:, first:first + n],
                                          start=False, stop=False)
                                last = pe.matmul(bank[c][:, lo:lo + n], g["ident_r"][:, :],
                                                 g["decay_lo"][:, first:first + n],
                                                 start=False, stop=True)
                            else:
                                at = lo + (P if kb == 3 else 0)
                                last = pe.matmul(bank[c][:, at:at + P], g["ident_bf"][:, :],
                                                 g["causal_k"][:, :], start=False, stop=True)
                        last.then_inc(s["s_ps"].sem, 1)

                def times_values(h):
                    half = h // 8
                    if h == 0:
                        pe.wait_ge(s["qk_lo"].sem, s["qk_lo"].now(b, 8))
                        pe.wait_ge(s["vs"].sem, s["vs"].now(b, 4))
                    if h == 8:
                        pe.wait_ge(s["route"].sem, s["route"].now(b, 1))
                    for kb, at, c in ((0, 0, 1), (1, 512, 2), (3, 896, 3), (2, 1024, 3)):
                        n = T - kb * P
                        pe.wait_ge(s["probs"].sem, s["probs"].now(b, 3 * h + c))
                        last = pe.matmul(bank[6 + half][:, kb * P:T], vs[:, kb, h, :],
                                         probs[:, h % 2, at:at + n],
                                         start=(h % 8 == 0 and kb == 0),
                                         stop=(h % 8 == 7 and kb == 2))
                    last.then_inc(s["pv"].sem, 1)

                for n in range(8):
                    queries_keys(n)
                    if n == 3:
                        per_block(wv[:, :], D, "v_ps")
                pe.wait_ge(s["vs"].sem, s["vs"].now(b, 4))
                per_block(wr[:, :], E8, "lg_ps")
                for h in range(4):
                    max_scores(h)
                transpose_max(0)
                for h in range(H):
                    scores(h)
                    if h + 4 < H:
                        max_scores(h + 4)
                        if h % 4 == 3:
                            transpose_max(h // 4 + 1)
                    if h:
                        times_values(h - 1)
                times_values(H - 1)
                pe.wait_ge(s["o_t"].sem, s["o_t"].now(b, 2))
                pe.matmul(bank[6][:, :], wo[:, :], o_t[:, :], start=True, stop=True)\
                    .then_inc(s["s_ps_out"].sem, 1)
                pe.wait_ge(s["route"].sem, s["route"].now(b, 16))
                for i in range(NB):
                    last = pe.transpose(bank[7][0:E8, i * P:(i + 1) * P], c_tok[:, i, :],
                                        g["ident"][:, :])
                last.then_inc(s["cT_ps"].sem, 1)

                def up(n):
                    if n >= 3:
                        pe.wait_ge(s["hid"].sem, s["hid"].now(b, n - 2))
                    else:
                        pe.wait_ge(s["probs"].sem, s["probs"].now(b, 48))
                    if n % 4 == 0:
                        pe.wait_ge(w_split, 2 * (QK_SPLITS + n // 4 + 1))
                    c = slice(n * P, (n + 1) * P)
                    product3(pe, bank[n % 3][:, :], wup_hi[:, c], wup_lo[:, c], m)\
                        .then_inc(s["up"].sem, 1)

                def down(n):
                    e, f = n // FC, n % FC
                    pe.wait_ge(s["hid"].sem, s["hid"].now(b, n + 1))
                    if n == 0:
                        pe.wait_ge(w_down, 16)
                    if f == 0 and e >= 2:
                        pe.wait_ge(s["y_mul"].sem, s["y_mul"].now(b, e - 1))
                    elif n == 0:
                        pe.wait_ge(s["neg_max"].sem, s["neg_max"].now(b, 16))
                    pe.matmul(bank[3 + e % 2][:, :], wdn[:, e, f, :], hid[:, n % 3, :],
                              start=(f == 0), stop=(f == FC - 1)).then_inc(s["dn"].sem, 1)

                def spread(e):
                    if e:
                        pe.wait_ge(s["c_all"].sem, s["c_all"].now(b, e))
                    else:
                        pe.wait_ge(s["c_lo"].sem, s["c_lo"].now(b, 1))
                        pe.wait_ge(s["qm_max"].sem, s["qm_max"].now(b, 16))
                    pe.matmul(bank[5][:, :], g["select"][:, e, :], c_t[:, :], start=True, stop=True)\
                        .then_inc(s["c_ps"].sem, 1)

                for n in range(NH):
                    up(n)
                    if n % FC == 2:
                        spread(n // FC)
                    if n >= 2:
                        down(n - 2)
                    if n == 20:
                        prep_tensor(pe, s, m, b + 1, bank[7])
                down(NH - 2)
                down(NH - 1)
                pe.wait_ge(s["upd"].sem, s["upd"].now(b, 1))
                for i in range(NB):
                    last = pe.transpose(bank[6][:, i * P:(i + 1) * P], upd[:, i * P:(i + 1) * P],
                                        g["ident"][:, :])
                last.then_inc(s["updT"].sem, 1)




E16 = 16
ROUTE_SCALE = 2.826
HW = HD + 1
UW = HD * HW
LIN = dict(qkv_ps=NB, e_qk=NB, v_one=NB, e_min=NB, phi=NB, u=NB, u_sum=2, s_ps=NB, w=NB, num=NB,
           den=NB, den_inv=NB, o=NB, oT_ps=1, oT=1, s_ps_out=1, s_t=1, gate=1, upd=1, updT=1,
           x_new=1)


def linear_tiles(m, sb):
    m["e_qk"] = sb("e_qk", [P, 2, 2 * D], F32)
    m["phi"] = sb("phi", [P, 2, 2 * D], F32)
    m["v_one"] = sb("v_one", [P, 2, H, HW], F32)
    m["u"] = sb("u", [P, NB, H * UW], F32)
    m["u_sum"] = sb("u_sum", [P, 2, H * UW], F32)
    m["w"] = sb("w", [P, H * UW], F32)
    m["num"] = sb("num", [P, H, HW], F32)
    m["den"] = sb("den", [P, H], F32)
    m["den_inv"] = sb("den_inv", [P, H], F32)
    m["o"] = sb("o", [P, NB, D], F32)
    m["oT"] = sb("oT", [P, T], F32)
    m["s_t"] = sb("s_t", [P, T], F32)
    m["gate"] = sb("gate", [P, T], F32)
    m["upd"] = sb("upd", [P, T], F32)
    m["wqkv"] = sb("wqkv", [P, 3 * D], F32)
    m["wo"] = sb("wo", [P, D], F32)


def linear_scalar(act, s, m, b, i, bank):
    act.wait_ge(s["qkv_ps"].sem, s["qkv_ps"].now(b, i + 1))
    for name in ("phi", "u"):
        if i >= 2:
            act.wait_ge(s[name].sem, s[name].now(b, i - 1))
        else:
            act.wait_ge(s[name].sem, s[name].before(b, NB - 1 + i))
    qkv = bank[4 + i % 2]
    act.activation(m["e_qk"][:, i % 2, :], qkv[:, 0:2 * D], ACT.Exp).then_inc(s["e_qk"].sem, 1)
    act.activation(m["v_one"][:, i % 2, :, 0:HD],
                   qkv[:, 2 * D:3 * D].rearrange("p (h e) -> p h e", h=H), ACT.Copy)\
        .then_inc(s["v_one"].sem, 1)


def linear_gpsimd(pool, s, m, b, i):
    pool.wait_ge(s["e_qk"].sem, s["e_qk"].now(b, i + 1))
    pool.sem_inc(m["passed"], 1)
    e = m["e_qk"][:, i % 2, :]
    pool.tensor_scalar(e, e, 1.0, 0.0, ALU.min, ALU.max).then_inc(s["e_min"].sem, 1)
    if i in (1, 2):
        pool.wait_ge(s["u"].sem, s["u"].now(b, i + 1))
        first = m["u"][:, 0, :] if i == 1 else m["u_sum"][:, 0, :]
        if i == 1:
            pool.wait_ge(s["s_ps"].sem, s["s_ps"].before(b, NB))
        else:
            pool.wait_ge(s["u_sum"].sem, s["u_sum"].now(b, 1))
        pool.tensor_tensor(m["u_sum"][:, i - 1, :], first, m["u"][:, i, :], ALU.add)\
            .then_inc(s["u_sum"].sem, 1)


def linear_vector_phi(dve, s, m, b, i, bank):
    dve.wait_ge(s["e_min"].sem, s["e_min"].now(b, i + 1))
    dve.wait_ge(s["v_one"].sem, s["v_one"].now(b, i + 1))
    phi = m["phi"][:, i % 2, :]
    if i >= 2:
        dve.wait_ge(s["w"].sem, s["w"].now(b, i - 1))
    else:
        dve.wait_ge(s["w"].sem, s["w"].before(b, NB - 1 + i))
    dve.scalar_tensor_tensor(out=phi, in0=bank[4 + i % 2][:, 0:2 * D], scalar=0.0,
                             in1=m["e_qk"][:, i % 2, :], op0=ALU.max, op1=ALU.add)\
        .then_inc(s["phi"].sem, 1)
    dve.wait_ge(s["phi"].sem, s["phi"].now(b, i + 1))
    if i == 0:
        dve.wait_ge(s["s_ps"].sem, s["s_ps"].before(b, NB))
    phi_k = phi[:, D:2 * D].rearrange("p (h d) -> p h d", h=H)
    shape = [P, H, HD, HW]
    dve.tensor_tensor(m["u"][:, i, :].rearrange("p (h d e) -> p h d e", h=H, d=HD),
                      phi_k.unsqueeze(3).to_broadcast(shape),
                      m["v_one"][:, i % 2, :, :].unsqueeze(2).to_broadcast(shape), ALU.mult)\
        .then_inc(s["u"].sem, 1)


def linear_vector_out(dve, s, m, b, i, psum, eps):
    dve.wait_ge(s["s_ps"].sem, s["s_ps"].now(b, i + 1))
    if i:
        dve.wait_ge(s["num"].sem, s["num"].now(b, i))
    else:
        dve.wait_ge(s["num"].sem, s["num"].before(b, NB))
    shape = [P, 4, 32, HW]
    phi_q = m["phi"][:, i % 2, 0:D].rearrange("p (k x) -> p k x", k=4)
    dve.tensor_tensor(m["w"][:, :].rearrange("p (k x e) -> p k x e", k=4, x=32),
                      psum[:, 0:4, 0:4 * UW].rearrange("p k (x e) -> p k x e", x=32),
                      phi_q.unsqueeze(3).to_broadcast(shape), ALU.mult).then_inc(s["w"].sem, 1)
    dve.wait_ge(s["w"].sem, s["w"].now(b, i + 1))
    dve.tensor_reduce(m["num"][:, :, :],
                      m["w"][:, :].rearrange("p (h d e) -> p h e d", h=H, d=HD), AX.X, ALU.add)\
        .then_inc(s["num"].sem, 1)
    dve.wait_ge(s["num"].sem, s["num"].now(b, i + 1))
    dve.tensor_scalar(m["den"][:, :], m["num"][:, :, HD], eps, None, ALU.add)\
        .then_inc(s["den"].sem, 1)
    dve.wait_ge(s["den"].sem, s["den"].now(b, i + 1))
    dve.reciprocal(m["den_inv"][:, :], m["den"][:, :]).then_inc(s["den_inv"].sem, 1)
    dve.wait_ge(s["den_inv"].sem, s["den_inv"].now(b, i + 1))
    if i == 0:
        dve.wait_ge(s["oT_ps"].sem, s["oT_ps"].before(b, 1))
    dve.tensor_tensor(m["o"][:, i, :].rearrange("p (h e) -> p h e", h=H), m["num"][:, :, 0:HD],
                      m["den_inv"][:, :].unsqueeze(2).to_broadcast([P, H, HD]), ALU.mult)\
        .then_inc(s["o"].sem, 1)


def linear_tensor_qkv(pe, s, m, b, i, bank):
    if i >= 2:
        pe.wait_ge(s["phi"].sem, s["phi"].now(b, i - 1))
    pe.matmul(bank[4 + i % 2][:, 0:3 * D], m["xnT"][:, i * P:(i + 1) * P], m["wqkv"][:, :],
              start=True, stop=True).then_inc(s["qkv_ps"].sem, 1)


def linear_tensor_sums(pe, s, m, b, i, bank):
    pe.wait_ge(s["u"].sem, s["u"].now(b, i + 1))
    if i >= 2:
        pe.wait_ge(s["u_sum"].sem, s["u_sum"].now(b, i - 1))
    if i:
        pe.wait_ge(s["w"].sem, s["w"].now(b, i))
    for k in range(4):
        c = slice(4 * UW * k, 4 * UW * (k + 1))
        last = pe.matmul(bank[k][:, 0:4 * UW], m["tri"][:, :], m["u"][:, i, c],
                         start=True, stop=i == 0)
        if i:
            older = m["u"][:, 0, c] if i == 1 else m["u_sum"][:, i - 2, c]
            last = pe.matmul(bank[k][:, 0:4 * UW], m["ones"][:, :], older, start=False, stop=True)
    last.then_inc(s["s_ps"].sem, 1)


def linear_layer(nc, layer, g, d):
    moe = layer == 0
    with ExitStack() as ctx:
        sems = Semaphores(nc, ctx)

        def sb(name, shape, dt):
            return ctx.enter_context(nc.sbuf_tensor(f"{name}_{layer}", shape, dt))

        m = dict(g)
        prep_tiles(m, sb)
        linear_tiles(m, sb)
        bank, psum = g["bank"], g["psum"]
        names = dict(PREP, **LIN)
        small = [(m["wqkv"], d["wqkv"]), (m["wo"], d["wo"])]
        if moe:
            NE = E16 + 1
            wup_hi = sb("wup_hi", [P, NE, 2, P], F32R)
            wup_lo = sb("wup_lo", [P, NE, 2, P], F32R)
            wdn = sb("wdn", [P, NE, D], F32)
            stage = sb("stage", [P, 2, 512], F32)
            wr = sb("wr", [P, E16], F32)
            rbias = sb("rbias", [P, E16], F32)
            small += [(wr, d["wr"]), (rbias, d["rbias"])]
            lg_exp = sb("lg_exp", [P, NB, E16], F32)
            lg_one = sb("lg_one", [P, NB, E16], F32)
            score = sb("score", [P, NB, E16], F32)
            biased = sb("biased", [P, NB, E16], F32)
            top = sb("top", [P, NB, 8], F32)
            rest = sb("rest", [P, NB, E16], F32)
            chosen = sb("chosen", [P, NB, E16], F32)
            c_raw = sb("c_raw", [P, NB, E16], F32)
            c_sum = sb("c_sum", [P, NB], F32)
            c_inv = sb("c_inv", [P, NB], F32)
            c_scaled = sb("c_scaled", [P, NB], F32)
            c_tok = sb("c_tok", [P, NB, E16], F32)
            c_t = sb("c_t", [64, T], F32R)
            silu = sb("silu", [P, 2, T], F32)
            c_all = sb("c_all", [P, 2, T], F32)
            hid_raw = sb("hid_raw", [P, 2, T], F32)
            hid = sb("hid", [P, 2, T], F32)
            names.update(lg_ps=1, lg_exp=1, route=16, cT_ps=1, c_hi=1, c_lo=1, up=NE, silu=NE,
                         c_ps=E16, c_all=E16, c_scaled=1, hid_raw=NE, hid=E16, dn=NE)
            flat_hi = wup_hi[:, :, :, :].rearrange("p e a c -> p (e a c)")
            flat_lo = wup_lo[:, :, :, :].rearrange("p e a c -> p (e a c)")
            PIECE = 256
            N_PIECES = NE
        else:
            bo = sb("bo", [P, D], F32)
            lnw = sb("lnw", [P, 4], F32)
            lnb = sb("lnb", [P, 4], F32)
            wfc_raw = sb("wfc_raw", [P, 4 * P], F32)
            wproj_raw = sb("wproj_raw", [P, 4 * P], F32)
            small += [(bo, d["bo"]), (lnw, d["lnw"]), (lnb, d["lnb"]), (wfc_raw, d["wfc"]),
                      (wproj_raw, d["wproj"])]
            abs_sum = sb("abs_sum", [P, 2], F32)
            half_gamma = sb("half_gamma", [P, 2], F32)
            minus_half_gamma = sb("minus_half_gamma", [P, 2], F32)
            above = sb("above", [P, 2, 4 * P], F32)
            below = sb("below", [P, 2, 4 * P], F32)
            wfc = sb("wfc", [P, 4, P], F32R)
            wproj = sb("wproj", [P, 4, P], F32)
            lnb_all = sb("lnb_all", [P, 4, P], F32)
            wproj_scaled = sb("wproj_scaled", [P, 4, D], F32)
            ffn_bias = sb("ffn_bias", [P, D], F32)
            mean_w = sb("mean_w", [P, P], F32)
            hid = sb("hid", [P, 4, T], F32)
            cen = sb("cen", [P, 4, T], F32)
            sq = sb("sq", [P, 4, T], F32)
            var_eps_t = sb("var_eps_t", [P, NB], F32)
            rstd_t = sb("rstd_t", [P, NB], F32)
            z = sb("z", [P, NB, D], F32)
            names.update(up=4, hid=4, mean_ps=1, cen=4, sq=4, var_ps=1, var_eps_t=1, rstd_t=1,
                         dn=1, z=4)
            names.pop("updT")
            ternary = sems.new("ternary")
            gamma_ps = sems.new("gamma_ps")
        s = signals(sems, layer, **names)
        setup = sems.new(f"setup_{layer}")
        m["passed"] = sems.new(f"passed_{layer}")
        w_small = sems.new(f"w_small_{layer}")
        w_stage = [sems.new(f"w_stage{i}_{layer}") for i in range(2)]
        w_split = sems.new(f"w_split_{layer}")
        w_down = sems.new(f"w_down_{layer}")
        N_SMALL = 16 * len(small)
        block = ctx.enter_context(nc.Block())

        @block.sync
        def _(sync):
            for x in s.values():
                sync.sem_inc(x.sem, x.per)
            for tile, src in small:
                sync.dma_start(tile[:], src).then_inc(w_small, 16)
            if moe:
                for n in range(N_PIECES):
                    if n >= 2:
                        sync.wait_ge(w_split, 2 * (n - 1))
                    sync.dma_start(stage[:, n % 2, 0:PIECE], d["wup"][:, n * PIECE:(n + 1) * PIECE])\
                        .then_inc(w_stage[n % 2], 16)
                    if n == 0:
                        sync.dma_start(wdn[:], d["wdn"]).then_inc(w_down, 16)

        @block.gpsimd
        def _(pool):
            fills = [(m["v_one"][:, :, :, :], 1.0)]
            if moe:
                fills += [(c_t[:, :].bitcast(F32), 0.0)]
            else:
                fills += [(mean_w[:, :], 1.0 / (4 * P))]
            for n, (tile, value) in enumerate(fills):
                if n:
                    pool.wait_ge(setup, n)
                pool.memset(tile, value).then_inc(setup, 1)
            pool.wait_ge(setup, len(fills))
            prep_gpsimd(pool, s, m, 0)
            if moe:
                for n in range(N_PIECES):
                    c = slice(n * PIECE, (n + 1) * PIECE)
                    pool.wait_ge(w_stage[n % 2], 16 * (n // 2 + 1))
                    split_gpsimd(pool, w_split, flat_hi[:, c], flat_lo[:, c],
                                 stage[:, n % 2, 0:PIECE], n)
            with pool.Fori(0, B) as b:
                for i in range(NB):
                    linear_gpsimd(pool, s, m, b, i)
                prep_gpsimd(pool, s, m, b + 1)
                if not moe:
                    pool.wait_ge(s["var_eps_t"].sem, s["var_eps_t"].now(b, 1))
                    pool.wait_ge(s["z"].sem, s["z"].before(b, 4))
                    pool.tensor_tensor(rstd_t[:, :], var_eps_t[:, :], m["minus_half"][:, :],
                                       ALU.pow).then_inc(s["rstd_t"].sem, 1)
                pool.wait_ge(s["gate"].sem, s["gate"].now(b, 1))
                pool.wait_ge(s["s_t"].sem, s["s_t"].now(b, 1))
                last_use = s["updT" if moe else "x_new"]
                pool.wait_ge(last_use.sem, last_use.before(b, 1))
                pool.tensor_tensor(m["upd"][:, :], m["gate"][:, :], m["s_t"][:, :], ALU.mult)\
                    .then_inc(s["upd"].sem, 1)

        @block.scalar
        def _(act):
            act.preload_act_table_set(EXP_LN)
            prep_scalar(act, s, m, 0, bank[7])
            act.wait_ge(w_small, N_SMALL)
            act.wait_ge(setup, 2)
            with act.Fori(0, B) as b:
                act.preload_act_table_set(EXP_LN)
                linear_scalar(act, s, m, b, 0, bank)
                linear_scalar(act, s, m, b, 1, bank)
                if moe:
                    act.wait_ge(s["lg_ps"].sem, s["lg_ps"].now(b, 1))
                    act.activation(lg_exp[:, :, :], bank[6][:, 0:NB * E16]
                                   .rearrange("p (i e) -> p i e", i=NB), ACT.Exp, scale=-1.0)\
                        .then_inc(s["lg_exp"].sem, 1)
                linear_scalar(act, s, m, b, 2, bank)
                linear_scalar(act, s, m, b, 3, bank)
                act.wait_ge(s["oT_ps"].sem, s["oT_ps"].now(b, 1))
                act.activation(m["oT"][:, :], bank[6][:, :], ACT.Copy).then_inc(s["oT"].sem, 1)
                if moe:
                    act.wait_ge(s["s_ps_out"].sem, s["s_ps_out"].now(b, 1))
                    act.wait_ge(s["upd"].sem, s["upd"].before(b, 1))
                    act.activation(m["s_t"][:, :], bank[5][:, :], ACT.Copy)\
                        .then_inc(s["s_t"].sem, 1)
                    act.wait_ge(s["cT_ps"].sem, s["cT_ps"].now(b, 1))
                    act.wait_ge(s["c_ps"].sem, s["c_ps"].before(b, E16))
                    act.activation(c_t[0:E16, :], bank[7][0:E16, :], ACT.Copy)\
                        .then_inc(s["c_hi"].sem, 1)
                    for e in range(NE):
                        act.wait_ge(s["up"].sem, s["up"].now(b, e + 1))
                        if e >= 2:
                            act.wait_ge(s["hid_raw"].sem, s["hid_raw"].now(b, e - 1))
                        else:
                            act.wait_ge(s["hid_raw"].sem, s["hid_raw"].before(b, NE - 1 + e))
                        act.activation(silu[:, e % 2, :], bank[2 * (e % 2)][:, :], ACT.Silu)\
                            .then_inc(s["silu"].sem, 1)
                        if e < E16:
                            act.wait_ge(s["c_ps"].sem, s["c_ps"].now(b, e + 1))
                            if e >= 2:
                                act.wait_ge(s["hid"].sem, s["hid"].now(b, e - 1))
                            else:
                                act.wait_ge(s["hid"].sem, s["hid"].before(b, E16 - 1 + e))
                            act.activation(c_all[:, e % 2, :], bank[5][:, :], ACT.Copy)\
                                .then_inc(s["c_all"].sem, 1)
                else:
                    for c in range(4):
                        act.wait_ge(s["up"].sem, s["up"].now(b, c + 1))
                        if c == 0:
                            act.wait_ge(s["cen"].sem, s["cen"].before(b, 4))
                        act.activation(hid[:, c, :], bank[c][:, :], ACT.Gelu)\
                            .then_inc(s["hid"].sem, 1)
                    for c in range(4):
                        act.wait_ge(s["cen"].sem, s["cen"].now(b, c + 1))
                        if c == 0:
                            act.wait_ge(s["var_ps"].sem, s["var_ps"].before(b, 1))
                        act.activation(sq[:, c, :], cen[:, c, :], ACT.Square)\
                            .then_inc(s["sq"].sem, 1)
                prep_scalar(act, s, m, b + 1, bank[7])
                act.wait_ge(s["upd"].sem, s["upd"].before(b, 1))
                if moe:
                    act.wait_ge(s["dn"].sem, s["dn"].now(b, NE))
                    act.activation(m["gate"][:, :], bank[4][:, :], ACT.Silu)\
                        .then_inc(s["gate"].sem, 1)
                else:
                    act.wait_ge(s["z"].sem, s["z"].now(b, 4))
                    act.activation(m["gate"][:, :], z[:, :, :].rearrange("p i d -> p (i d)"),
                                   ACT.Silu).then_inc(s["gate"].sem, 1)

        def router(dve, b):
            def route(n):
                dve.wait_ge(s["route"].sem, s["route"].now(b, n))

            def done(ins):
                ins.then_inc(s["route"].sem, 1)

            dve.wait_ge(s["lg_exp"].sem, s["lg_exp"].now(b, 1))
            done(dve.tensor_scalar(lg_one[:, :, :], lg_exp[:, :, :], 1.0, None, ALU.add))
            route(1)
            done(dve.reciprocal(score[:, :, :], lg_one[:, :, :]))
            route(2)
            done(dve.tensor_tensor(biased[:, :, :], score[:, :, :],
                                   rbias[:, :].unsqueeze(1).to_broadcast([P, NB, E16]), ALU.add))
            route(3)
            dve.sem_inc(m["passed"], 1)
            for i in range(NB):
                done(dve.max(top[:, i, :], biased[:, i, :]))
            route(7)
            dve.sem_inc(m["passed"], 1)
            for i in range(NB):
                done(dve.match_replace(rest[:, i, :], top[:, i, :], biased[:, i, :], 3e38))
            route(11)
            done(dve.tensor_tensor(chosen[:, :, :], rest[:, :, :], biased[:, :, :], ALU.not_equal))
            route(12)
            done(dve.tensor_tensor(c_raw[:, :, :], score[:, :, :], chosen[:, :, :], ALU.mult))
            route(13)
            done(dve.tensor_reduce(c_sum[:, :], c_raw[:, :, :], AX.X, ALU.add))
            route(14)
            done(dve.reciprocal(c_inv[:, :], c_sum[:, :]))
            route(15)
            dve.tensor_scalar(c_scaled[:, :], c_inv[:, :], ROUTE_SCALE, None, ALU.mult)\
                .then_inc(s["c_scaled"].sem, 1)
            dve.wait_ge(s["c_scaled"].sem, s["c_scaled"].now(b, 1))
            dve.wait_ge(s["cT_ps"].sem, s["cT_ps"].before(b, 1))
            done(dve.tensor_tensor(c_tok[:, :, :], c_raw[:, :, :],
                                   c_scaled[:, :].unsqueeze(2).to_broadcast([P, NB, E16]),
                                   ALU.mult))

        def experts(dve, b):
            dve.wait_ge(s["c_hi"].sem, s["c_hi"].now(b, 1))
            dve.tensor_tensor(c_t[32:32 + E16, :], bank[7][0:E16, :],
                              c_t[0:E16, :].bitcast(F32), ALU.subtract).then_inc(s["c_lo"].sem, 1)
            for e in range(NE):
                dve.wait_ge(s["silu"].sem, s["silu"].now(b, e + 1))
                shared = e == E16
                if shared:
                    dve.wait_ge(s["dn"].sem, s["dn"].now(b, e - 1))
                elif e == 0:
                    dve.wait_ge(s["hid"].sem, s["hid"].before(b, E16))
                elif e >= 2:
                    dve.wait_ge(s["hid"].sem, s["hid"].now(b, e - 1))
                dve.tensor_tensor((hid if shared else hid_raw)[:, e % 2, :],
                                  bank[2 * (e % 2) + 1][:, :], silu[:, e % 2, :], ALU.mult)\
                    .then_inc(s["hid_raw"].sem, 1)
                if not shared:
                    dve.wait_ge(s["hid_raw"].sem, s["hid_raw"].now(b, e + 1))
                    dve.wait_ge(s["c_all"].sem, s["c_all"].now(b, e + 1))
                    if e >= 2:
                        dve.wait_ge(s["dn"].sem, s["dn"].now(b, e - 1))
                    elif e == 0:
                        dve.wait_ge(s["dn"].sem, s["dn"].before(b, NE))
                    dve.tensor_tensor(hid[:, e % 2, :], hid_raw[:, e % 2, :], c_all[:, e % 2, :],
                                      ALU.mult).then_inc(s["hid"].sem, 1)
                if e == 8:
                    prep_vector(dve, s, m, b + 1)

        def ternary_weights(dve):
            for n, w in enumerate((wfc_raw, wproj_raw)):
                dve.tensor_reduce(abs_sum[:, n:n + 1], w[:, :], AX.X, ALU.add,
                                  apply_absolute_value=True).then_inc(ternary, 1)
            dve.wait_ge(gamma_ps, 1)
            size = float(4 * P * D)
            dve.tensor_scalar(half_gamma[:, :], bank[0][:, 0:2], 0.5 / size, 0.5e-6, ALU.mult,
                              ALU.add).then_inc(ternary, 1)
            dve.wait_ge(ternary, 3)
            dve.tensor_scalar(minus_half_gamma[:, :], half_gamma[:, :], -1.0, None, ALU.mult)\
                .then_inc(ternary, 1)
            dve.wait_ge(ternary, 4)
            for n, w in enumerate((wfc_raw, wproj_raw)):
                dve.tensor_scalar(above[:, n, :], w[:, :], half_gamma[:, n:n + 1], None,
                                  ALU.is_gt).then_inc(ternary, 1)
                dve.tensor_scalar(below[:, n, :], w[:, :], minus_half_gamma[:, n:n + 1], None,
                                  ALU.is_lt).then_inc(ternary, 1)
            dve.wait_ge(ternary, 8)
            for n, w in enumerate((wfc, wproj)):
                dve.tensor_tensor(w[:, :, :].rearrange("p c f -> p (c f)"), above[:, n, :],
                                  below[:, n, :], ALU.subtract).then_inc(ternary, 1)
            dve.tensor_copy(lnb_all[:, :, :], lnb[:, :].unsqueeze(2).to_broadcast([P, 4, P]))\
                .then_inc(ternary, 1)
            dve.wait_ge(ternary, 10)
            for c in range(4):
                dve.tensor_scalar(wproj_scaled[:, c, :], wproj[:, c, :], lnw[:, c:c + 1], None,
                                  ALU.mult).then_inc(ternary, 1)
            dve.wait_ge(gamma_ps, 2)
            dve.tensor_copy(ffn_bias[:, :], bank[1][:, 0:D]).then_inc(ternary, 1)

        def normed(dve, b):
            dve.wait_ge(s["s_ps_out"].sem, s["s_ps_out"].now(b, 1))
            dve.wait_ge(s["upd"].sem, s["upd"].before(b, 1))
            dve.tensor_tensor(m["s_t"][:, :].rearrange("p (i d) -> p i d", i=NB),
                              bank[5][:, :].rearrange("p (i d) -> p i d", i=NB),
                              bo[:, :].unsqueeze(1).to_broadcast([P, NB, D]), ALU.add)\
                .then_inc(s["s_t"].sem, 1)
            dve.wait_ge(s["mean_ps"].sem, s["mean_ps"].now(b, 1))
            dve.wait_ge(s["dn"].sem, s["dn"].before(b, 1))
            dve.wait_ge(s["sq"].sem, s["sq"].before(b, 4))
            for c in range(4):
                dve.tensor_tensor(cen[:, c, :], hid[:, c, :], bank[4][:, :], ALU.subtract)\
                    .then_inc(s["cen"].sem, 1)
            prep_vector(dve, s, m, b + 1)
            dve.wait_ge(s["var_ps"].sem, s["var_ps"].now(b, 1))
            dve.wait_ge(s["rstd_t"].sem, s["rstd_t"].before(b, 1))
            dve.tensor_scalar(var_eps_t[:, :], bank[6][:, 0:NB], LN_EPS, None, ALU.add)\
                .then_inc(s["var_eps_t"].sem, 1)
            dve.wait_ge(s["dn"].sem, s["dn"].now(b, 1))
            dve.wait_ge(s["rstd_t"].sem, s["rstd_t"].now(b, 1))
            dve.wait_ge(s["gate"].sem, s["gate"].before(b, 1))
            for i in range(NB):
                dve.scalar_tensor_tensor(out=z[:, i, :], in0=bank[4][:, i * P:(i + 1) * P],
                                         scalar=rstd_t[:, i:i + 1], in1=ffn_bias[:, :],
                                         op0=ALU.mult, op1=ALU.add).then_inc(s["z"].sem, 1)

        @block.vector
        def _(dve):
            prep_vector(dve, s, m, 0)
            prep_vector_lo(dve, s, m, 0, bank[7])
            dve.wait_ge(w_small, N_SMALL)
            dve.wait_ge(setup, 2)
            if not moe:
                ternary_weights(dve)
            with dve.Fori(0, B) as b:
                linear_vector_phi(dve, s, m, b, 0, bank)
                linear_vector_phi(dve, s, m, b, 1, bank)
                if moe:
                    router(dve, b)
                for i in range(NB):
                    linear_vector_out(dve, s, m, b, i, psum, 1e-6 if moe else 1e-5)
                    if i + 2 < NB:
                        linear_vector_phi(dve, s, m, b, i + 2, bank)
                if moe:
                    experts(dve, b)
                else:
                    normed(dve, b)
                prep_vector_lo(dve, s, m, b + 1, bank[7])
                update = s["updT" if moe else "upd"]
                dve.wait_ge(update.sem, update.now(b, 1))
                xb = g["x"][:, bass.ds(b * NB, NB), :]
                dve.tensor_tensor(xb, xb, (bank[6] if moe else m["upd"])[:, :]
                                  .rearrange("p (i d) -> p i d", i=NB), ALU.add)\
                    .then_inc(s["x_new"].sem, 1)

        @block.tensor
        def _(pe):
            prep_tensor(pe, s, m, 0, bank[7])
            pe.wait_ge(w_small, N_SMALL)
            pe.wait_ge(setup, 2)
            if not moe:
                pe.wait_ge(ternary, 2)
                pe.matmul(bank[0][:, 0:2], g["ones"][:, :], abs_sum[:, :], start=True, stop=True)\
                    .then_inc(gamma_ps, 1)
                pe.wait_ge(ternary, 11)
                for c in range(4):
                    last = pe.matmul(bank[1][:, 0:D], lnb_all[:, c, :], wproj[:, c, :],
                                     start=c == 0, stop=c == 3)
                last.then_inc(gamma_ps, 1)
                pe.wait_ge(ternary, 16)
            with pe.Fori(0, B) as b:
                pe.wait_ge(s["xnT"].sem, s["xnT"].now(b, 1))
                if moe:
                    pe.wait_ge(s["gate"].sem, s["gate"].before(b, 1))
                    pe.wait_ge(s["c_all"].sem, s["c_all"].before(b, E16))
                else:
                    pe.wait_ge(s["z"].sem, s["z"].before(b, 4))
                    pe.wait_ge(s["s_t"].sem, s["s_t"].before(b, 1))
                linear_tensor_qkv(pe, s, m, b, 0, bank)
                linear_tensor_qkv(pe, s, m, b, 1, bank)
                if moe:
                    pe.wait_ge(s["x_new"].sem, s["x_new"].before(b, 1))
                    for i in range(NB):
                        last = pe.matmul(bank[6][:, i * E16:(i + 1) * E16],
                                         m["xnT"][:, i * P:(i + 1) * P], wr[:, :],
                                         start=True, stop=True)
                    last.then_inc(s["lg_ps"].sem, 1)
                for i in range(NB):
                    if i == 0:
                        free = ("hid_raw", NE) if moe else ("hid", 4)
                        pe.wait_ge(s[free[0]].sem, s[free[0]].before(b, free[1]))
                    linear_tensor_sums(pe, s, m, b, i, bank)
                    if i + 2 < NB:
                        linear_tensor_qkv(pe, s, m, b, i + 2, bank)
                if moe:
                    pe.wait_ge(s["lg_exp"].sem, s["lg_exp"].now(b, 1))
                else:
                    pe.wait_ge(s["var_eps_t"].sem, s["var_eps_t"].before(b, 1))
                for i in range(NB):
                    pe.wait_ge(s["o"].sem, s["o"].now(b, i + 1))
                    last = pe.transpose(bank[6][:, i * P:(i + 1) * P], m["o"][:, i, :],
                                        g["ident"][:, :])
                last.then_inc(s["oT_ps"].sem, 1)
                pe.wait_ge(s["oT"].sem, s["oT"].now(b, 1))
                pe.wait_ge(s["phi"].sem, s["phi"].now(b, NB))
                if moe:
                    pe.matmul(bank[5][:, :], m["wo"][:, :], m["oT"][:, :], start=True, stop=True)\
                        .then_inc(s["s_ps_out"].sem, 1)
                else:
                    for i in range(NB):
                        c = slice(i * P, (i + 1) * P)
                        last = pe.matmul(bank[5][:, c], m["oT"][:, c], m["wo"][:, :], start=True,
                                         stop=True)
                    last.then_inc(s["s_ps_out"].sem, 1)
                pe.wait_ge(s["xnT_lo"].sem, s["xnT_lo"].now(b, 1))
                if moe:
                    pe.wait_ge(s["route"].sem, s["route"].now(b, 16))
                    for i in range(NB):
                        last = pe.transpose(bank[7][0:E16, i * P:(i + 1) * P], c_tok[:, i, :],
                                            g["ident"][:, :])
                    last.then_inc(s["cT_ps"].sem, 1)
                    pe.wait_ge(s["w"].sem, s["w"].now(b, NB))
                    for e in range(NE + 1):
                        if e < NE:
                            if e >= 2:
                                pe.wait_ge(s["hid_raw"].sem, s["hid_raw"].now(b, e - 1))
                            pe.wait_ge(w_split, 2 * (e + 1))
                            product3(pe, bank[2 * (e % 2)][:, :], wup_hi[:, e, 0, :],
                                     wup_lo[:, e, 0, :], m)
                            product3(pe, bank[2 * (e % 2) + 1][:, :], wup_hi[:, e, 1, :],
                                     wup_lo[:, e, 1, :], m).then_inc(s["up"].sem, 1)
                        if e < E16:
                            if e:
                                pe.wait_ge(s["c_all"].sem, s["c_all"].now(b, e))
                            else:
                                pe.wait_ge(s["c_lo"].sem, s["c_lo"].now(b, 1))
                                pe.wait_ge(s["s_t"].sem, s["s_t"].now(b, 1))
                            pe.matmul(bank[5][:, :], g["select"][:, e, :], c_t[:, :], start=True,
                                      stop=True).then_inc(s["c_ps"].sem, 1)
                        if e:
                            j = e - 1
                            if j < E16:
                                pe.wait_ge(s["hid"].sem, s["hid"].now(b, j + 1))
                            else:
                                pe.wait_ge(s["hid_raw"].sem, s["hid_raw"].now(b, NE))
                            if j == 0:
                                pe.wait_ge(w_down, 16)
                            pe.matmul(bank[4][:, :], wdn[:, j, :], hid[:, j % 2, :],
                                      start=(j == 0), stop=(j == NE - 1))\
                                .then_inc(s["dn"].sem, 1)
                        if e == 13:
                            prep_tensor(pe, s, m, b + 1, bank[7])
                else:
                    pe.wait_ge(s["w"].sem, s["w"].now(b, NB))
                    for c in range(4):
                        pe.matmul(bank[c][:, :], wfc[:, c, :], m["xnT_hi"][:, :], start=True,
                                  stop=False)
                        pe.matmul(bank[c][:, :], wfc[:, c, :], m["xnT_lo"][:, :], start=False,
                                  stop=True).then_inc(s["up"].sem, 1)
                    for c in range(4):
                        pe.wait_ge(s["hid"].sem, s["hid"].now(b, c + 1))
                        last = pe.matmul(bank[4][:, :], mean_w[:, :], hid[:, c, :],
                                         start=c == 0, stop=c == 3)
                    last.then_inc(s["mean_ps"].sem, 1)
                    pe.wait_ge(s["cen"].sem, s["cen"].now(b, 4))
                    for i in range(NB):
                        for c in range(4):
                            last = pe.matmul(bank[4][:, i * P:(i + 1) * P],
                                             cen[:, c, i * P:(i + 1) * P], wproj_scaled[:, c, :],
                                             start=c == 0, stop=c == 3)
                    last.then_inc(s["dn"].sem, 1)
                    pe.wait_ge(s["sq"].sem, s["sq"].now(b, 4))
                    for i in range(NB):
                        for c in range(4):
                            last = pe.matmul(bank[6][:, i:i + 1], sq[:, c, i * P:(i + 1) * P],
                                             mean_w[:, 0:1], start=c == 0, stop=c == 3)
                    last.then_inc(s["var_ps"].sem, 1)
                    prep_tensor(pe, s, m, b + 1, bank[7])
                if moe:
                    pe.wait_ge(s["upd"].sem, s["upd"].now(b, 1))
                    for i in range(NB):
                        last = pe.transpose(bank[6][:, i * P:(i + 1) * P],
                                            m["upd"][:, i * P:(i + 1) * P], g["ident"][:, :])
                    last.then_inc(s["updT"].sem, 1)




def decay_table():
    k, q = np.arange(P)[:, None], np.arange(T)[None, :]
    delta = (q - k).astype(np.float64)
    t = np.where(delta > 0, -0.25 * np.log(np.maximum(delta, 1.0)) * np.sqrt(HD), 0.0)
    t = np.where(delta < 0, NEG, t)
    return np.concatenate([np.zeros((P, P)), t], 1).astype(np.float32)


def constants():
    p = np.arange(P)
    head = np.zeros((P, H), np.float32)
    for h in range(H):
        head[:96, h] = (p[:96] % 32) // HD == h % 4
        head[96 + h, h] = 1
    select = np.zeros((64, 16, P), np.float32)
    for e in range(16):
        select[e, e] = select[32 + e, e] = 1
    return {
        "c_ident": np.eye(P, dtype=np.float32),
        "c_causal_q": np.where(p[None, :] > p[:, None], NEG, 0).astype(np.float32),
        "c_causal_k": np.where(p[:, None] > p[None, :], NEG, 0).astype(np.float32),
        "c_head_mask": head,
        "c_select": select,
        "c_decay": decay_table(),
        "c_tri": (p[:, None] <= p[None, :]).astype(np.float32),
    }


def load_constants(nc, ctx, dram):
    def sb(name, shape, dt):
        return ctx.enter_context(nc.sbuf_tensor(name, shape, dt))

    psum = ctx.enter_context(nc.psum_tensor("psum", [P, 8, 512], F32))
    g = {"psum": psum, "bank": [psum[:, i, :] for i in range(8)]}
    g["x"] = sb("x_res", [P, (B + 1) * NB, D], F32)
    g["ident"] = sb("ident", [P, P], F32)
    g["ident_r"] = sb("ident_r", [P, P], F32R)
    g["ident_bf"] = sb("ident_bf", [P, P], BF16)
    g["causal_q"] = sb("causal_q", [P, P], BF16)
    g["causal_k"] = sb("causal_k", [P, P], BF16)
    g["head_mask"] = sb("head_mask", [P, H], F32)
    g["select"] = sb("select", [64, 16, P], F32R)
    g["tri"] = sb("tri", [P, P], F32)
    g["ones"] = sb("ones", [P, P], F32)
    g["minus_half"] = sb("minus_half", [P, NB], F32)
    if 3 in LAYERS:
        g["decay_hi"] = sb("decay_hi", [P, P + T], F32R)
        g["decay_lo"] = sb("decay_lo", [P, P + T], F32R)
    with ExitStack() as tmp:
        raw = tmp.enter_context(nc.sbuf_tensor("raw_mask", [P, 2, P], F32))
        raw_dec = tmp.enter_context(nc.sbuf_tensor("raw_decay", [P, P + T], F32))
        raw_sel = tmp.enter_context(nc.sbuf_tensor("raw_select", [64, 16 * P], F32))
        consts = nc.alloc_semaphore(name="consts")
        x_in = nc.alloc_semaphore(name="x_in")
        narrowed = nc.alloc_semaphore(name="narrowed")
        block = tmp.enter_context(nc.Block())
        loads = [(g["ident"][:, :], dram["c_ident"]), (raw[:, 0, :], dram["c_causal_q"]),
                 (raw[:, 1, :], dram["c_causal_k"]), (g["head_mask"][:, :], dram["c_head_mask"]),
                 (raw_sel[:, :], dram["c_select"].rearrange("k e p -> k (e p)")),
                 (raw_dec[:, :], dram["c_decay"]), (g["tri"][:, :], dram["c_tri"])]

        @block.sync
        def _(sync):
            for tile, src in loads:
                sync.dma_start(tile, src).then_inc(consts, 16)
            sync.wait_ge(consts, 16 * len(loads))
            sync.wait_ge(x_in, 16 * B)

        @block.scalar
        def _(act):
            x_blocks = dram["L0_attn_x"].rearrange("(t p) d -> p t d", p=P)
            for b in range(B):
                act.dma_start(g["x"][:, b * NB:(b + 1) * NB, :],
                              x_blocks[:, b * NB:(b + 1) * NB, :]).then_inc(x_in, 16)

        @block.gpsimd
        def _(pool):
            pool.memset(g["ones"][:, :], 1.0)
            pool.memset(g["minus_half"][:, :], -0.5)
            pool.memset(g["x"][:, B * NB:(B + 1) * NB, :], 0.0)

        @block.vector
        def _(dve):
            dve.wait_ge(consts, 16 * len(loads))
            dve.tensor_copy(g["ident_bf"][:, :], g["ident"][:, :])
            dve.tensor_copy(g["ident_r"][:, :], g["ident"][:, :])
            dve.tensor_copy(g["causal_q"][:, :], raw[:, 0, :])
            dve.tensor_copy(g["causal_k"][:, :], raw[:, 1, :])
            dve.tensor_copy(g["select"][:, :, :].rearrange("k e p -> k (e p)"), raw_sel[:, :])
            if 3 in LAYERS:
                dve.tensor_copy(g["decay_hi"][:, :], raw_dec[:, :]).then_inc(narrowed, 1)
                dve.wait_ge(narrowed, 1)
                dve.tensor_tensor(g["decay_lo"][:, :], raw_dec[:, :],
                                  g["decay_hi"][:, :].bitcast(F32), ALU.subtract)
    return g


def store_x(nc, g, out):
    with ExitStack() as ctx:
        stored = nc.alloc_semaphore(name="stored")
        block = ctx.enter_context(nc.Block())

        @block.sync
        def _(sync):
            blocks = out.rearrange("(t p) d -> p t d", p=P)
            for b in range(B):
                sync.dma_start(blocks[:, b * NB:(b + 1) * NB, :],
                               g["x"][:, b * NB:(b + 1) * NB, :]).then_inc(stored, 16)
            sync.wait_ge(stored, 16 * B)


LAYERS = (0, 1, 2, 3)


def build(nc, dram, out):
    with ExitStack() as ctx:
        g = load_constants(nc, ctx, dram)
        for layer in LAYERS:
            ops = {k.split("_", 1)[1]: v for k, v in dram.items() if k.startswith(f"l{layer}_")}
            (softmax_layer if layer % 2 else linear_layer)(nc, layer, g, ops)
        store_x(nc, g, out)


def lay_out(a):
    c = np.ascontiguousarray
    r = {"L0_attn_x": a["L0_attn_x"].reshape(B * T, D)}

    def four(w):
        return np.tile(w.reshape(D, 4, 1, 32), (1, 1, 4, 1)).reshape(D, 4, P)

    def rows(v):
        return c(np.broadcast_to(v[None, :], (P, v.shape[0])))

    r["l0_wqkv"] = c(a["L0_attn_w_attn"].T)
    r["l0_wo"] = c(a["L0_attn_w_proj"].T)
    r["l0_wr"] = c(a["L0_ffn_gate_w"].T)
    r["l0_rbias"] = rows(a["L0_ffn_expert_bias"])
    gate = np.concatenate([a["L0_ffn_w_gate"], a["L0_ffn_shared_gate_w"][None]])
    up = np.concatenate([a["L0_ffn_w_up"], a["L0_ffn_shared_up_w"][None]])
    down = np.concatenate([a["L0_ffn_w_down"], a["L0_ffn_shared_down_w"][None]])
    r["l0_wup"] = c(np.stack([gate, up], 1).transpose(3, 0, 1, 2).reshape(D, -1))
    r["l0_wdn"] = c(down.transpose(2, 0, 1))
    qkv, bias = a["L1_attn_qkv_w"], a["L1_attn_qkv_b"]
    r["l1_wqk"] = c(np.stack([four(qkv[:, :D]), four(qkv[:, D:2 * D])], 1).reshape(D, -1))
    r["l1_bqk"] = c(np.stack([four(np.broadcast_to(v, (D, D)))[0].T
                              for v in (bias[:D], bias[D:2 * D])], 1))
    r["l1_wv"] = c(qkv[:, 2 * D:])
    r["l1_bv"] = rows(bias[2 * D:])
    r["l1_wo"], r["l1_bo"] = a["L1_attn_out_w"], c(a["L1_attn_out_b"][:, None])
    r["l1_wr"] = c(a["L1_ffn_Wg"].T)
    r["l1_wup"] = c(a["L1_ffn_W1"].transpose(1, 0, 2).reshape(D, -1))
    r["l1_wdn"] = c(a["L1_ffn_W2"].reshape(E8, FC, P, D).transpose(2, 0, 1, 3))
    r["l2_wqkv"] = c(np.concatenate([a[f"L2_attn_W{n}"].T for n in "qkv"], 1))
    r["l2_wo"], r["l2_bo"] = c(a["L2_attn_Wo"].T), rows(a["L2_attn_bo"])
    r["l2_wfc"] = c(a["L2_ffn_W_fc"].T)
    r["l2_wproj"] = c(a["L2_ffn_W_proj"].reshape(D, 4, P).transpose(2, 1, 0).reshape(P, -1))
    r["l2_lnw"] = c(a["L2_ffn_ln_w"].reshape(4, P).T)
    r["l2_lnb"] = c(a["L2_ffn_ln_b"].reshape(4, P).T)
    r["l3_wqk"] = c(np.stack([four(a["L3_attn_Wq"]), four(a["L3_attn_Wk"])], 1).reshape(D, -1))
    r["l3_bqk"] = c(np.stack([four(np.broadcast_to(v, (D, D)))[0].T
                              for v in (a["L3_attn_bq"], a["L3_attn_bk"])], 1))
    r["l3_wv"], r["l3_bv"] = a["L3_attn_Wv"], rows(a["L3_attn_bv"])
    r["l3_wo"], r["l3_bo"] = a["L3_attn_Wo"], c(a["L3_attn_bo"][:, None])
    r["l3_wr"] = c(a["L3_ffn_router_w"].T)
    r["l3_wup"] = c(a["L3_ffn_w1"].transpose(2, 0, 1).reshape(D, -1))
    r["l3_b1"] = c(a["L3_ffn_b1"].reshape(E8, FC, P).transpose(2, 0, 1))
    r["l3_wdn"] = c(a["L3_ffn_w2"].transpose(2, 0, 1).reshape(FC, P, E8, D).transpose(1, 2, 0, 3))
    r["l3_b2"] = c(a["L3_ffn_b2"].T)
    return {k: c(v) for k, v in {**r, **constants()}.items()}


def kernel(**inputs):
    import concourse.bacc as bacc
    from concourse.bass_utils import run_bass_kernel_spmd

    arrays = lay_out({k: np.asarray(v) for k, v in inputs.items()})
    nc = bacc.Bacc("TRN2", target_bir_lowering=False, num_devices=1)
    dram = {k: nc.dram_tensor(k, v.shape, mybir.dt.from_np(v.dtype), kind="ExternalInput").ap()
            for k, v in arrays.items()}
    out = nc.dram_tensor("x_out", (B * T, D), F32, kind="ExternalOutput").ap()
    build(nc, dram, out)
    r = run_bass_kernel_spmd(nc, [arrays], core_ids=[0])
    return r.results[0]["x_out"].reshape(B, T, D)
```

```python
from contextlib import ExitStack

import numpy as np

import concourse.bass as bass
from concourse import mybir

F32 = mybir.dt.float32
F32R = mybir.dt.float32r
BF16 = mybir.dt.bfloat16
ALU = mybir.AluOpType
ACT = mybir.ActivationFunctionType
AX = mybir.AxisListType

P = 128
D = 128
B, T = 8, 512
NB = T // P
H, HD = 16, 8
LN_EPS = 1e-5
EXP_LN = "natural_log_exp_and_others"
NEG = -1e30




class Semaphores:

    def __init__(self, nc, ctx):
        self.nc, self.made = nc, []
        ctx.callback(self.clear)

    def new(self, name):
        self.made.append(self.nc.alloc_semaphore(name=name))
        return self.made[-1]

    def clear(self):
        self.nc.clear_and_free_semaphores(self.made)
        self.nc.all_engine_barrier()


class Signal:

    def __init__(self, sems, name, per):
        self.sem, self.per = sems.new(name), per

    def now(self, b, n):
        return (b + 1) * self.per + n

    def before(self, b, n):
        return b * self.per + n


def signals(sems, layer, **per):
    return {k: Signal(sems, f"{k}_{layer}", n) for k, n in per.items()}


def block_of(x_res, b, i):
    return x_res[:, bass.ds(b * NB + i, 1), :].rearrange("p a d -> p (a d)")




def prep_vector(dve, s, m, k):
    for i in range(NB):
        dve.bn_stats(m["stats"][:, i, :], block_of(m["x"], k, i)).then_inc(s["stats"].sem, 1)
    for i in range(NB):
        dve.wait_ge(s["stats"].sem, s["stats"].now(k, i + 1))
        dve.sem_inc(m["passed"], 1)
        dve.bn_aggr(m["mean_var"][:, i, :], m["stats"][:, i, :]).then_inc(s["mean_var"].sem, 1)
    dve.wait_ge(s["rstd"].sem, s["rstd"].now(k, 1))
    dve.wait_ge(s["xnT_ps"].sem, s["xnT_ps"].before(k, 1))
    for i in range(NB):
        dve.tensor_scalar(m["xn"][:, i, :], block_of(m["x"], k, i), m["mean_var"][:, i, 0:1],
                          m["rstd"][:, i:i + 1], ALU.subtract, ALU.mult).then_inc(s["xn"].sem, 1)


def prep_gpsimd(pool, s, m, k):
    pool.wait_ge(s["mean_var"].sem, s["mean_var"].now(k, NB))
    pool.sem_inc(m["passed"], 1)
    pool.tensor_scalar(m["var_eps"][:, :], m["mean_var"][:, :, 1], LN_EPS, 1.0, ALU.add,
                       ALU.mult).then_inc(s["var_eps"].sem, 1)
    pool.wait_ge(s["var_eps"].sem, s["var_eps"].now(k, 1))
    pool.tensor_tensor(m["rstd"][:, :], m["var_eps"][:, :], m["minus_half"][:, :],
                       ALU.pow).then_inc(s["rstd"].sem, 1)


def prep_tensor(pe, s, m, k, bank):
    pe.wait_ge(s["xn"].sem, s["xn"].now(k, NB))
    for i in range(NB):
        last = pe.transpose(bank[:, i * P:(i + 1) * P], m["xn"][:, i, :], m["ident"][:, :])
    last.then_inc(s["xnT_ps"].sem, 1)


def prep_scalar(act, s, m, k, bank):
    act.wait_ge(s["xnT_ps"].sem, s["xnT_ps"].now(k, 1))
    act.activation(m["xnT"][:, :], bank[:, :], ACT.Copy).then_inc(s["xnT"].sem, 1)
    act.activation(m["xnT_hi"][:, :], bank[:, :], ACT.Copy).then_inc(s["xnT_hi"].sem, 1)


def prep_vector_lo(dve, s, m, k, bank):
    dve.wait_ge(s["xnT_hi"].sem, s["xnT_hi"].now(k, 1))
    dve.tensor_tensor(m["xnT_lo"][:, :], bank[:, :], m["xnT_hi"][:, :].bitcast(F32),
                      ALU.subtract).then_inc(s["xnT_lo"].sem, 1)


PREP = dict(stats=NB, mean_var=NB, var_eps=1, rstd=1, xn=NB, xnT_ps=1, xnT=1, xnT_hi=1, xnT_lo=1)


def prep_tiles(m, sb):
    m["stats"] = sb("stats", [P, NB, 6], F32)
    m["mean_var"] = sb("mean_var", [P, NB, 2], F32)
    m["var_eps"] = sb("var_eps", [P, NB], F32)
    m["rstd"] = sb("rstd", [P, NB], F32)
    m["xn"] = sb("xn", [P, NB, D], F32)
    m["xnT"] = sb("xnT", [P, T], F32)
    m["xnT_hi"] = sb("xnT_hi", [P, T], F32R)
    m["xnT_lo"] = sb("xnT_lo", [P, T], F32R)


def product3(pe, out, w_hi, w_lo, m):
    pe.matmul(out, w_hi, m["xnT_hi"][:, :], start=True, stop=False)
    pe.matmul(out, w_lo, m["xnT_hi"][:, :], start=False, stop=False)
    return pe.matmul(out, w_hi, m["xnT_lo"][:, :], start=False, stop=True)




def split_gpsimd(pool, done, hi, lo, stage, n0):
    pool.tensor_scalar(hi, stage, 1.0, 1.0, ALU.mult, ALU.mult).then_inc(done, 1)
    pool.wait_ge(done, 2 * n0 + 1)
    pool.tensor_tensor(lo, stage, hi.bitcast(F32), ALU.subtract).then_inc(done, 1)





E8, FC = 8, 4
CHUNKS = [(0, 512, 0), (0, 384, 512), (128, 384, 1024)]
PW = 1408
PV_AT = [(0, 0, 0), (1, 128, 512), (3, 256, 896), (2, 256, 1152)]
HALVES = [(0, 896), (896, PW)]
AHEAD_MAX = 5
MAX_AT = [(5, 256, 128), (5, 0, 256), (4, 0, 384), (3, 0, 512)]


def softmax_layer(nc, layer, g, d):
    power_law = layer == 3
    with ExitStack() as ctx:
        sems = Semaphores(nc, ctx)

        def sb(name, shape, dt):
            return ctx.enter_context(nc.sbuf_tensor(f"{name}_{layer}", shape, dt))

        m = dict(g)
        prep_tiles(m, sb)
        NPIECE = E8 * FC * P // 512
        wup_hi = sb("wup_hi", [P, E8 * FC * P], F32R)
        wup_lo = sb("wup_lo", [P, E8 * FC * P], F32R)
        wdn = sb("wdn", [P, E8, FC, D], F32)
        wqk_hi = sb("wqk_hi", [P, 2, 4, P], F32R)
        wqk_lo = sb("wqk_lo", [P, 2, 4, P], F32R)
        wv = sb("wv", [P, D], F32)
        wo = sb("wo", [P, 2, D], F32)
        wr = sb("wr", [P, E8], F32)
        bqk = sb("bqk", [P, 2, 4], F32)
        bv = sb("bv", [P, D], F32)
        bo = sb("bo", [P, 1], F32)
        b1 = sb("b1", [P, E8, FC], F32)
        b2 = sb("b2", [P, E8], F32)
        q4 = sb("q4", [P, 4, T], F32R)
        k4 = sb("k4", [P, 4, T], F32R)
        qm = sb("qm", [P, 8, T], F32R)
        v_f = sb("v_f", [P, NB, D], F32)
        vs = sb("vs", [P, 2, NB, 4, P], F32R)
        probs = sb("probs", [P, 2, PW], F32)
        p_hi = sb("p_hi", [P, 2, PW], F32R)
        p_lo = sb("p_lo", [P, 2, PW], F32R)
        neg_max = sb("neg_max", [P, NB, 112], F32)
        den_inv = sb("den_inv", [P, T], F32)
        o_t = sb("o_t", [P, 2, T], F32)
        s_t = sb("s_t", [P, T], F32)
        lg = sb("lg", [P, NB, 16], F32)
        top = sb("top", [P, NB, 8], F32)
        two = sb("two", [P, NB, 8], F32)
        rest = sb("rest", [P, NB, 16], F32)
        chosen = sb("chosen", [P, NB, E8], F32)
        lg_rel = sb("lg_rel", [P, NB, E8], F32)
        lg_exp = sb("lg_exp", [P, NB, E8], F32)
        c_raw = sb("c_raw", [P, NB, E8], F32)
        c_sum = sb("c_sum", [P, NB], F32)
        c_inv = sb("c_inv", [P, NB], F32)
        c_tok = sb("c_tok", [P, NB, E8], F32)
        c_t = sb("c_t", [64, T], F32R)
        hid = sb("hid", [P, 3, T], F32)
        c_all = sb("c_all", [P, T], F32)
        y_one = sb("y_one", [P, T], F32)
        acc = sb("acc", [P, T], F32)
        gate = y_one
        upd = den_inv
        select = sb("select", [64, E8, P], F32R)

        NH = len(range(E8 * FC))
        s = signals(sems, layer, **PREP, qk_ps=8, qk_hi=8, qk_lo=8, qm=16, v_ps=1,
                    v_f=1, vs=8, max_ps=64, neg_max=64, maxT=4, max_t=4, qm_max=16, s_ps=48,
                    probs=48, p_hi=32, p_lo=32, pv=16, den_ln=4, den_inv=4, o_t=4, s_ps_out=1,
                    s_t=1,
                    lg_ps=1, route=16, lg_exp=1, cT_ps=1, c_hi=1, c_lo=1, c_ps=E8, c_all=E8,
                    up=NH, hid=NH, dn=NH, y_mul=E8, y=E8 - 1, gate=1, upd=1, updT=1, x_new=1)
        setup = sems.new(f"setup_{layer}")
        m["passed"] = sems.new(f"passed_{layer}")
        w_small = sems.new(f"w_small_{layer}")
        stage = [acc, y_one, c_all, s_t]
        w_stage = [sems.new(f"w_stage{i}_{layer}") for i in range(len(stage))]
        w_hi = sems.new(f"w_hi_{layer}")
        w_lo = sems.new(f"w_lo_{layer}")
        w_down = sems.new(f"w_down_{layer}")
        block = ctx.enter_context(nc.Block())
        bank = g["bank"]
        QK_SPLITS = 4
        small = [(wv, d["wv"]), (wo, d["wo"]), (wr, d["wr"]), (bqk, d["bqk"]), (bv, d["bv"]),
                 (bo, d["bo"])]
        if power_law:
            small += [(b1, d["b1"]), (b2, d["b2"])]
        N_SMALL = 16 * len(small)
        N_SPLIT = QK_SPLITS + NPIECE
        N_PIECES = N_SPLIT + E8 * P // 512

        def piece(n):
            if n < QK_SPLITS:
                c = slice(n * 2 * P, (n + 1) * 2 * P)
                flat = [w[:, :, :, :].rearrange("p a g c -> p (a g c)") for w in (wqk_hi, wqk_lo)]
                return flat[0][:, c], flat[1][:, c], d["wqk"][:, c]
            if n < N_SPLIT:
                c = slice((n - QK_SPLITS) * 512, (n - QK_SPLITS + 1) * 512)
                return wup_hi[:, c], wup_lo[:, c], d["wup"][:, c]
            c = slice((n - N_SPLIT) * 512, (n - N_SPLIT + 1) * 512)
            return select[:, :, :].rearrange("k e p -> k (e p)")[:, c], None, d["select"][:, c]

        def staged(n):
            src = piece(n)[2]
            return stage[n % len(stage)][0:src.shape[0], 0:src.shape[1]]

        @block.sync
        def _(sync):
            for x in s.values():
                sync.sem_inc(x.sem, x.per)
            for tile, src in small:
                sync.dma_start(tile[:], src).then_inc(w_small, 16)
            for n in range(N_PIECES):
                if n >= len(stage):
                    sync.wait_ge(w_lo, n - len(stage) + 1)
                sync.dma_start(staged(n), piece(n)[2]).then_inc(w_stage[n % len(stage)], 16)
                if n == QK_SPLITS:
                    sync.dma_start(wdn[:], d["wdn"]).then_inc(w_down, 16)

        SETUP = 8 + 8

        @block.gpsimd
        def _(pool):
            prep_gpsimd(pool, s, m, 0)
            fills = [(k4[96:P, :, :].bitcast(F32), 1.0), (qm[96:P, :, :].bitcast(F32), 0.0),
                     (neg_max[:, :, :], 0.0), (c_t[:, :].bitcast(F32), 0.0), (lg[:, :, :], -3e38),
                     (two[:, :, :], -3e38), (probs[:, :, 896:1024], 0.0),
                     (vs[:, :, :, :, :].bitcast(F32), 0.0)]
            for par in range(2):
                for j in range(4):
                    c = 64 * (1 - par) + 16 * j
                    fills.append((vs[:, par, :, j, c:c + 16].bitcast(F32), 1.0))
            pool.wait_ge(s["rstd"].sem, s["rstd"].now(0, 1))
            for n, (tile, value) in enumerate(fills):
                if n:
                    pool.wait_ge(setup, n)
                pool.memset(tile, value).then_inc(setup, 1)

            with pool.Fori(0, B) as b:
                def masked(h):
                    gr = h // 4
                    pool.wait_ge(s["qk_lo"].sem, s["qk_lo"].now(b, 2 * gr + 1))
                    if h < 8:
                        pool.wait_ge(s["s_ps"].sem, s["s_ps"].before(b, 3 * (h + 8) + 3))
                    else:
                        pool.wait_ge(s["s_ps"].sem, s["s_ps"].now(b, 3 * (h - 8) + 3))
                    pool.sem_inc(m["passed"], 1)
                    pool.tensor_scalar(qm[0:96, h % 8, :], q4[0:96, gr, :].bitcast(F32),
                                       g["head_mask"][0:96, h:h + 1], 1.0, ALU.mult,
                                       ALU.mult).then_inc(s["qm"].sem, 1)

                def masked_max(h):
                    gr = h // 4
                    pool.wait_ge(s["max_t"].sem, s["max_t"].now(b, gr + 1))
                    pool.wait_ge(s["qm"].sem, s["qm"].now(b, (8, 11, 15, 16)[gr]))
                    if h:
                        pool.wait_ge(s["qm_max"].sem, s["qm_max"].now(b, h))
                    pool.sem_inc(m["passed"], 1)
                    pool.tensor_scalar(qm[96:112, h % 8, :], q4[96:112, gr, :].bitcast(F32),
                                       g["head_mask"][96:112, h:h + 1], 1.0, ALU.mult,
                                       ALU.mult).then_inc(s["qm_max"].sem, 1)

                for h in range(8):
                    masked(h)
                for gr in range(4):
                    for h in range(4 * gr, 4 * gr + 4):
                        masked_max(h)
                    for h in range(4 * gr + 7, 4 * gr + 11):
                        if 8 <= h < H:
                            pool.wait_ge(s["qm_max"].sem, s["qm_max"].now(b, 4 * gr + 4))
                            masked(h)
                pool.wait_ge(s["qm_max"].sem, s["qm_max"].now(b, 16))
                prep_gpsimd(pool, s, m, b + 1)
                pool.wait_ge(s["gate"].sem, s["gate"].now(b, 1))
                pool.wait_ge(s["updT"].sem, s["updT"].before(b, 1))
                pool.tensor_tensor(upd[:, :], gate[:, :], s_t[:, :], ALU.mult)\
                    .then_inc(s["upd"].sem, 1)

        @block.scalar
        def _(act):
            act.preload_act_table_set(EXP_LN)
            prep_scalar(act, s, m, 0, bank[7])
            for n in range(N_PIECES):
                act.wait_ge(w_stage[n % len(stage)], 16 * (n // len(stage) + 1))
                act.activation(piece(n)[0], staged(n), ACT.Copy).then_inc(w_hi, 1)
            act.wait_ge(w_small, N_SMALL)
            act.wait_ge(w_lo, N_SPLIT)
            act.wait_ge(setup, SETUP)
            with act.Fori(0, B) as b:
                act.preload_act_table_set(EXP_LN)
                for n in range(8):
                    a, gr = n % 2, n // 2
                    act.wait_ge(s["qk_ps"].sem, s["qk_ps"].now(b, n + 1))
                    if n == 0:
                        act.wait_ge(s["qm"].sem, s["qm"].before(b, 16))
                        act.wait_ge(s["s_ps"].sem, s["s_ps"].before(b, 48))
                    out = (k4 if a else q4)[0:96, gr, :]
                    act.activation(out, bank[3 + n % 4][0:96, :], ACT.Identity,
                                   bias=bqk[0:96, a, gr:gr + 1]).then_inc(s["qk_hi"].sem, 1)

                def router_exp():
                    act.wait_ge(s["route"].sem, s["route"].now(b, 12))
                    act.activation(lg_exp[:, :, :], lg_rel[:, :, :], ACT.Exp)\
                        .then_inc(s["lg_exp"].sem, 1)

                def max_to_sbuf(gr):
                    act.wait_ge(s["maxT"].sem, s["maxT"].now(b, gr + 1))
                    act.activation(q4[96:112, gr, :], bank[5][96:112, :], ACT.Copy)\
                        .then_inc(s["max_t"].sem, 1)

                def exps(h):
                    for c, (lo, n, at) in enumerate(CHUNKS):
                        act.wait_ge(s["s_ps"].sem, s["s_ps"].now(b, 3 * h + c + 1))
                        if c == 0:
                            if h >= 2:
                                act.wait_ge(s["p_lo"].sem, s["p_lo"].now(b, 2 * h - 2))
                            else:
                                act.wait_ge(s["p_lo"].sem, s["p_lo"].before(b, 30 + 2 * h))
                        act.activation(probs[:, h % 2, at:at + n], bank[c][:, lo:lo + n], ACT.Exp,
                                       scale=float(HD) ** -0.5).then_inc(s["probs"].sem, 1)
                    for k, (lo, end) in enumerate(HALVES):
                        act.wait_ge(s["probs"].sem, s["probs"].now(b, 3 * h + 2 + k))
                        if k == 0:
                            if h >= 2:
                                act.wait_ge(s["pv"].sem, s["pv"].now(b, h - 1))
                            else:
                                act.wait_ge(s["pv"].sem, s["pv"].before(b, 15 + h))
                        act.activation(p_hi[:, h % 2, lo:end], probs[:, h % 2, lo:end], ACT.Copy)\
                            .then_inc(s["p_hi"].sem, 1)

                def denominator(gr):
                    rows = slice(64, 128) if gr % 2 == 0 else slice(0, 64)
                    act.wait_ge(s["pv"].sem, s["pv"].now(b, 4 * gr + 4))
                    if gr >= 2:
                        act.wait_ge(s["o_t"].sem, s["o_t"].now(b, gr - 1))
                    else:
                        act.wait_ge(s["o_t"].sem, s["o_t"].before(b, gr + 3))
                    act.activation(den_inv[rows, :], bank[6 + gr % 2][rows, :], ACT.Ln)\
                        .then_inc(s["den_ln"].sem, 1)
                    act.wait_ge(s["den_ln"].sem, s["den_ln"].now(b, gr + 1))
                    act.activation(den_inv[rows, :], den_inv[rows, :], ACT.Exp, scale=-1.0)\
                        .then_inc(s["den_inv"].sem, 1)

                max_to_sbuf(0)
                router_exp()
                for h in range(H):
                    exps(h)
                    if h % 4 == 2 and h + 4 < H:
                        max_to_sbuf(h // 4 + 1)
                    if h % 4 == 1 and h > 4:
                        denominator(h // 4 - 1)
                denominator(3)

                def hidden(n):
                    e, f = n // FC, n % FC
                    act.wait_ge(s["up"].sem, s["up"].now(b, n + 1))
                    if n >= 3:
                        act.wait_ge(s["dn"].sem, s["dn"].now(b, n - 2))
                    else:
                        act.wait_ge(s["dn"].sem, s["dn"].before(b, NH - 2 + n))
                    act.activation(hid[:, n % 3, :], bank[n % 3][:, :],
                                   ACT.Gelu if power_law else ACT.Silu,
                                   bias=b1[:, e, f:f + 1] if power_law else 0.0)\
                        .then_inc(s["hid"].sem, 1)

                hidden(0)
                hidden(1)
                act.wait_ge(s["s_ps_out"].sem, s["s_ps_out"].now(b, 1))
                act.wait_ge(s["upd"].sem, s["upd"].before(b, 1))
                act.activation(s_t[:, :], bank[6][:, :], ACT.Identity, bias=bo[:, 0:1])\
                    .then_inc(s["s_t"].sem, 1)
                act.wait_ge(s["cT_ps"].sem, s["cT_ps"].now(b, 1))
                act.wait_ge(s["c_ps"].sem, s["c_ps"].before(b, E8))
                act.activation(c_t[0:E8, :], bank[7][0:E8, :], ACT.Copy).then_inc(s["c_hi"].sem, 1)
                for e in range(E8):
                    for f in range(FC):
                        if e or f >= 2:
                            hidden(e * FC + f)
                    act.wait_ge(s["c_ps"].sem, s["c_ps"].now(b, e + 1))
                    if e:
                        act.wait_ge(s["y_mul"].sem, s["y_mul"].now(b, e))
                    else:
                        act.wait_ge(s["y_mul"].sem, s["y_mul"].before(b, E8))
                    act.activation(c_all[:, :], bank[5][:, :], ACT.Copy).then_inc(s["c_all"].sem, 1)
                prep_scalar(act, s, m, b + 1, bank[7])
                act.wait_ge(s["y"].sem, s["y"].now(b, E8 - 1))
                act.activation(gate[:, :], acc[:, :], ACT.Silu).then_inc(s["gate"].sem, 1)

        @block.vector
        def _(dve):
            prep_vector(dve, s, m, 0)
            prep_vector_lo(dve, s, m, 0, bank[7])
            dve.wait_ge(w_small, N_SMALL)
            dve.wait_ge(setup, SETUP)
            for n in range(N_SPLIT):
                dve.wait_ge(w_hi, n + 1)
                hi, lo, _ = piece(n)
                dve.tensor_tensor(lo, staged(n), hi.bitcast(F32), ALU.subtract).then_inc(w_lo, 1)
            dve.wait_ge(w_hi, N_PIECES)
            with dve.Fori(0, B) as b:
                def values():
                    dve.wait_ge(s["v_ps"].sem, s["v_ps"].now(b, 1))
                    dve.wait_ge(s["vs"].sem, s["vs"].before(b, 8))
                    dve.tensor_tensor(v_f[:, :, :],
                                      bank[7][:, :].rearrange("p (i e) -> p i e", i=NB),
                                      bv[:, :].unsqueeze(1).to_broadcast([P, NB, D]), ALU.add)\
                        .then_inc(s["v_f"].sem, 1)

                def group_values(gr):
                    dve.wait_ge(s["v_f"].sem, s["v_f"].now(b, 1))
                    if gr >= 2:
                        dve.wait_ge(s["pv"].sem, s["pv"].now(b, 4 * (gr - 1)))
                    else:
                        dve.wait_ge(s["pv"].sem, s["pv"].before(b, 4 * (gr + 3)))
                    par = gr % 2
                    v = v_f[:, :, 32 * gr:32 * gr + 32].rearrange("p i (j e) -> p i j e", j=4)

                    def part(at):
                        t0 = vs[:, par, 0, 0, 64 * par + at:64 * par + at + HD]
                        return bass.AP(tensor=t0.tensor, offset=t0.offset,
                                       ap=[t0.ap[0], [4 * P, NB], [P + 16, 4], [1, HD]])

                    dve.tensor_copy(part(0), v).then_inc(s["vs"].sem, 1)
                    dve.wait_ge(s["vs"].sem, s["vs"].now(b, 2 * gr + 1))
                    dve.tensor_tensor(part(HD), v, part(0).bitcast(F32), ALU.subtract)\
                        .then_inc(s["vs"].sem, 1)

                def route(n):
                    dve.wait_ge(s["route"].sem, s["route"].now(b, n))

                def route_top():
                    dve.wait_ge(s["lg_ps"].sem, s["lg_ps"].now(b, 1))
                    dve.tensor_copy(lg[:, :, 0:E8],
                                    bank[7][:, 0:NB * E8].rearrange("p (i e) -> p i e", i=NB))\
                        .then_inc(s["route"].sem, 1)
                    route(1)
                    dve.sem_inc(m["passed"], 1)
                    for i in range(NB):
                        dve.max(top[:, i, :], lg[:, i, :]).then_inc(s["route"].sem, 1)
                    route(5)
                    dve.tensor_copy(two[:, :, 0:2], top[:, :, 0:2]).then_inc(s["route"].sem, 1)
                    route(6)
                    dve.sem_inc(m["passed"], 1)
                    for i in range(NB):
                        dve.match_replace(rest[:, i, :], two[:, i, :], lg[:, i, :], 3e38)\
                            .then_inc(s["route"].sem, 1)
                    route(10)
                    dve.tensor_tensor(chosen[:, :, :], rest[:, :, 0:E8], lg[:, :, 0:E8],
                                      ALU.not_equal).then_inc(s["route"].sem, 1)
                    dve.tensor_tensor(lg_rel[:, :, :], lg[:, :, 0:E8],
                                      top[:, :, 0:1].to_broadcast([P, NB, E8]), ALU.subtract)\
                        .then_inc(s["route"].sem, 1)

                def route_rest():
                    dve.wait_ge(s["lg_exp"].sem, s["lg_exp"].now(b, 1))
                    dve.tensor_tensor(c_raw[:, :, :], lg_exp[:, :, :], chosen[:, :, :], ALU.mult)\
                        .then_inc(s["route"].sem, 1)
                    route(13)
                    dve.tensor_reduce(c_sum[:, :], c_raw[:, :, :], AX.X, ALU.add)\
                        .then_inc(s["route"].sem, 1)
                    route(14)
                    dve.reciprocal(c_inv[:, :], c_sum[:, :]).then_inc(s["route"].sem, 1)
                    route(15)
                    dve.wait_ge(s["cT_ps"].sem, s["cT_ps"].before(b, 1))
                    dve.tensor_tensor(c_tok[:, :, :], c_raw[:, :, :],
                                      c_inv[:, :].unsqueeze(2).to_broadcast([P, NB, E8]),
                                      ALU.mult).then_inc(s["route"].sem, 1)

                for n in range(8):
                    a, gr = n % 2, n // 2
                    rows = slice(64, 96) if a == 0 else slice(32, 64)
                    tile = (k4 if a else q4)[:, gr, :]
                    dve.wait_ge(s["qk_hi"].sem, s["qk_hi"].now(b, n + 1))
                    dve.scalar_tensor_tensor(out=tile[rows, :], in0=bank[3 + n % 4][rows, :],
                                             scalar=bqk[rows, a, gr:gr + 1],
                                             in1=tile[rows, :].bitcast(F32), op0=ALU.add,
                                             op1=ALU.subtract).then_inc(s["qk_lo"].sem, 1)
                    if n == 3:
                        values()
                group_values(0)
                group_values(1)
                route_top()

                def neg_maxima(h):
                    if h % 4 == 0:
                        if h:
                            dve.wait_ge(s["maxT"].sem, s["maxT"].now(b, h // 4))
                        else:
                            dve.wait_ge(s["maxT"].sem, s["maxT"].before(b, 4))
                    for k, i in enumerate(reversed(range(NB))):
                        bk, lo, n = MAX_AT[i]
                        ready = 4 * h + (k + 1 if k < 2 else 4)
                        dve.wait_ge(s["max_ps"].sem, s["max_ps"].now(b, ready))
                        dve.tensor_reduce(neg_max[:, i, 96 + h:97 + h], bank[bk][:, lo:lo + n],
                                          AX.X, ALU.max, negate=True)\
                            .then_inc(s["neg_max"].sem, 1)

                def normalise(gr):
                    num = slice(64, 128) if gr % 2 else slice(0, 64)
                    den = slice(0, 64) if gr % 2 else slice(64, 128)
                    dve.wait_ge(s["den_inv"].sem, s["den_inv"].now(b, gr + 1))
                    if gr == 0:
                        dve.wait_ge(s["s_ps_out"].sem, s["s_ps_out"].before(b, 1))
                    dve.tensor_tensor(o_t[num, gr // 2, :], bank[6 + gr % 2][num, :],
                                      den_inv[den, :], ALU.mult).then_inc(s["o_t"].sem, 1)

                def lower(h):
                    for k, (lo, end) in enumerate(HALVES):
                        dve.wait_ge(s["p_hi"].sem, s["p_hi"].now(b, 2 * h + k + 1))
                        dve.tensor_tensor(p_lo[:, h % 2, lo:end], probs[:, h % 2, lo:end],
                                          p_hi[:, h % 2, lo:end].bitcast(F32), ALU.subtract)\
                            .then_inc(s["p_lo"].sem, 1)

                for h in range(AHEAD_MAX):
                    neg_maxima(h)
                route_rest()
                for h in range(H):
                    if h + AHEAD_MAX < H:
                        neg_maxima(h + AHEAD_MAX)
                    lower(h)
                    if h % 4 == 2 and h > 4:
                        normalise(h // 4 - 1)
                        if h // 4 < 3:
                            group_values(h // 4 + 1)
                normalise(3)
                dve.wait_ge(s["c_hi"].sem, s["c_hi"].now(b, 1))
                dve.tensor_tensor(c_t[32:32 + E8, :], bank[7][0:E8, :],
                                  c_t[0:E8, :].bitcast(F32), ALU.subtract)\
                    .then_inc(s["c_lo"].sem, 1)
                for e in range(E8):
                    dve.wait_ge(s["dn"].sem, s["dn"].now(b, FC * (e + 1)))
                    dve.wait_ge(s["c_all"].sem, s["c_all"].now(b, e + 1))
                    if e == 0:
                        dve.wait_ge(s["gate"].sem, s["gate"].before(b, 1))
                    elif e > 1:
                        dve.wait_ge(s["y"].sem, s["y"].now(b, e - 1))
                    out = y_one[:, :] if e else acc[:, :]
                    if power_law:
                        dve.scalar_tensor_tensor(out=out, in0=bank[3 + e % 2][:, :],
                                                 scalar=b2[:, e:e + 1], in1=c_all[:, :],
                                                 op0=ALU.add, op1=ALU.mult)\
                            .then_inc(s["y_mul"].sem, 1)
                    else:
                        dve.tensor_tensor(out, bank[3 + e % 2][:, :], c_all[:, :], ALU.mult)\
                            .then_inc(s["y_mul"].sem, 1)
                    if e:
                        dve.wait_ge(s["y_mul"].sem, s["y_mul"].now(b, e + 1))
                        dve.tensor_tensor(acc[:, :], acc[:, :], y_one[:, :], ALU.add)\
                            .then_inc(s["y"].sem, 1)
                    if e == 2:
                        prep_vector(dve, s, m, b + 1)
                prep_vector_lo(dve, s, m, b + 1, bank[7])
                dve.wait_ge(s["updT"].sem, s["updT"].now(b, 1))
                xb = g["x"][:, bass.ds(b * NB, NB), :]
                dve.tensor_tensor(xb, xb, bank[6][:, :].rearrange("p (i d) -> p i d", i=NB),
                                  ALU.add).then_inc(s["x_new"].sem, 1)

        @block.tensor
        def _(pe):
            prep_tensor(pe, s, m, 0, bank[7])
            pe.wait_ge(w_small, N_SMALL)
            pe.wait_ge(setup, SETUP)
            pe.wait_ge(w_lo, N_SPLIT)
            pe.wait_ge(w_hi, N_PIECES)

            def queries_keys(k, n):
                a, gr = n % 2, n // 2
                if n >= 4:
                    pe.wait_ge(s["qk_lo"].sem, s["qk_lo"].now(k, n - 3))
                elif n < 2:
                    pe.wait_ge(s["y_mul"].sem, s["y_mul"].before(k, E8 - 1 + n))
                elif n == 2:
                    pe.wait_ge(s["c_all"].sem, s["c_all"].before(k, E8))
                else:
                    pe.wait_ge(s["x_new"].sem, s["x_new"].before(k, 1))
                product3(pe, bank[3 + n % 4][:, :], wqk_hi[:, a, gr, :], wqk_lo[:, a, gr, :],
                         m).then_inc(s["qk_ps"].sem, 1)

            def first_queries_keys(k):
                pe.wait_ge(s["xnT_hi"].sem, s["xnT_hi"].now(k, 1))
                pe.wait_ge(s["xnT_lo"].sem, s["xnT_lo"].now(k, 1))
                for n in range(3):
                    queries_keys(k, n)

            first_queries_keys(0)
            with pe.Fori(0, B) as b:
                pe.wait_ge(s["xnT"].sem, s["xnT"].now(b, 1))

                def per_block(w, n, signal):
                    for i in range(NB):
                        last = pe.matmul(bank[7][:, i * n:(i + 1) * n],
                                         m["xnT"][:, i * P:(i + 1) * P], w, start=True, stop=True)
                    last.then_inc(s[signal].sem, 1)

                def max_scores(h):
                    gr = h // 4
                    pe.wait_ge(s["qm"].sem, s["qm"].now(b, h + 1))
                    if h == 0:
                        pe.wait_ge(s["qk_lo"].sem, s["qk_lo"].now(b, 8))
                    for k, i in enumerate(reversed(range(NB))):
                        bk, lo, n = MAX_AT[i]
                        n = max(n, 256)
                        if h and k < 3:
                            pe.wait_ge(s["neg_max"].sem,
                                       s["neg_max"].now(b, 4 * (h - 1) + (k + 1 if k < 2 else 4)))
                        if h and h % 4 == 0 and k == 2:
                            pe.wait_ge(s["max_t"].sem, s["max_t"].now(b, h // 4))
                        pe.matmul(bank[bk][:, lo:lo + n], qm[0:96, h % 8, i * P:(i + 1) * P],
                                  k4[0:96, gr, 0:n], start=True, stop=False)
                        last = pe.matmul(bank[bk][:, lo + i * P:lo + (i + 1) * P],
                                         g["ident_bf"][:, :], g["causal_q"][:, :],
                                         start=False, stop=True)
                        last.then_inc(s["max_ps"].sem, 1)

                def transpose_max(gr):
                    pe.wait_ge(s["neg_max"].sem, s["neg_max"].now(b, 16 * gr + 16))
                    for i in range(NB):
                        last = pe.transpose(bank[5][0:112, i * P:(i + 1) * P], neg_max[:, i, :],
                                            g["ident"][:, :])
                    last.then_inc(s["maxT"].sem, 1)

                def scores(h):
                    gr = h // 4
                    pe.wait_ge(s["qm_max"].sem, s["qm_max"].now(b, h + 1))
                    for c, blocks in enumerate([(0,), (1,), (3, 2)]):
                        if h:
                            pe.wait_ge(s["probs"].sem, s["probs"].now(b, 3 * (h - 1) + c + 1))
                        else:
                            pe.wait_ge(s["hid"].sem, s["hid"].before(b, NH))
                        for kb in blocks:
                            lo, n = (0, T - kb * P) if kb < 2 else (256 * (3 - kb), 256)
                            if kb == 3:
                                lo = 0
                            pe.matmul(bank[c][:, lo:lo + n], k4[:, gr, kb * P:(kb + 1) * P],
                                      qm[:, h % 8, T - n:T], start=True, stop=False)
                            if power_law:
                                first = 0 if kb == 3 else P
                                pe.matmul(bank[c][:, lo:lo + n], g["ident_r"][:, :],
                                          g["decay_hi"][:, first:first + n],
                                          start=False, stop=False)
                                last = pe.matmul(bank[c][:, lo:lo + n], g["ident_r"][:, :],
                                                 g["decay_lo"][:, first:first + n],
                                                 start=False, stop=True)
                            else:
                                at = lo + (P if kb == 3 else 0)
                                last = pe.matmul(bank[c][:, at:at + P], g["ident_bf"][:, :],
                                                 g["causal_k"][:, :], start=False, stop=True)
                        last.then_inc(s["s_ps"].sem, 1)

                def times_values(h):
                    gr, par = h // 4, h // 4 % 2
                    if h % 4 == 0:
                        pe.wait_ge(s["vs"].sem, s["vs"].now(b, 2 * gr + 2))
                        if gr == 0:
                            pe.wait_ge(s["qk_lo"].sem, s["qk_lo"].now(b, 8))
                        elif gr == 1:
                            pe.wait_ge(s["route"].sem, s["route"].now(b, 1))
                        else:
                            pe.wait_ge(s["o_t"].sem, s["o_t"].now(b, gr - 1))
                    for k, (kb, q0, at) in enumerate(PV_AT):
                        n = T - q0
                        pe.wait_ge(s["p_lo"].sem, s["p_lo"].now(b, 2 * h + 1 + k // 2))
                        pe.matmul(bank[6 + par][:, q0:T], vs[:, par, kb, h % 4, :],
                                  p_hi[:, h % 2, at:at + n], start=h % 4 == 0 and k == 0,
                                  stop=False)
                        last = pe.matmul(bank[6 + par][:, q0:T], vs[:, par, kb, h % 4, :],
                                         p_lo[:, h % 2, at:at + n], start=False,
                                         stop=h % 4 == 3 and k == 3)
                    last.then_inc(s["pv"].sem, 1)

                for n in range(3, 8):
                    queries_keys(b, n)
                    if n == 3:
                        per_block(wv[:, :], D, "v_ps")
                pe.wait_ge(s["v_f"].sem, s["v_f"].now(b, 1))
                per_block(wr[:, :], E8, "lg_ps")
                for h in range(4):
                    max_scores(h)
                transpose_max(0)
                max_scores(4)
                for h in range(H):
                    scores(h)
                    if h + AHEAD_MAX < H:
                        max_scores(h + AHEAD_MAX)
                    if h:
                        times_values(h - 1)
                    if h % 4 == 2 and h + 4 < H:
                        transpose_max(h // 4 + 1)
                times_values(H - 1)

                def up(n):
                    if n >= 3:
                        pe.wait_ge(s["hid"].sem, s["hid"].now(b, n - 2))
                    else:
                        pe.wait_ge(s["probs"].sem, s["probs"].now(b, 48))
                    c = slice(n * P, (n + 1) * P)
                    product3(pe, bank[n % 3][:, :], wup_hi[:, c], wup_lo[:, c], m)\
                        .then_inc(s["up"].sem, 1)

                AHEAD = 3
                for n in range(AHEAD):
                    up(n)
                pe.wait_ge(s["o_t"].sem, s["o_t"].now(b, 4))
                pe.matmul(bank[6][:, :], wo[:, 0, :], o_t[:, 0, :], start=True, stop=False)
                pe.matmul(bank[6][:, :], wo[:, 1, :], o_t[:, 1, :], start=False, stop=True)\
                    .then_inc(s["s_ps_out"].sem, 1)
                pe.wait_ge(s["route"].sem, s["route"].now(b, 16))
                for i in range(NB):
                    last = pe.transpose(bank[7][0:E8, i * P:(i + 1) * P], c_tok[:, i, :],
                                        g["ident"][:, :])
                last.then_inc(s["cT_ps"].sem, 1)

                def down(n):
                    e, f = n // FC, n % FC
                    pe.wait_ge(s["hid"].sem, s["hid"].now(b, n + 1))
                    if n == 0:
                        pe.wait_ge(w_down, 16)
                    if f == 0 and e >= 2:
                        pe.wait_ge(s["y_mul"].sem, s["y_mul"].now(b, e - 1))
                    elif n == 0:
                        pe.wait_ge(s["neg_max"].sem, s["neg_max"].now(b, 64))
                    pe.matmul(bank[3 + e % 2][:, :], wdn[:, e, f, :], hid[:, n % 3, :],
                              start=(f == 0), stop=(f == FC - 1)).then_inc(s["dn"].sem, 1)

                def spread(e):
                    if e:
                        pe.wait_ge(s["c_all"].sem, s["c_all"].now(b, e))
                    else:
                        pe.wait_ge(s["c_lo"].sem, s["c_lo"].now(b, 1))
                        pe.wait_ge(s["max_t"].sem, s["max_t"].now(b, 4))
                    pe.matmul(bank[5][:, :], select[:, e, :], c_t[:, :], start=True, stop=True)\
                        .then_inc(s["c_ps"].sem, 1)

                for n in range(NH):
                    if n >= AHEAD:
                        up(n)
                    if n % FC == 2:
                        spread(n // FC)
                    if n >= 2:
                        down(n - 2)
                    if n == 20:
                        prep_tensor(pe, s, m, b + 1, bank[7])
                down(NH - 2)
                down(NH - 1)
                first_queries_keys(b + 1)
                pe.wait_ge(s["upd"].sem, s["upd"].now(b, 1))
                for i in range(NB):
                    last = pe.transpose(bank[6][:, i * P:(i + 1) * P], upd[:, i * P:(i + 1) * P],
                                        g["ident"][:, :])
                last.then_inc(s["updT"].sem, 1)




E16 = 16
ROUTE_SCALE = 2.826
HW = HD + 1
UW = HD * HW
LIN = dict(qkv_ps=NB, e_qk=NB, v_one=NB, e_min=NB, phi=NB, u=NB, u_sum=2, s_ps=NB, w=NB, num=NB,
           den=NB, den_inv=NB, o=NB, oT_ps=1, oT=1, s_ps_out=1, s_t=1, gate=1, upd=1, updT=1,
           x_new=1)


def linear_tiles(m, sb):
    m["e_qk"] = sb("e_qk", [P, 2, 2 * D], F32)
    m["phi"] = sb("phi", [P, 2, 2 * D], F32)
    m["v_one"] = sb("v_one", [P, 2, H, HW], F32)
    m["u"] = sb("u", [P, NB, H * UW], F32)
    m["u_sum"] = sb("u_sum", [P, 2, H * UW], F32)
    m["w"] = sb("w", [P, H * UW], F32)
    m["num"] = sb("num", [P, H, HW], F32)
    m["den"] = sb("den", [P, H], F32)
    m["den_inv"] = sb("den_inv", [P, H], F32)
    m["o"] = sb("o", [P, NB, D], F32)
    m["oT"] = sb("oT", [P, T], F32)
    m["s_t"] = sb("s_t", [P, T], F32)
    m["gate"] = sb("gate", [P, T], F32)
    m["upd"] = sb("upd", [P, T], F32)
    m["wqkv"] = sb("wqkv", [P, 3 * D], F32)
    m["wo"] = sb("wo", [P, D], F32)


def linear_scalar(act, s, m, b, i, bank):
    act.wait_ge(s["qkv_ps"].sem, s["qkv_ps"].now(b, i + 1))
    for name in ("phi", "u"):
        if i >= 2:
            act.wait_ge(s[name].sem, s[name].now(b, i - 1))
        else:
            act.wait_ge(s[name].sem, s[name].before(b, NB - 1 + i))
    qkv = bank[4 + i % 2]
    act.activation(m["e_qk"][:, i % 2, :], qkv[:, 0:2 * D], ACT.Exp).then_inc(s["e_qk"].sem, 1)
    act.activation(m["v_one"][:, i % 2, :, 0:HD],
                   qkv[:, 2 * D:3 * D].rearrange("p (h e) -> p h e", h=H), ACT.Copy)\
        .then_inc(s["v_one"].sem, 1)


def linear_gpsimd(pool, s, m, b, i):
    pool.wait_ge(s["e_qk"].sem, s["e_qk"].now(b, i + 1))
    pool.sem_inc(m["passed"], 1)
    e = m["e_qk"][:, i % 2, :]
    pool.tensor_scalar(e, e, 1.0, 0.0, ALU.min, ALU.max).then_inc(s["e_min"].sem, 1)
    if i in (1, 2):
        pool.wait_ge(s["u"].sem, s["u"].now(b, i + 1))
        first = m["u"][:, 0, :] if i == 1 else m["u_sum"][:, 0, :]
        if i == 1:
            pool.wait_ge(s["s_ps"].sem, s["s_ps"].before(b, NB))
        else:
            pool.wait_ge(s["u_sum"].sem, s["u_sum"].now(b, 1))
        pool.tensor_tensor(m["u_sum"][:, i - 1, :], first, m["u"][:, i, :], ALU.add)\
            .then_inc(s["u_sum"].sem, 1)


def linear_vector_phi(dve, s, m, b, i, bank):
    dve.wait_ge(s["e_min"].sem, s["e_min"].now(b, i + 1))
    dve.wait_ge(s["v_one"].sem, s["v_one"].now(b, i + 1))
    phi = m["phi"][:, i % 2, :]
    if i >= 2:
        dve.wait_ge(s["w"].sem, s["w"].now(b, i - 1))
    else:
        dve.wait_ge(s["w"].sem, s["w"].before(b, NB - 1 + i))
    dve.scalar_tensor_tensor(out=phi, in0=bank[4 + i % 2][:, 0:2 * D], scalar=0.0,
                             in1=m["e_qk"][:, i % 2, :], op0=ALU.max, op1=ALU.add)\
        .then_inc(s["phi"].sem, 1)
    dve.wait_ge(s["phi"].sem, s["phi"].now(b, i + 1))
    if i == 0:
        dve.wait_ge(s["s_ps"].sem, s["s_ps"].before(b, NB))
    phi_k = phi[:, D:2 * D].rearrange("p (h d) -> p h d", h=H)
    shape = [P, H, HD, HW]
    dve.tensor_tensor(m["u"][:, i, :].rearrange("p (h d e) -> p h d e", h=H, d=HD),
                      phi_k.unsqueeze(3).to_broadcast(shape),
                      m["v_one"][:, i % 2, :, :].unsqueeze(2).to_broadcast(shape), ALU.mult)\
        .then_inc(s["u"].sem, 1)


def linear_vector_out(dve, s, m, b, i, psum, eps):
    dve.wait_ge(s["s_ps"].sem, s["s_ps"].now(b, i + 1))
    if i:
        dve.wait_ge(s["num"].sem, s["num"].now(b, i))
    else:
        dve.wait_ge(s["num"].sem, s["num"].before(b, NB))
    shape = [P, 4, 32, HW]
    phi_q = m["phi"][:, i % 2, 0:D].rearrange("p (k x) -> p k x", k=4)
    dve.tensor_tensor(m["w"][:, :].rearrange("p (k x e) -> p k x e", k=4, x=32),
                      psum[:, 0:4, 0:4 * UW].rearrange("p k (x e) -> p k x e", x=32),
                      phi_q.unsqueeze(3).to_broadcast(shape), ALU.mult).then_inc(s["w"].sem, 1)
    dve.wait_ge(s["w"].sem, s["w"].now(b, i + 1))
    dve.tensor_reduce(m["num"][:, :, :],
                      m["w"][:, :].rearrange("p (h d e) -> p h e d", h=H, d=HD), AX.X, ALU.add)\
        .then_inc(s["num"].sem, 1)
    dve.wait_ge(s["num"].sem, s["num"].now(b, i + 1))
    dve.tensor_scalar(m["den"][:, :], m["num"][:, :, HD], eps, None, ALU.add)\
        .then_inc(s["den"].sem, 1)
    dve.wait_ge(s["den"].sem, s["den"].now(b, i + 1))
    dve.reciprocal(m["den_inv"][:, :], m["den"][:, :]).then_inc(s["den_inv"].sem, 1)
    dve.wait_ge(s["den_inv"].sem, s["den_inv"].now(b, i + 1))
    if i == 0:
        dve.wait_ge(s["oT_ps"].sem, s["oT_ps"].before(b, 1))
    dve.tensor_tensor(m["o"][:, i, :].rearrange("p (h e) -> p h e", h=H), m["num"][:, :, 0:HD],
                      m["den_inv"][:, :].unsqueeze(2).to_broadcast([P, H, HD]), ALU.mult)\
        .then_inc(s["o"].sem, 1)


def linear_tensor_qkv(pe, s, m, b, i, bank):
    if i >= 2:
        pe.wait_ge(s["phi"].sem, s["phi"].now(b, i - 1))
    pe.matmul(bank[4 + i % 2][:, 0:3 * D], m["xnT"][:, i * P:(i + 1) * P], m["wqkv"][:, :],
              start=True, stop=True).then_inc(s["qkv_ps"].sem, 1)


def linear_tensor_sums(pe, s, m, b, i, bank):
    pe.wait_ge(s["u"].sem, s["u"].now(b, i + 1))
    if i >= 2:
        pe.wait_ge(s["u_sum"].sem, s["u_sum"].now(b, i - 1))
    if i:
        pe.wait_ge(s["w"].sem, s["w"].now(b, i))
    for k in range(4):
        c = slice(4 * UW * k, 4 * UW * (k + 1))
        last = pe.matmul(bank[k][:, 0:4 * UW], m["tri"][:, :], m["u"][:, i, c],
                         start=True, stop=i == 0)
        if i:
            older = m["u"][:, 0, c] if i == 1 else m["u_sum"][:, i - 2, c]
            last = pe.matmul(bank[k][:, 0:4 * UW], m["ones"][:, :], older, start=False, stop=True)
    last.then_inc(s["s_ps"].sem, 1)


def linear_layer(nc, layer, g, d):
    moe = layer == 0
    with ExitStack() as ctx:
        sems = Semaphores(nc, ctx)

        def sb(name, shape, dt):
            return ctx.enter_context(nc.sbuf_tensor(f"{name}_{layer}", shape, dt))

        m = dict(g)
        prep_tiles(m, sb)
        linear_tiles(m, sb)
        bank, psum = g["bank"], g["psum"]
        names = dict(PREP, **LIN)
        small = [(m["wqkv"], d["wqkv"]), (m["wo"], d["wo"])]
        if moe:
            NE = E16 + 1
            wup_hi = sb("wup_hi", [P, NE, 2, P], F32R)
            wup_lo = sb("wup_lo", [P, NE, 2, P], F32R)
            wdn = sb("wdn", [P, NE, D], F32)
            stage = sb("stage", [P, 2, 512], F32)
            select_raw = sb("select_raw", [64, E16 * P], F32)
            select = sb("select", [64, E16, P], F32R)
            wr = sb("wr", [P, E16], F32)
            rbias = sb("rbias", [P, E16], F32)
            small += [(wr, d["wr"]), (rbias, d["rbias"]), (select_raw, d["select"])]
            lg_exp = sb("lg_exp", [P, NB, E16], F32)
            lg_one = sb("lg_one", [P, NB, E16], F32)
            score = sb("score", [P, NB, E16], F32)
            biased = sb("biased", [P, NB, E16], F32)
            top = sb("top", [P, NB, 8], F32)
            rest = sb("rest", [P, NB, E16], F32)
            chosen = sb("chosen", [P, NB, E16], F32)
            c_raw = sb("c_raw", [P, NB, E16], F32)
            c_sum = sb("c_sum", [P, NB], F32)
            c_inv = sb("c_inv", [P, NB], F32)
            c_scaled = sb("c_scaled", [P, NB], F32)
            c_tok = sb("c_tok", [P, NB, E16], F32)
            c_t = sb("c_t", [64, T], F32R)
            silu = sb("silu", [P, 2, T], F32)
            c_all = sb("c_all", [P, 2, T], F32)
            hid_raw = sb("hid_raw", [P, 2, T], F32)
            hid = sb("hid", [P, 2, T], F32)
            names.update(lg_ps=1, lg_exp=1, route=16, cT_ps=1, c_hi=1, c_lo=1, up=NE, silu=NE,
                         c_ps=E16, c_all=E16, c_scaled=1, hid_raw=NE, hid=E16, dn=NE)
            flat_hi = wup_hi[:, :, :, :].rearrange("p e a c -> p (e a c)")
            flat_lo = wup_lo[:, :, :, :].rearrange("p e a c -> p (e a c)")
            PIECE = 256
            N_PIECES = NE
        else:
            bo = sb("bo", [P, D], F32)
            lnw = sb("lnw", [P, 4], F32)
            lnb = sb("lnb", [P, 4], F32)
            wfc_raw = sb("wfc_raw", [P, 4 * P], F32)
            wproj_raw = sb("wproj_raw", [P, 4 * P], F32)
            small += [(bo, d["bo"]), (lnw, d["lnw"]), (lnb, d["lnb"]), (wfc_raw, d["wfc"]),
                      (wproj_raw, d["wproj"])]
            abs_sum = sb("abs_sum", [P, 2], F32)
            half_gamma = sb("half_gamma", [P, 2], F32)
            minus_half_gamma = sb("minus_half_gamma", [P, 2], F32)
            above = sb("above", [P, 2, 4 * P], F32)
            below = sb("below", [P, 2, 4 * P], F32)
            wfc = sb("wfc", [P, 4, P], F32R)
            wproj = sb("wproj", [P, 4, P], F32)
            lnb_all = sb("lnb_all", [P, 4, P], F32)
            wproj_scaled = sb("wproj_scaled", [P, 4, D], F32)
            ffn_bias = sb("ffn_bias", [P, D], F32)
            mean_w = sb("mean_w", [P, P], F32)
            hid = sb("hid", [P, 4, T], F32)
            cen = sb("cen", [P, 4, T], F32)
            sq = sb("sq", [P, 4, T], F32)
            var_eps_t = sb("var_eps_t", [P, NB], F32)
            rstd_t = sb("rstd_t", [P, NB], F32)
            z = sb("z", [P, NB, D], F32)
            names.update(up=4, hid=4, mean_ps=1, cen=4, sq=4, var_ps=1, var_eps_t=1, rstd_t=1,
                         dn=1, z=4)
            names.pop("updT")
            ternary = sems.new("ternary")
            gamma_ps = sems.new("gamma_ps")
        s = signals(sems, layer, **names)
        setup = sems.new(f"setup_{layer}")
        m["passed"] = sems.new(f"passed_{layer}")
        w_small = sems.new(f"w_small_{layer}")
        w_stage = [sems.new(f"w_stage{i}_{layer}") for i in range(2)]
        w_split = sems.new(f"w_split_{layer}")
        w_down = sems.new(f"w_down_{layer}")
        N_SMALL = 16 * len(small)
        block = ctx.enter_context(nc.Block())

        @block.sync
        def _(sync):
            for x in s.values():
                sync.sem_inc(x.sem, x.per)
            for tile, src in small:
                sync.dma_start(tile[:], src).then_inc(w_small, 16)
            if moe:
                for n in range(N_PIECES):
                    if n >= 2:
                        sync.wait_ge(w_split, 2 * (n - 1))
                    sync.dma_start(stage[:, n % 2, 0:PIECE], d["wup"][:, n * PIECE:(n + 1) * PIECE])\
                        .then_inc(w_stage[n % 2], 16)
                    if n == 0:
                        sync.dma_start(wdn[:], d["wdn"]).then_inc(w_down, 16)

        @block.gpsimd
        def _(pool):
            fills = [(m["v_one"][:, :, :, :], 1.0)]
            if moe:
                fills += [(c_t[:, :].bitcast(F32), 0.0)]
            else:
                fills += [(mean_w[:, :], 1.0 / (4 * P))]
            for n, (tile, value) in enumerate(fills):
                if n:
                    pool.wait_ge(setup, n)
                pool.memset(tile, value).then_inc(setup, 1)
            pool.wait_ge(setup, len(fills))
            prep_gpsimd(pool, s, m, 0)
            if moe:
                for n in range(N_PIECES):
                    c = slice(n * PIECE, (n + 1) * PIECE)
                    pool.wait_ge(w_stage[n % 2], 16 * (n // 2 + 1))
                    split_gpsimd(pool, w_split, flat_hi[:, c], flat_lo[:, c],
                                 stage[:, n % 2, 0:PIECE], n)
            with pool.Fori(0, B) as b:
                for i in range(NB):
                    linear_gpsimd(pool, s, m, b, i)
                prep_gpsimd(pool, s, m, b + 1)
                if not moe:
                    pool.wait_ge(s["var_eps_t"].sem, s["var_eps_t"].now(b, 1))
                    pool.wait_ge(s["z"].sem, s["z"].before(b, 4))
                    pool.tensor_tensor(rstd_t[:, :], var_eps_t[:, :], m["minus_half"][:, :],
                                       ALU.pow).then_inc(s["rstd_t"].sem, 1)
                pool.wait_ge(s["gate"].sem, s["gate"].now(b, 1))
                pool.wait_ge(s["s_t"].sem, s["s_t"].now(b, 1))
                last_use = s["updT" if moe else "x_new"]
                pool.wait_ge(last_use.sem, last_use.before(b, 1))
                pool.tensor_tensor(m["upd"][:, :], m["gate"][:, :], m["s_t"][:, :], ALU.mult)\
                    .then_inc(s["upd"].sem, 1)

        @block.scalar
        def _(act):
            act.preload_act_table_set(EXP_LN)
            prep_scalar(act, s, m, 0, bank[7])
            act.wait_ge(w_small, N_SMALL)
            act.wait_ge(setup, 2)
            with act.Fori(0, B) as b:
                act.preload_act_table_set(EXP_LN)
                linear_scalar(act, s, m, b, 0, bank)
                linear_scalar(act, s, m, b, 1, bank)
                if moe:
                    act.wait_ge(s["lg_ps"].sem, s["lg_ps"].now(b, 1))
                    act.activation(lg_exp[:, :, :], bank[6][:, 0:NB * E16]
                                   .rearrange("p (i e) -> p i e", i=NB), ACT.Exp, scale=-1.0)\
                        .then_inc(s["lg_exp"].sem, 1)
                linear_scalar(act, s, m, b, 2, bank)
                linear_scalar(act, s, m, b, 3, bank)
                act.wait_ge(s["oT_ps"].sem, s["oT_ps"].now(b, 1))
                act.activation(m["oT"][:, :], bank[6][:, :], ACT.Copy).then_inc(s["oT"].sem, 1)
                if moe:
                    act.wait_ge(s["s_ps_out"].sem, s["s_ps_out"].now(b, 1))
                    act.wait_ge(s["upd"].sem, s["upd"].before(b, 1))
                    act.activation(m["s_t"][:, :], bank[5][:, :], ACT.Copy)\
                        .then_inc(s["s_t"].sem, 1)
                    act.wait_ge(s["cT_ps"].sem, s["cT_ps"].now(b, 1))
                    act.wait_ge(s["c_ps"].sem, s["c_ps"].before(b, E16))
                    act.activation(c_t[0:E16, :], bank[7][0:E16, :], ACT.Copy)\
                        .then_inc(s["c_hi"].sem, 1)
                    for e in range(NE):
                        act.wait_ge(s["up"].sem, s["up"].now(b, e + 1))
                        if e >= 2:
                            act.wait_ge(s["hid_raw"].sem, s["hid_raw"].now(b, e - 1))
                        else:
                            act.wait_ge(s["hid_raw"].sem, s["hid_raw"].before(b, NE - 1 + e))
                        act.activation(silu[:, e % 2, :], bank[2 * (e % 2)][:, :], ACT.Silu)\
                            .then_inc(s["silu"].sem, 1)
                        if e < E16:
                            act.wait_ge(s["c_ps"].sem, s["c_ps"].now(b, e + 1))
                            if e >= 2:
                                act.wait_ge(s["hid"].sem, s["hid"].now(b, e - 1))
                            else:
                                act.wait_ge(s["hid"].sem, s["hid"].before(b, E16 - 1 + e))
                            act.activation(c_all[:, e % 2, :], bank[5][:, :], ACT.Copy)\
                                .then_inc(s["c_all"].sem, 1)
                else:
                    for c in range(4):
                        act.wait_ge(s["up"].sem, s["up"].now(b, c + 1))
                        if c == 0:
                            act.wait_ge(s["cen"].sem, s["cen"].before(b, 4))
                        act.activation(hid[:, c, :], bank[c][:, :], ACT.Gelu)\
                            .then_inc(s["hid"].sem, 1)
                    for c in range(4):
                        act.wait_ge(s["cen"].sem, s["cen"].now(b, c + 1))
                        if c == 0:
                            act.wait_ge(s["var_ps"].sem, s["var_ps"].before(b, 1))
                        act.activation(sq[:, c, :], cen[:, c, :], ACT.Square)\
                            .then_inc(s["sq"].sem, 1)
                prep_scalar(act, s, m, b + 1, bank[7])
                act.wait_ge(s["upd"].sem, s["upd"].before(b, 1))
                if moe:
                    act.wait_ge(s["dn"].sem, s["dn"].now(b, NE))
                    act.activation(m["gate"][:, :], bank[4][:, :], ACT.Silu)\
                        .then_inc(s["gate"].sem, 1)
                else:
                    act.wait_ge(s["z"].sem, s["z"].now(b, 4))
                    act.activation(m["gate"][:, :], z[:, :, :].rearrange("p i d -> p (i d)"),
                                   ACT.Silu).then_inc(s["gate"].sem, 1)

        def router(dve, b):
            def route(n):
                dve.wait_ge(s["route"].sem, s["route"].now(b, n))

            def done(ins):
                ins.then_inc(s["route"].sem, 1)

            dve.wait_ge(s["lg_exp"].sem, s["lg_exp"].now(b, 1))
            done(dve.tensor_scalar(lg_one[:, :, :], lg_exp[:, :, :], 1.0, None, ALU.add))
            route(1)
            done(dve.reciprocal(score[:, :, :], lg_one[:, :, :]))
            route(2)
            done(dve.tensor_tensor(biased[:, :, :], score[:, :, :],
                                   rbias[:, :].unsqueeze(1).to_broadcast([P, NB, E16]), ALU.add))
            route(3)
            dve.sem_inc(m["passed"], 1)
            for i in range(NB):
                done(dve.max(top[:, i, :], biased[:, i, :]))
            route(7)
            dve.sem_inc(m["passed"], 1)
            for i in range(NB):
                done(dve.match_replace(rest[:, i, :], top[:, i, :], biased[:, i, :], 3e38))
            route(11)
            done(dve.tensor_tensor(chosen[:, :, :], rest[:, :, :], biased[:, :, :], ALU.not_equal))
            route(12)
            done(dve.tensor_tensor(c_raw[:, :, :], score[:, :, :], chosen[:, :, :], ALU.mult))
            route(13)
            done(dve.tensor_reduce(c_sum[:, :], c_raw[:, :, :], AX.X, ALU.add))
            route(14)
            done(dve.reciprocal(c_inv[:, :], c_sum[:, :]))
            route(15)
            dve.tensor_scalar(c_scaled[:, :], c_inv[:, :], ROUTE_SCALE, None, ALU.mult)\
                .then_inc(s["c_scaled"].sem, 1)
            dve.wait_ge(s["c_scaled"].sem, s["c_scaled"].now(b, 1))
            dve.wait_ge(s["cT_ps"].sem, s["cT_ps"].before(b, 1))
            done(dve.tensor_tensor(c_tok[:, :, :], c_raw[:, :, :],
                                   c_scaled[:, :].unsqueeze(2).to_broadcast([P, NB, E16]),
                                   ALU.mult))

        def experts(dve, b):
            dve.wait_ge(s["c_hi"].sem, s["c_hi"].now(b, 1))
            dve.tensor_tensor(c_t[32:32 + E16, :], bank[7][0:E16, :],
                              c_t[0:E16, :].bitcast(F32), ALU.subtract).then_inc(s["c_lo"].sem, 1)
            for e in range(NE):
                dve.wait_ge(s["silu"].sem, s["silu"].now(b, e + 1))
                shared = e == E16
                if shared:
                    dve.wait_ge(s["dn"].sem, s["dn"].now(b, e - 1))
                elif e == 0:
                    dve.wait_ge(s["hid"].sem, s["hid"].before(b, E16))
                elif e >= 2:
                    dve.wait_ge(s["hid"].sem, s["hid"].now(b, e - 1))
                dve.tensor_tensor((hid if shared else hid_raw)[:, e % 2, :],
                                  bank[2 * (e % 2) + 1][:, :], silu[:, e % 2, :], ALU.mult)\
                    .then_inc(s["hid_raw"].sem, 1)
                if not shared:
                    dve.wait_ge(s["hid_raw"].sem, s["hid_raw"].now(b, e + 1))
                    dve.wait_ge(s["c_all"].sem, s["c_all"].now(b, e + 1))
                    if e >= 2:
                        dve.wait_ge(s["dn"].sem, s["dn"].now(b, e - 1))
                    elif e == 0:
                        dve.wait_ge(s["dn"].sem, s["dn"].before(b, NE))
                    dve.tensor_tensor(hid[:, e % 2, :], hid_raw[:, e % 2, :], c_all[:, e % 2, :],
                                      ALU.mult).then_inc(s["hid"].sem, 1)
                if e == 8:
                    prep_vector(dve, s, m, b + 1)

        def ternary_weights(dve):
            for n, w in enumerate((wfc_raw, wproj_raw)):
                dve.tensor_reduce(abs_sum[:, n:n + 1], w[:, :], AX.X, ALU.add,
                                  apply_absolute_value=True).then_inc(ternary, 1)
            dve.wait_ge(gamma_ps, 1)
            size = float(4 * P * D)
            dve.tensor_scalar(half_gamma[:, :], bank[0][:, 0:2], 0.5 / size, 0.5e-6, ALU.mult,
                              ALU.add).then_inc(ternary, 1)
            dve.wait_ge(ternary, 3)
            dve.tensor_scalar(minus_half_gamma[:, :], half_gamma[:, :], -1.0, None, ALU.mult)\
                .then_inc(ternary, 1)
            dve.wait_ge(ternary, 4)
            for n, w in enumerate((wfc_raw, wproj_raw)):
                dve.tensor_scalar(above[:, n, :], w[:, :], half_gamma[:, n:n + 1], None,
                                  ALU.is_gt).then_inc(ternary, 1)
                dve.tensor_scalar(below[:, n, :], w[:, :], minus_half_gamma[:, n:n + 1], None,
                                  ALU.is_lt).then_inc(ternary, 1)
            dve.wait_ge(ternary, 8)
            for n, w in enumerate((wfc, wproj)):
                dve.tensor_tensor(w[:, :, :].rearrange("p c f -> p (c f)"), above[:, n, :],
                                  below[:, n, :], ALU.subtract).then_inc(ternary, 1)
            dve.tensor_copy(lnb_all[:, :, :], lnb[:, :].unsqueeze(2).to_broadcast([P, 4, P]))\
                .then_inc(ternary, 1)
            dve.wait_ge(ternary, 10)
            for c in range(4):
                dve.tensor_scalar(wproj_scaled[:, c, :], wproj[:, c, :], lnw[:, c:c + 1], None,
                                  ALU.mult).then_inc(ternary, 1)
            dve.wait_ge(gamma_ps, 2)
            dve.tensor_copy(ffn_bias[:, :], bank[1][:, 0:D]).then_inc(ternary, 1)

        def normed(dve, b):
            dve.wait_ge(s["s_ps_out"].sem, s["s_ps_out"].now(b, 1))
            dve.wait_ge(s["upd"].sem, s["upd"].before(b, 1))
            dve.tensor_tensor(m["s_t"][:, :].rearrange("p (i d) -> p i d", i=NB),
                              bank[5][:, :].rearrange("p (i d) -> p i d", i=NB),
                              bo[:, :].unsqueeze(1).to_broadcast([P, NB, D]), ALU.add)\
                .then_inc(s["s_t"].sem, 1)
            dve.wait_ge(s["mean_ps"].sem, s["mean_ps"].now(b, 1))
            dve.wait_ge(s["dn"].sem, s["dn"].before(b, 1))
            dve.wait_ge(s["sq"].sem, s["sq"].before(b, 4))
            for c in range(4):
                dve.tensor_tensor(cen[:, c, :], hid[:, c, :], bank[4][:, :], ALU.subtract)\
                    .then_inc(s["cen"].sem, 1)
            prep_vector(dve, s, m, b + 1)
            dve.wait_ge(s["var_ps"].sem, s["var_ps"].now(b, 1))
            dve.wait_ge(s["rstd_t"].sem, s["rstd_t"].before(b, 1))
            dve.tensor_scalar(var_eps_t[:, :], bank[6][:, 0:NB], LN_EPS, None, ALU.add)\
                .then_inc(s["var_eps_t"].sem, 1)
            dve.wait_ge(s["dn"].sem, s["dn"].now(b, 1))
            dve.wait_ge(s["rstd_t"].sem, s["rstd_t"].now(b, 1))
            dve.wait_ge(s["gate"].sem, s["gate"].before(b, 1))
            for i in range(NB):
                dve.scalar_tensor_tensor(out=z[:, i, :], in0=bank[4][:, i * P:(i + 1) * P],
                                         scalar=rstd_t[:, i:i + 1], in1=ffn_bias[:, :],
                                         op0=ALU.mult, op1=ALU.add).then_inc(s["z"].sem, 1)

        @block.vector
        def _(dve):
            prep_vector(dve, s, m, 0)
            prep_vector_lo(dve, s, m, 0, bank[7])
            dve.wait_ge(w_small, N_SMALL)
            dve.wait_ge(setup, 2)
            if moe:
                dve.tensor_copy(select[:, :, :].rearrange("k e p -> k (e p)"), select_raw[:, :])
            else:
                ternary_weights(dve)
            with dve.Fori(0, B) as b:
                linear_vector_phi(dve, s, m, b, 0, bank)
                linear_vector_phi(dve, s, m, b, 1, bank)
                if moe:
                    router(dve, b)
                for i in range(NB):
                    linear_vector_out(dve, s, m, b, i, psum, 1e-6 if moe else 1e-5)
                    if i + 2 < NB:
                        linear_vector_phi(dve, s, m, b, i + 2, bank)
                if moe:
                    experts(dve, b)
                else:
                    normed(dve, b)
                prep_vector_lo(dve, s, m, b + 1, bank[7])
                update = s["updT" if moe else "upd"]
                dve.wait_ge(update.sem, update.now(b, 1))
                xb = g["x"][:, bass.ds(b * NB, NB), :]
                dve.tensor_tensor(xb, xb, (bank[6] if moe else m["upd"])[:, :]
                                  .rearrange("p (i d) -> p i d", i=NB), ALU.add)\
                    .then_inc(s["x_new"].sem, 1)

        @block.tensor
        def _(pe):
            prep_tensor(pe, s, m, 0, bank[7])
            pe.wait_ge(w_small, N_SMALL)
            pe.wait_ge(setup, 2)
            if not moe:
                pe.wait_ge(ternary, 2)
                pe.matmul(bank[0][:, 0:2], g["ones"][:, :], abs_sum[:, :], start=True, stop=True)\
                    .then_inc(gamma_ps, 1)
                pe.wait_ge(ternary, 11)
                for c in range(4):
                    last = pe.matmul(bank[1][:, 0:D], lnb_all[:, c, :], wproj[:, c, :],
                                     start=c == 0, stop=c == 3)
                last.then_inc(gamma_ps, 1)
                pe.wait_ge(ternary, 16)
            with pe.Fori(0, B) as b:
                pe.wait_ge(s["xnT"].sem, s["xnT"].now(b, 1))
                if moe:
                    pe.wait_ge(s["gate"].sem, s["gate"].before(b, 1))
                    pe.wait_ge(s["c_all"].sem, s["c_all"].before(b, E16))
                else:
                    pe.wait_ge(s["z"].sem, s["z"].before(b, 4))
                    pe.wait_ge(s["s_t"].sem, s["s_t"].before(b, 1))
                linear_tensor_qkv(pe, s, m, b, 0, bank)
                linear_tensor_qkv(pe, s, m, b, 1, bank)
                if moe:
                    pe.wait_ge(s["x_new"].sem, s["x_new"].before(b, 1))
                    for i in range(NB):
                        last = pe.matmul(bank[6][:, i * E16:(i + 1) * E16],
                                         m["xnT"][:, i * P:(i + 1) * P], wr[:, :],
                                         start=True, stop=True)
                    last.then_inc(s["lg_ps"].sem, 1)
                for i in range(NB):
                    if i == 0:
                        free = ("hid_raw", NE) if moe else ("hid", 4)
                        pe.wait_ge(s[free[0]].sem, s[free[0]].before(b, free[1]))
                    linear_tensor_sums(pe, s, m, b, i, bank)
                    if i + 2 < NB:
                        linear_tensor_qkv(pe, s, m, b, i + 2, bank)
                if moe:
                    pe.wait_ge(s["lg_exp"].sem, s["lg_exp"].now(b, 1))
                else:
                    pe.wait_ge(s["var_eps_t"].sem, s["var_eps_t"].before(b, 1))
                for i in range(NB):
                    pe.wait_ge(s["o"].sem, s["o"].now(b, i + 1))
                    last = pe.transpose(bank[6][:, i * P:(i + 1) * P], m["o"][:, i, :],
                                        g["ident"][:, :])
                last.then_inc(s["oT_ps"].sem, 1)
                pe.wait_ge(s["oT"].sem, s["oT"].now(b, 1))
                pe.wait_ge(s["phi"].sem, s["phi"].now(b, NB))
                if moe:
                    pe.matmul(bank[5][:, :], m["wo"][:, :], m["oT"][:, :], start=True, stop=True)\
                        .then_inc(s["s_ps_out"].sem, 1)
                else:
                    for i in range(NB):
                        c = slice(i * P, (i + 1) * P)
                        last = pe.matmul(bank[5][:, c], m["oT"][:, c], m["wo"][:, :], start=True,
                                         stop=True)
                    last.then_inc(s["s_ps_out"].sem, 1)
                pe.wait_ge(s["xnT_lo"].sem, s["xnT_lo"].now(b, 1))
                if moe:
                    pe.wait_ge(s["route"].sem, s["route"].now(b, 16))
                    for i in range(NB):
                        last = pe.transpose(bank[7][0:E16, i * P:(i + 1) * P], c_tok[:, i, :],
                                            g["ident"][:, :])
                    last.then_inc(s["cT_ps"].sem, 1)
                    pe.wait_ge(s["w"].sem, s["w"].now(b, NB))
                    for e in range(NE + 1):
                        if e < NE:
                            if e >= 2:
                                pe.wait_ge(s["hid_raw"].sem, s["hid_raw"].now(b, e - 1))
                            pe.wait_ge(w_split, 2 * (e + 1))
                            product3(pe, bank[2 * (e % 2)][:, :], wup_hi[:, e, 0, :],
                                     wup_lo[:, e, 0, :], m)
                            product3(pe, bank[2 * (e % 2) + 1][:, :], wup_hi[:, e, 1, :],
                                     wup_lo[:, e, 1, :], m).then_inc(s["up"].sem, 1)
                        if e < E16:
                            if e:
                                pe.wait_ge(s["c_all"].sem, s["c_all"].now(b, e))
                            else:
                                pe.wait_ge(s["c_lo"].sem, s["c_lo"].now(b, 1))
                                pe.wait_ge(s["s_t"].sem, s["s_t"].now(b, 1))
                            pe.matmul(bank[5][:, :], select[:, e, :], c_t[:, :], start=True,
                                      stop=True).then_inc(s["c_ps"].sem, 1)
                        if e:
                            j = e - 1
                            if j < E16:
                                pe.wait_ge(s["hid"].sem, s["hid"].now(b, j + 1))
                            else:
                                pe.wait_ge(s["hid_raw"].sem, s["hid_raw"].now(b, NE))
                            if j == 0:
                                pe.wait_ge(w_down, 16)
                            pe.matmul(bank[4][:, :], wdn[:, j, :], hid[:, j % 2, :],
                                      start=(j == 0), stop=(j == NE - 1))\
                                .then_inc(s["dn"].sem, 1)
                        if e == 13:
                            prep_tensor(pe, s, m, b + 1, bank[7])
                else:
                    pe.wait_ge(s["w"].sem, s["w"].now(b, NB))
                    for c in range(4):
                        pe.matmul(bank[c][:, :], wfc[:, c, :], m["xnT_hi"][:, :], start=True,
                                  stop=False)
                        pe.matmul(bank[c][:, :], wfc[:, c, :], m["xnT_lo"][:, :], start=False,
                                  stop=True).then_inc(s["up"].sem, 1)
                    for c in range(4):
                        pe.wait_ge(s["hid"].sem, s["hid"].now(b, c + 1))
                        last = pe.matmul(bank[4][:, :], mean_w[:, :], hid[:, c, :],
                                         start=c == 0, stop=c == 3)
                    last.then_inc(s["mean_ps"].sem, 1)
                    pe.wait_ge(s["cen"].sem, s["cen"].now(b, 4))
                    for i in range(NB):
                        for c in range(4):
                            last = pe.matmul(bank[4][:, i * P:(i + 1) * P],
                                             cen[:, c, i * P:(i + 1) * P], wproj_scaled[:, c, :],
                                             start=c == 0, stop=c == 3)
                    last.then_inc(s["dn"].sem, 1)
                    pe.wait_ge(s["sq"].sem, s["sq"].now(b, 4))
                    for i in range(NB):
                        for c in range(4):
                            last = pe.matmul(bank[6][:, i:i + 1], sq[:, c, i * P:(i + 1) * P],
                                             mean_w[:, 0:1], start=c == 0, stop=c == 3)
                    last.then_inc(s["var_ps"].sem, 1)
                    prep_tensor(pe, s, m, b + 1, bank[7])
                if moe:
                    pe.wait_ge(s["upd"].sem, s["upd"].now(b, 1))
                    for i in range(NB):
                        last = pe.transpose(bank[6][:, i * P:(i + 1) * P],
                                            m["upd"][:, i * P:(i + 1) * P], g["ident"][:, :])
                    last.then_inc(s["updT"].sem, 1)




def decay_table():
    k, q = np.arange(P)[:, None], np.arange(T)[None, :]
    delta = (q - k).astype(np.float64)
    t = np.where(delta > 0, -0.25 * np.log(np.maximum(delta, 1.0)) * np.sqrt(HD), 0.0)
    t = np.where(delta < 0, NEG, t)
    return np.concatenate([np.zeros((P, P)), t], 1).astype(np.float32)


def constants():
    p = np.arange(P)
    head = np.zeros((P, H), np.float32)
    for h in range(H):
        head[:96, h] = (p[:96] % 32) // HD == h % 4
        head[96 + h, h] = 1
    select = np.zeros((64, 16, P), np.float32)
    for e in range(16):
        select[e, e] = select[32 + e, e] = 1
    return {
        "c_ident": np.eye(P, dtype=np.float32),
        "c_causal_q": np.where(p[None, :] > p[:, None], NEG, 0).astype(np.float32),
        "c_causal_k": np.where(p[:, None] > p[None, :], NEG, 0).astype(np.float32),
        "c_head_mask": head,
        "l0_select": select.reshape(64, -1),
        "l1_select": select[:, :E8].reshape(64, -1),
        "l3_select": select[:, :E8].reshape(64, -1),
        "c_decay": decay_table(),
        "c_tri": (p[:, None] <= p[None, :]).astype(np.float32),
    }


def load_constants(nc, ctx, dram):
    def sb(name, shape, dt):
        return ctx.enter_context(nc.sbuf_tensor(name, shape, dt))

    psum = ctx.enter_context(nc.psum_tensor("psum", [P, 8, 512], F32))
    g = {"psum": psum, "bank": [psum[:, i, :] for i in range(8)]}
    g["x"] = sb("x_res", [P, (B + 1) * NB, D], F32)
    g["ident"] = sb("ident", [P, P], F32)
    g["ident_r"] = sb("ident_r", [P, P], F32R)
    g["ident_bf"] = sb("ident_bf", [P, P], BF16)
    g["causal_q"] = sb("causal_q", [P, P], BF16)
    g["causal_k"] = sb("causal_k", [P, P], BF16)
    g["head_mask"] = sb("head_mask", [P, H], F32)
    g["tri"] = sb("tri", [P, P], F32)
    g["ones"] = sb("ones", [P, P], F32)
    g["minus_half"] = sb("minus_half", [P, NB], F32)
    if 3 in LAYERS:
        g["decay_hi"] = sb("decay_hi", [P, P + T], F32R)
        g["decay_lo"] = sb("decay_lo", [P, P + T], F32R)
    with ExitStack() as tmp:
        raw = tmp.enter_context(nc.sbuf_tensor("raw_mask", [P, 2, P], F32))
        raw_dec = tmp.enter_context(nc.sbuf_tensor("raw_decay", [P, P + T], F32))
        consts = nc.alloc_semaphore(name="consts")
        x_in = nc.alloc_semaphore(name="x_in")
        narrowed = nc.alloc_semaphore(name="narrowed")
        block = tmp.enter_context(nc.Block())
        loads = [(g["ident"][:, :], dram["c_ident"]), (raw[:, 0, :], dram["c_causal_q"]),
                 (raw[:, 1, :], dram["c_causal_k"]), (g["head_mask"][:, :], dram["c_head_mask"]),
                 (raw_dec[:, :], dram["c_decay"]), (g["tri"][:, :], dram["c_tri"])]

        @block.sync
        def _(sync):
            for tile, src in loads:
                sync.dma_start(tile, src).then_inc(consts, 16)
            sync.wait_ge(consts, 16 * len(loads))
            sync.wait_ge(x_in, 16 * B)

        @block.scalar
        def _(act):
            x_blocks = dram["L0_attn_x"].rearrange("(t p) d -> p t d", p=P)
            for b in range(B):
                act.dma_start(g["x"][:, b * NB:(b + 1) * NB, :],
                              x_blocks[:, b * NB:(b + 1) * NB, :]).then_inc(x_in, 16)

        @block.gpsimd
        def _(pool):
            pool.memset(g["ones"][:, :], 1.0)
            pool.memset(g["minus_half"][:, :], -0.5)
            pool.memset(g["x"][:, B * NB:(B + 1) * NB, :], 0.0)

        @block.vector
        def _(dve):
            dve.wait_ge(consts, 16 * len(loads))
            dve.tensor_copy(g["ident_bf"][:, :], g["ident"][:, :])
            dve.tensor_copy(g["ident_r"][:, :], g["ident"][:, :])
            dve.tensor_copy(g["causal_q"][:, :], raw[:, 0, :])
            dve.tensor_copy(g["causal_k"][:, :], raw[:, 1, :])
            if 3 in LAYERS:
                dve.tensor_copy(g["decay_hi"][:, :], raw_dec[:, :]).then_inc(narrowed, 1)
                dve.wait_ge(narrowed, 1)
                dve.tensor_tensor(g["decay_lo"][:, :], raw_dec[:, :],
                                  g["decay_hi"][:, :].bitcast(F32), ALU.subtract)
    return g


def store_x(nc, g, out):
    with ExitStack() as ctx:
        stored = nc.alloc_semaphore(name="stored")
        block = ctx.enter_context(nc.Block())

        @block.sync
        def _(sync):
            blocks = out.rearrange("(t p) d -> p t d", p=P)
            for b in range(B):
                sync.dma_start(blocks[:, b * NB:(b + 1) * NB, :],
                               g["x"][:, b * NB:(b + 1) * NB, :]).then_inc(stored, 16)
            sync.wait_ge(stored, 16 * B)


LAYERS = (0, 1, 2, 3)


def build(nc, dram, out):
    with ExitStack() as ctx:
        g = load_constants(nc, ctx, dram)
        for layer in LAYERS:
            ops = {k.split("_", 1)[1]: v for k, v in dram.items() if k.startswith(f"l{layer}_")}
            (softmax_layer if layer % 2 else linear_layer)(nc, layer, g, ops)
        store_x(nc, g, out)


def lay_out(a):
    c = np.ascontiguousarray
    r = {"L0_attn_x": a["L0_attn_x"].reshape(B * T, D)}

    def four(w):
        return np.tile(w.reshape(D, 4, 1, 32), (1, 1, 4, 1)).reshape(D, 4, P)

    def out_rows(w):
        return np.tile(w.reshape(2, 8, 1, HD, D), (1, 1, 2, 1, 1)).reshape(2, P, D)\
            .transpose(1, 0, 2)

    def rows(v):
        return c(np.broadcast_to(v[None, :], (P, v.shape[0])))

    r["l0_wqkv"] = c(a["L0_attn_w_attn"].T)
    r["l0_wo"] = c(a["L0_attn_w_proj"].T)
    r["l0_wr"] = c(a["L0_ffn_gate_w"].T)
    r["l0_rbias"] = rows(a["L0_ffn_expert_bias"])
    gate = np.concatenate([a["L0_ffn_w_gate"], a["L0_ffn_shared_gate_w"][None]])
    up = np.concatenate([a["L0_ffn_w_up"], a["L0_ffn_shared_up_w"][None]])
    down = np.concatenate([a["L0_ffn_w_down"], a["L0_ffn_shared_down_w"][None]])
    r["l0_wup"] = c(np.stack([gate, up], 1).transpose(3, 0, 1, 2).reshape(D, -1))
    r["l0_wdn"] = c(down.transpose(2, 0, 1))
    qkv, bias = a["L1_attn_qkv_w"], a["L1_attn_qkv_b"]
    r["l1_wqk"] = c(np.stack([four(qkv[:, :D]), four(qkv[:, D:2 * D])], 1).reshape(D, -1))
    r["l1_bqk"] = c(np.stack([four(np.broadcast_to(v, (D, D)))[0].T
                              for v in (bias[:D], bias[D:2 * D])], 1))
    r["l1_wv"] = c(qkv[:, 2 * D:])
    r["l1_bv"] = rows(bias[2 * D:])
    r["l1_wo"], r["l1_bo"] = out_rows(a["L1_attn_out_w"]), c(a["L1_attn_out_b"][:, None])
    r["l1_wr"] = c(a["L1_ffn_Wg"].T)
    r["l1_wup"] = c(a["L1_ffn_W1"].transpose(1, 0, 2).reshape(D, -1))
    r["l1_wdn"] = c(a["L1_ffn_W2"].reshape(E8, FC, P, D).transpose(2, 0, 1, 3))
    r["l2_wqkv"] = c(np.concatenate([a[f"L2_attn_W{n}"].T for n in "qkv"], 1))
    r["l2_wo"], r["l2_bo"] = c(a["L2_attn_Wo"].T), rows(a["L2_attn_bo"])
    r["l2_wfc"] = c(a["L2_ffn_W_fc"].T)
    r["l2_wproj"] = c(a["L2_ffn_W_proj"].reshape(D, 4, P).transpose(2, 1, 0).reshape(P, -1))
    r["l2_lnw"] = c(a["L2_ffn_ln_w"].reshape(4, P).T)
    r["l2_lnb"] = c(a["L2_ffn_ln_b"].reshape(4, P).T)
    r["l3_wqk"] = c(np.stack([four(a["L3_attn_Wq"]), four(a["L3_attn_Wk"])], 1).reshape(D, -1))
    r["l3_bqk"] = c(np.stack([four(np.broadcast_to(v, (D, D)))[0].T
                              for v in (a["L3_attn_bq"], a["L3_attn_bk"])], 1))
    r["l3_wv"], r["l3_bv"] = a["L3_attn_Wv"], rows(a["L3_attn_bv"])
    r["l3_wo"], r["l3_bo"] = out_rows(a["L3_attn_Wo"]), c(a["L3_attn_bo"][:, None])
    r["l3_wr"] = c(a["L3_ffn_router_w"].T)
    r["l3_wup"] = c(a["L3_ffn_w1"].transpose(2, 0, 1).reshape(D, -1))
    r["l3_b1"] = c(a["L3_ffn_b1"].reshape(E8, FC, P).transpose(2, 0, 1))
    r["l3_wdn"] = c(a["L3_ffn_w2"].transpose(2, 0, 1).reshape(FC, P, E8, D).transpose(1, 2, 0, 3))
    r["l3_b2"] = c(a["L3_ffn_b2"].T)
    return {k: c(v) for k, v in {**r, **constants()}.items()}


def kernel(**inputs):
    import concourse.bacc as bacc
    from concourse.bass_utils import run_bass_kernel_spmd

    arrays = lay_out({k: np.asarray(v) for k, v in inputs.items()})
    nc = bacc.Bacc("TRN2", target_bir_lowering=False, num_devices=1)
    dram = {k: nc.dram_tensor(k, v.shape, mybir.dt.from_np(v.dtype), kind="ExternalInput").ap()
            for k, v in arrays.items()}
    out = nc.dram_tensor("x_out", (B * T, D), F32, kind="ExternalOutput").ap()
    build(nc, dram, out)
    r = run_bass_kernel_spmd(nc, [arrays], core_ids=[0])
    return r.results[0]["x_out"].reshape(B, T, D)
```

```python
from contextlib import ExitStack

import numpy as np

import concourse.bass as bass
from concourse import mybir

F32 = mybir.dt.float32
F32R = mybir.dt.float32r
BF16 = mybir.dt.bfloat16
ALU = mybir.AluOpType
ACT = mybir.ActivationFunctionType
AX = mybir.AxisListType

P = 128
D = 128
B, T = 8, 512
NB = T // P
H, HD = 16, 8
LN_EPS = 1e-5
EXP_LN = "natural_log_exp_and_others"
NEG = -1e30




class Semaphores:

    def __init__(self, nc, ctx):
        self.nc, self.made = nc, []
        ctx.callback(self.clear)

    def new(self, name):
        self.made.append(self.nc.alloc_semaphore(name=name))
        return self.made[-1]

    def clear(self):
        self.nc.clear_and_free_semaphores(self.made)
        self.nc.all_engine_barrier()


class Signal:

    def __init__(self, sems, name, per):
        self.sem, self.per = sems.new(name), per

    def now(self, b, n):
        return (b + 1) * self.per + n

    def before(self, b, n):
        return b * self.per + n


def signals(sems, layer, **per):
    return {k: Signal(sems, f"{k}_{layer}", n) for k, n in per.items()}


def block_of(x_res, b, i):
    return x_res[:, bass.ds(b * NB + i, 1), :].rearrange("p a d -> p (a d)")




def prep_vector_stats(dve, s, m, k):
    for i in range(NB):
        dve.bn_stats(m["stats"][:, i, :], block_of(m["x"], k, i)).then_inc(s["stats"].sem, 1)
    for i in range(NB):
        dve.wait_ge(s["stats"].sem, s["stats"].now(k, i + 1))
        dve.sem_inc(m["passed"], 1)
        dve.bn_aggr(m["mean_var"][:, i, :], m["stats"][:, i, :]).then_inc(s["mean_var"].sem, 1)


def prep_vector_xn(dve, s, m, k):
    dve.wait_ge(s["rstd"].sem, s["rstd"].now(k, 1))
    dve.wait_ge(s["xnT_ps"].sem, s["xnT_ps"].before(k, 1))
    for i in range(NB):
        dve.tensor_scalar(m["xn"][:, i, :], block_of(m["x"], k, i), m["mean_var"][:, i, 0:1],
                          m["rstd"][:, i:i + 1], ALU.subtract, ALU.mult).then_inc(s["xn"].sem, 1)


def prep_gpsimd(pool, s, m, k):
    pool.wait_ge(s["mean_var"].sem, s["mean_var"].now(k, NB))
    pool.sem_inc(m["passed"], 1)
    pool.tensor_scalar(m["var_eps"][:, :], m["mean_var"][:, :, 1], LN_EPS, 1.0, ALU.add,
                       ALU.mult).then_inc(s["var_eps"].sem, 1)
    pool.wait_ge(s["var_eps"].sem, s["var_eps"].now(k, 1))
    pool.tensor_tensor(m["rstd"][:, :], m["var_eps"][:, :], m["minus_half"][:, :],
                       ALU.pow).then_inc(s["rstd"].sem, 1)


def prep_tensor(pe, s, m, k, bank):
    pe.wait_ge(s["xn"].sem, s["xn"].now(k, NB))
    for i in range(NB):
        last = pe.transpose(bank[:, i * P:(i + 1) * P], m["xn"][:, i, :], m["ident"][:, :])
    last.then_inc(s["xnT_ps"].sem, 1)


def prep_scalar(act, s, m, k, bank, tile):
    act.wait_ge(s["xnT_ps"].sem, s["xnT_ps"].now(k, 1))
    act.activation(m[tile][:, :], bank[:, :], ACT.Copy).then_inc(s[tile].sem, 1)


def prep_vector_lo(dve, s, m, k):
    dve.wait_ge(s["xnT_hi"].sem, s["xnT_hi"].now(k, 1))
    dve.tensor_tensor(m["xnT_lo"][:, :], m["xnT"][:, :], m["xnT_hi"][:, :].bitcast(F32),
                      ALU.subtract).then_inc(s["xnT_lo"].sem, 1)


PREP = dict(stats=NB, mean_var=NB, var_eps=1, rstd=1, xn=NB, xnT_ps=1, xnT=1, xnT_hi=1, xnT_lo=1)


def prep_tiles(m, sb):
    m["stats"] = sb("stats", [P, NB, 6], F32)
    m["mean_var"] = sb("mean_var", [P, NB, 2], F32)
    m["var_eps"] = sb("var_eps", [P, NB], F32)
    m["rstd"] = sb("rstd", [P, NB], F32)
    m["xn"] = sb("xn", [P, NB, D], F32)
    m["xnT"] = sb("xnT", [P, T], F32)
    m["xnT_hi"] = sb("xnT_hi", [P, T], F32R)
    m["xnT_lo"] = sb("xnT_lo", [P, T], F32R)


def product3(pe, out, w_hi, w_lo, m):
    pe.matmul(out, w_hi, m["xnT_hi"][:, :], start=True, stop=False)
    pe.matmul(out, w_lo, m["xnT_hi"][:, :], start=False, stop=False)
    return pe.matmul(out, w_hi, m["xnT_lo"][:, :], start=False, stop=True)




def split_gpsimd(pool, done, hi, lo, stage, n0):
    pool.tensor_scalar(hi, stage, 1.0, 1.0, ALU.mult, ALU.mult).then_inc(done, 1)
    pool.wait_ge(done, 2 * n0 + 1)
    pool.tensor_tensor(lo, stage, hi.bitcast(F32), ALU.subtract).then_inc(done, 1)





E8, FC = 8, 4
CHUNKS = [(0, 512, 0), (0, 384, 512), (128, 384, 1024)]
PW = 1408
PV_AT = [(0, 0, 0), (1, 128, 512), (3, 256, 896), (2, 256, 1152)]
HALVES = [(0, 896), (896, PW)]
AHEAD_MAX = 5
MAX_AT = [(5, 256, 128), (5, 0, 256), (4, 0, 384), (3, 0, 512)]


def softmax_layer(nc, layer, g, d):
    power_law = layer == 3
    with ExitStack() as ctx:
        sems = Semaphores(nc, ctx)

        def sb(name, shape, dt):
            return ctx.enter_context(nc.sbuf_tensor(f"{name}_{layer}", shape, dt))

        m = dict(g)
        prep_tiles(m, sb)
        NPIECE = E8 * FC * P // 512
        wup_hi = sb("wup_hi", [P, E8 * FC * P], F32R)
        wup_lo = sb("wup_lo", [P, E8 * FC * P], F32R)
        wdn = sb("wdn", [P, E8, FC, D], F32)
        wqk_hi = sb("wqk_hi", [P, 2, 4, P], F32R)
        wqk_lo = sb("wqk_lo", [P, 2, 4, P], F32R)
        wv = sb("wv", [P, D], F32)
        wo = sb("wo", [P, 2, D], F32)
        wr = sb("wr", [P, E8], F32)
        bqk = sb("bqk", [P, 2, 4], F32)
        bv = sb("bv", [P, D], F32)
        bo = sb("bo", [P, 1], F32)
        b1 = sb("b1", [P, E8, FC], F32)
        b2 = sb("b2", [P, E8], F32)
        q4 = sb("q4", [P, 4, T], F32R)
        k4 = sb("k4", [P, 4, T], F32R)
        qm = sb("qm", [P, 8, T], F32R)
        v_f = sb("v_f", [P, NB, D], F32)
        vs = sb("vs", [P, 2, NB, 4, P], F32R)
        probs = sb("probs", [P, 2, PW], F32)
        p_hi = sb("p_hi", [P, 2, PW], F32R)
        p_lo = sb("p_lo", [P, 2, PW], F32R)
        neg_max = sb("neg_max", [P, NB, 112], F32)
        den_inv = sb("den_inv", [P, T], F32)
        o_t = sb("o_t", [P, 2, T], F32)
        s_t = sb("s_t", [P, T], F32)
        lg = sb("lg", [P, NB, 16], F32)
        top = sb("top", [P, NB, 8], F32)
        two = sb("two", [P, NB, 8], F32)
        rest = sb("rest", [P, NB, 16], F32)
        chosen = sb("chosen", [P, NB, E8], F32)
        lg_rel = sb("lg_rel", [P, NB, E8], F32)
        lg_exp = sb("lg_exp", [P, NB, E8], F32)
        c_raw = sb("c_raw", [P, NB, E8], F32)
        c_sum = sb("c_sum", [P, NB], F32)
        c_inv = sb("c_inv", [P, NB], F32)
        c_tok = sb("c_tok", [P, NB, E8], F32)
        c_t = sb("c_t", [64, T], F32R)
        hid = sb("hid", [P, 3, T], F32)
        c_all = sb("c_all", [P, T], F32)
        y_one = sb("y_one", [P, T], F32)
        acc = sb("acc", [P, T], F32)
        gate = y_one
        upd = den_inv
        select = sb("select", [64, E8, P], F32R)

        NH = len(range(E8 * FC))
        s = signals(sems, layer, **PREP, qk_ps=8, qk_hi=8, qk_lo=8, qm=16, v_ps=1,
                    v_f=1, vs=8, max_ps=64, neg_max=64, maxT=4, max_t=4, qm_max=16, s_ps=48,
                    probs=48, p_hi=32, p_lo=32, pv=16, den_ln=4, den_inv=4, o_t=4, s_ps_out=1,
                    s_t=1,
                    lg_ps=1, route=16, lg_exp=1, cT_ps=1, c_hi=1, c_lo=1, c_ps=E8, c_all=E8,
                    up=NH, hid=NH, dn=NH, y_mul=E8, y=E8 - 1, gate=1, upd=1, updT=1, x_new=1)
        setup = sems.new(f"setup_{layer}")
        m["passed"] = sems.new(f"passed_{layer}")
        w_small = sems.new(f"w_small_{layer}")
        stage = [acc, y_one, c_all, s_t]
        w_stage = [sems.new(f"w_stage{i}_{layer}") for i in range(len(stage))]
        w_hi = sems.new(f"w_hi_{layer}")
        w_lo = sems.new(f"w_lo_{layer}")
        w_down = sems.new(f"w_down_{layer}")
        block = ctx.enter_context(nc.Block())
        bank = g["bank"]
        QK_SPLITS = 4
        small = [(wv, d["wv"]), (wo, d["wo"]), (wr, d["wr"]), (bqk, d["bqk"]), (bv, d["bv"]),
                 (bo, d["bo"])]
        if power_law:
            small += [(b1, d["b1"]), (b2, d["b2"])]
        N_SMALL = 16 * len(small)
        N_SPLIT = QK_SPLITS + NPIECE
        N_PIECES = N_SPLIT + E8 * P // 512

        def piece(n):
            if n < QK_SPLITS:
                c = slice(n * 2 * P, (n + 1) * 2 * P)
                flat = [w[:, :, :, :].rearrange("p a g c -> p (a g c)") for w in (wqk_hi, wqk_lo)]
                return flat[0][:, c], flat[1][:, c], d["wqk"][:, c]
            if n < N_SPLIT:
                c = slice((n - QK_SPLITS) * 512, (n - QK_SPLITS + 1) * 512)
                return wup_hi[:, c], wup_lo[:, c], d["wup"][:, c]
            c = slice((n - N_SPLIT) * 512, (n - N_SPLIT + 1) * 512)
            return select[:, :, :].rearrange("k e p -> k (e p)")[:, c], None, d["select"][:, c]

        def staged(n):
            src = piece(n)[2]
            return stage[n % len(stage)][0:src.shape[0], 0:src.shape[1]]

        @block.sync
        def _(sync):
            for x in s.values():
                sync.sem_inc(x.sem, x.per)
            for tile, src in small:
                sync.dma_start(tile[:], src).then_inc(w_small, 16)
            for n in range(N_PIECES):
                if n >= len(stage):
                    sync.wait_ge(w_lo, n - len(stage) + 1)
                sync.dma_start(staged(n), piece(n)[2]).then_inc(w_stage[n % len(stage)], 16)
            sync.dma_start(wdn[:], d["wdn"]).then_inc(w_down, 16)

        SETUP = 8 + 8

        @block.gpsimd
        def _(pool):
            prep_gpsimd(pool, s, m, 0)
            fills = [(k4[96:P, :, :].bitcast(F32), 1.0), (qm[96:P, :, :].bitcast(F32), 0.0),
                     (neg_max[:, :, :], 0.0), (c_t[:, :].bitcast(F32), 0.0), (lg[:, :, :], -3e38),
                     (two[:, :, :], -3e38), (probs[:, :, 896:1024], 0.0),
                     (vs[:, :, :, :, :].bitcast(F32), 0.0)]
            for par in range(2):
                for j in range(4):
                    c = 64 * (1 - par) + 16 * j
                    fills.append((vs[:, par, :, j, c:c + 16].bitcast(F32), 1.0))
            pool.wait_ge(s["rstd"].sem, s["rstd"].now(0, 1))
            for n, (tile, value) in enumerate(fills):
                if n:
                    pool.wait_ge(setup, n)
                pool.memset(tile, value).then_inc(setup, 1)

            with pool.Fori(0, B) as b:
                def masked(h):
                    gr = h // 4
                    pool.wait_ge(s["qk_lo"].sem, s["qk_lo"].now(b, 2 * gr + 1))
                    if h < 8:
                        pool.wait_ge(s["s_ps"].sem, s["s_ps"].before(b, 3 * (h + 8) + 3))
                    else:
                        pool.wait_ge(s["s_ps"].sem, s["s_ps"].now(b, 3 * (h - 8) + 3))
                    pool.sem_inc(m["passed"], 1)
                    pool.tensor_scalar(qm[0:96, h % 8, :], q4[0:96, gr, :].bitcast(F32),
                                       g["head_mask"][0:96, h:h + 1], 1.0, ALU.mult,
                                       ALU.mult).then_inc(s["qm"].sem, 1)

                def masked_max(h):
                    gr = h // 4
                    pool.wait_ge(s["max_t"].sem, s["max_t"].now(b, gr + 1))
                    pool.wait_ge(s["qm"].sem, s["qm"].now(b, (8, 11, 15, 16)[gr]))
                    if h:
                        pool.wait_ge(s["qm_max"].sem, s["qm_max"].now(b, h))
                    pool.sem_inc(m["passed"], 1)
                    pool.tensor_scalar(qm[96:112, h % 8, :], q4[96:112, gr, :].bitcast(F32),
                                       g["head_mask"][96:112, h:h + 1], 1.0, ALU.mult,
                                       ALU.mult).then_inc(s["qm_max"].sem, 1)

                for h in range(8):
                    masked(h)
                for gr in range(4):
                    for h in range(4 * gr, 4 * gr + 4):
                        masked_max(h)
                    for h in range(4 * gr + 7, 4 * gr + 11):
                        if 8 <= h < H:
                            pool.wait_ge(s["qm_max"].sem, s["qm_max"].now(b, 4 * gr + 4))
                            masked(h)
                pool.wait_ge(s["qm_max"].sem, s["qm_max"].now(b, 16))
                prep_gpsimd(pool, s, m, b + 1)
                pool.wait_ge(s["gate"].sem, s["gate"].now(b, 1))
                pool.wait_ge(s["updT"].sem, s["updT"].before(b, 1))
                pool.tensor_tensor(upd[:, :], gate[:, :], s_t[:, :], ALU.mult)\
                    .then_inc(s["upd"].sem, 1)

        @block.scalar
        def _(act):
            act.preload_act_table_set(EXP_LN)
            prep_scalar(act, s, m, 0, bank[7], "xnT")
            prep_scalar(act, s, m, 0, bank[7], "xnT_hi")
            for n in range(N_PIECES):
                act.wait_ge(w_stage[n % len(stage)], 16 * (n // len(stage) + 1))
                act.activation(piece(n)[0], staged(n), ACT.Copy).then_inc(w_hi, 1)
            act.wait_ge(w_small, N_SMALL)
            act.wait_ge(w_lo, N_SPLIT)
            act.wait_ge(setup, SETUP)
            with act.Fori(0, B) as b:
                act.preload_act_table_set(EXP_LN)
                for n in range(8):
                    a, gr = n % 2, n // 2
                    act.wait_ge(s["qk_ps"].sem, s["qk_ps"].now(b, n + 1))
                    if n == 0:
                        act.wait_ge(s["qm"].sem, s["qm"].before(b, 16))
                        act.wait_ge(s["s_ps"].sem, s["s_ps"].before(b, 48))
                    out = (k4 if a else q4)[0:96, gr, :]
                    act.activation(out, bank[3 + n % 4][0:96, :], ACT.Identity,
                                   bias=bqk[0:96, a, gr:gr + 1]).then_inc(s["qk_hi"].sem, 1)

                def router_exp():
                    act.wait_ge(s["route"].sem, s["route"].now(b, 12))
                    act.activation(lg_exp[:, :, :], lg_rel[:, :, :], ACT.Exp)\
                        .then_inc(s["lg_exp"].sem, 1)

                def max_to_sbuf(gr):
                    act.wait_ge(s["maxT"].sem, s["maxT"].now(b, gr + 1))
                    act.activation(q4[96:112, gr, :], bank[5][96:112, :], ACT.Copy)\
                        .then_inc(s["max_t"].sem, 1)

                def exps(h):
                    for c, (lo, n, at) in enumerate(CHUNKS):
                        act.wait_ge(s["s_ps"].sem, s["s_ps"].now(b, 3 * h + c + 1))
                        if c == 0:
                            if h >= 2:
                                act.wait_ge(s["p_lo"].sem, s["p_lo"].now(b, 2 * h - 2))
                            else:
                                act.wait_ge(s["p_lo"].sem, s["p_lo"].before(b, 30 + 2 * h))
                        act.activation(probs[:, h % 2, at:at + n], bank[c][:, lo:lo + n], ACT.Exp,
                                       scale=float(HD) ** -0.5).then_inc(s["probs"].sem, 1)
                    for k, (lo, end) in enumerate(HALVES):
                        act.wait_ge(s["probs"].sem, s["probs"].now(b, 3 * h + 2 + k))
                        if k == 0:
                            if h >= 2:
                                act.wait_ge(s["pv"].sem, s["pv"].now(b, h - 1))
                            else:
                                act.wait_ge(s["pv"].sem, s["pv"].before(b, 15 + h))
                        act.activation(p_hi[:, h % 2, lo:end], probs[:, h % 2, lo:end], ACT.Copy)\
                            .then_inc(s["p_hi"].sem, 1)

                def denominator(gr):
                    rows = slice(64, 128) if gr % 2 == 0 else slice(0, 64)
                    act.wait_ge(s["pv"].sem, s["pv"].now(b, 4 * gr + 4))
                    if gr >= 2:
                        act.wait_ge(s["o_t"].sem, s["o_t"].now(b, gr - 1))
                    else:
                        act.wait_ge(s["o_t"].sem, s["o_t"].before(b, gr + 3))
                    act.activation(den_inv[rows, :], bank[6 + gr % 2][rows, :], ACT.Ln)\
                        .then_inc(s["den_ln"].sem, 1)
                    act.wait_ge(s["den_ln"].sem, s["den_ln"].now(b, gr + 1))
                    act.activation(den_inv[rows, :], den_inv[rows, :], ACT.Exp, scale=-1.0)\
                        .then_inc(s["den_inv"].sem, 1)

                max_to_sbuf(0)
                for h in range(H):
                    exps(h)
                    if h == 2:
                        router_exp()
                    if h % 4 == 2 and h + 4 < H:
                        max_to_sbuf(h // 4 + 1)
                    if h % 4 == 1 and h > 4:
                        denominator(h // 4 - 1)
                denominator(3)

                def hidden(n):
                    e, f = n // FC, n % FC
                    act.wait_ge(s["up"].sem, s["up"].now(b, n + 1))
                    if n >= 3:
                        act.wait_ge(s["dn"].sem, s["dn"].now(b, n - 2))
                    else:
                        act.wait_ge(s["dn"].sem, s["dn"].before(b, NH - 2 + n))
                    act.activation(hid[:, n % 3, :], bank[n % 3][:, :],
                                   ACT.Gelu if power_law else ACT.Silu,
                                   bias=b1[:, e, f:f + 1] if power_law else 0.0)\
                        .then_inc(s["hid"].sem, 1)

                hidden(0)
                hidden(1)
                act.wait_ge(s["s_ps_out"].sem, s["s_ps_out"].now(b, 1))
                act.wait_ge(s["upd"].sem, s["upd"].before(b, 1))
                act.activation(s_t[:, :], bank[6][:, :], ACT.Identity, bias=bo[:, 0:1])\
                    .then_inc(s["s_t"].sem, 1)
                act.wait_ge(s["cT_ps"].sem, s["cT_ps"].now(b, 1))
                act.wait_ge(s["c_ps"].sem, s["c_ps"].before(b, E8))
                act.activation(c_t[0:E8, :], bank[7][0:E8, :], ACT.Copy).then_inc(s["c_hi"].sem, 1)
                for e in range(E8):
                    for f in range(FC):
                        if e * FC + f == NH - 3:
                            prep_scalar(act, s, m, b + 1, bank[7], "xnT")
                        if e * FC + f == NH - 1:
                            act.wait_ge(s["up"].sem, s["up"].now(b, NH))
                            prep_scalar(act, s, m, b + 1, bank[7], "xnT_hi")
                        if e or f >= 2:
                            hidden(e * FC + f)
                    act.wait_ge(s["c_ps"].sem, s["c_ps"].now(b, e + 1))
                    if e:
                        act.wait_ge(s["y_mul"].sem, s["y_mul"].now(b, e))
                    else:
                        act.wait_ge(s["y_mul"].sem, s["y_mul"].before(b, E8))
                    act.activation(c_all[:, :], bank[5][:, :], ACT.Copy).then_inc(s["c_all"].sem, 1)
                act.wait_ge(s["y"].sem, s["y"].now(b, E8 - 1))
                act.activation(gate[:, :], acc[:, :], ACT.Silu).then_inc(s["gate"].sem, 1)

        @block.vector
        def _(dve):
            prep_vector_stats(dve, s, m, 0)
            prep_vector_xn(dve, s, m, 0)
            prep_vector_lo(dve, s, m, 0)
            dve.wait_ge(w_small, N_SMALL)
            for n in range(N_SPLIT):
                dve.wait_ge(w_hi, n + 1)
                hi, lo, _ = piece(n)
                dve.tensor_tensor(lo, staged(n), hi.bitcast(F32), ALU.subtract).then_inc(w_lo, 1)
            dve.wait_ge(w_hi, N_PIECES)
            dve.wait_ge(setup, SETUP)
            with dve.Fori(0, B) as b:
                def values():
                    dve.wait_ge(s["v_ps"].sem, s["v_ps"].now(b, 1))
                    dve.wait_ge(s["vs"].sem, s["vs"].before(b, 8))
                    dve.tensor_tensor(v_f[:, :, :],
                                      bank[7][:, :].rearrange("p (i e) -> p i e", i=NB),
                                      bv[:, :].unsqueeze(1).to_broadcast([P, NB, D]), ALU.add)\
                        .then_inc(s["v_f"].sem, 1)

                def group_values(gr):
                    dve.wait_ge(s["v_f"].sem, s["v_f"].now(b, 1))
                    if gr >= 2:
                        dve.wait_ge(s["pv"].sem, s["pv"].now(b, 4 * (gr - 1)))
                    else:
                        dve.wait_ge(s["pv"].sem, s["pv"].before(b, 4 * (gr + 3)))
                    par = gr % 2
                    v = v_f[:, :, 32 * gr:32 * gr + 32].rearrange("p i (j e) -> p i j e", j=4)

                    def part(at):
                        t0 = vs[:, par, 0, 0, 64 * par + at:64 * par + at + HD]
                        return bass.AP(tensor=t0.tensor, offset=t0.offset,
                                       ap=[t0.ap[0], [4 * P, NB], [P + 16, 4], [1, HD]])

                    dve.tensor_copy(part(0), v).then_inc(s["vs"].sem, 1)
                    dve.wait_ge(s["vs"].sem, s["vs"].now(b, 2 * gr + 1))
                    dve.tensor_tensor(part(HD), v, part(0).bitcast(F32), ALU.subtract)\
                        .then_inc(s["vs"].sem, 1)

                def route(n):
                    dve.wait_ge(s["route"].sem, s["route"].now(b, n))

                def route_top():
                    dve.wait_ge(s["lg_ps"].sem, s["lg_ps"].now(b, 1))
                    dve.tensor_copy(lg[:, :, 0:E8],
                                    bank[7][:, 0:NB * E8].rearrange("p (i e) -> p i e", i=NB))\
                        .then_inc(s["route"].sem, 1)
                    route(1)
                    dve.sem_inc(m["passed"], 1)
                    for i in range(NB):
                        dve.max(top[:, i, :], lg[:, i, :]).then_inc(s["route"].sem, 1)
                    route(5)
                    dve.tensor_copy(two[:, :, 0:2], top[:, :, 0:2]).then_inc(s["route"].sem, 1)
                    route(6)
                    dve.sem_inc(m["passed"], 1)
                    for i in range(NB):
                        dve.match_replace(rest[:, i, :], two[:, i, :], lg[:, i, :], 3e38)\
                            .then_inc(s["route"].sem, 1)
                    route(10)
                    dve.tensor_tensor(chosen[:, :, :], rest[:, :, 0:E8], lg[:, :, 0:E8],
                                      ALU.not_equal).then_inc(s["route"].sem, 1)
                    dve.tensor_tensor(lg_rel[:, :, :], lg[:, :, 0:E8],
                                      top[:, :, 0:1].to_broadcast([P, NB, E8]), ALU.subtract)\
                        .then_inc(s["route"].sem, 1)

                def route_rest():
                    dve.wait_ge(s["lg_exp"].sem, s["lg_exp"].now(b, 1))
                    dve.tensor_tensor(c_raw[:, :, :], lg_exp[:, :, :], chosen[:, :, :], ALU.mult)\
                        .then_inc(s["route"].sem, 1)
                    route(13)
                    dve.tensor_reduce(c_sum[:, :], c_raw[:, :, :], AX.X, ALU.add)\
                        .then_inc(s["route"].sem, 1)
                    route(14)
                    dve.reciprocal(c_inv[:, :], c_sum[:, :]).then_inc(s["route"].sem, 1)
                    route(15)
                    dve.wait_ge(s["cT_ps"].sem, s["cT_ps"].before(b, 1))
                    dve.tensor_tensor(c_tok[:, :, :], c_raw[:, :, :],
                                      c_inv[:, :].unsqueeze(2).to_broadcast([P, NB, E8]),
                                      ALU.mult).then_inc(s["route"].sem, 1)

                for n in range(8):
                    a, gr = n % 2, n // 2
                    rows = slice(64, 96) if a == 0 else slice(32, 64)
                    tile = (k4 if a else q4)[:, gr, :]
                    dve.wait_ge(s["qk_hi"].sem, s["qk_hi"].now(b, n + 1))
                    dve.scalar_tensor_tensor(out=tile[rows, :], in0=bank[3 + n % 4][rows, :],
                                             scalar=bqk[rows, a, gr:gr + 1],
                                             in1=tile[rows, :].bitcast(F32), op0=ALU.add,
                                             op1=ALU.subtract).then_inc(s["qk_lo"].sem, 1)
                    if n == 3:
                        values()

                def neg_maxima(h):
                    if h % 4 == 0:
                        if h:
                            dve.wait_ge(s["maxT"].sem, s["maxT"].now(b, h // 4))
                        else:
                            dve.wait_ge(s["maxT"].sem, s["maxT"].before(b, 4))
                    for k, i in enumerate(reversed(range(NB))):
                        bk, lo, n = MAX_AT[i]
                        ready = 4 * h + (k + 1 if k < 2 else 4)
                        dve.wait_ge(s["max_ps"].sem, s["max_ps"].now(b, ready))
                        dve.tensor_reduce(neg_max[:, i, 96 + h:97 + h], bank[bk][:, lo:lo + n],
                                          AX.X, ALU.max, negate=True)\
                            .then_inc(s["neg_max"].sem, 1)

                def normalise(gr):
                    num = slice(64, 128) if gr % 2 else slice(0, 64)
                    den = slice(0, 64) if gr % 2 else slice(64, 128)
                    dve.wait_ge(s["den_inv"].sem, s["den_inv"].now(b, gr + 1))
                    if gr == 0:
                        dve.wait_ge(s["s_ps_out"].sem, s["s_ps_out"].before(b, 1))
                    dve.tensor_tensor(o_t[num, gr // 2, :], bank[6 + gr % 2][num, :],
                                      den_inv[den, :], ALU.mult).then_inc(s["o_t"].sem, 1)

                def lower(h):
                    for k, (lo, end) in enumerate(HALVES):
                        dve.wait_ge(s["p_hi"].sem, s["p_hi"].now(b, 2 * h + k + 1))
                        dve.tensor_tensor(p_lo[:, h % 2, lo:end], probs[:, h % 2, lo:end],
                                          p_hi[:, h % 2, lo:end].bitcast(F32), ALU.subtract)\
                            .then_inc(s["p_lo"].sem, 1)

                for h in range(AHEAD_MAX):
                    neg_maxima(h)
                group_values(0)
                group_values(1)
                for h in range(H):
                    if h == 1:
                        route_top()
                    if h == 4:
                        route_rest()
                    if h + AHEAD_MAX < H:
                        neg_maxima(h + AHEAD_MAX)
                    lower(h)
                    if h % 4 == 2 and h > 4:
                        normalise(h // 4 - 1)
                        if h // 4 < 3:
                            group_values(h // 4 + 1)
                normalise(3)
                dve.wait_ge(s["c_hi"].sem, s["c_hi"].now(b, 1))
                dve.tensor_tensor(c_t[32:32 + E8, :], bank[7][0:E8, :],
                                  c_t[0:E8, :].bitcast(F32), ALU.subtract)\
                    .then_inc(s["c_lo"].sem, 1)
                for e in range(E8):
                    if e == E8 - 1:
                        prep_vector_lo(dve, s, m, b + 1)
                    dve.wait_ge(s["dn"].sem, s["dn"].now(b, FC * (e + 1)))
                    dve.wait_ge(s["c_all"].sem, s["c_all"].now(b, e + 1))
                    if e == 0:
                        dve.wait_ge(s["gate"].sem, s["gate"].before(b, 1))
                    elif e > 1:
                        dve.wait_ge(s["y"].sem, s["y"].now(b, e - 1))
                    out = y_one[:, :] if e else acc[:, :]
                    if power_law:
                        dve.scalar_tensor_tensor(out=out, in0=bank[3 + e % 2][:, :],
                                                 scalar=b2[:, e:e + 1], in1=c_all[:, :],
                                                 op0=ALU.add, op1=ALU.mult)\
                            .then_inc(s["y_mul"].sem, 1)
                    else:
                        dve.tensor_tensor(out, bank[3 + e % 2][:, :], c_all[:, :], ALU.mult)\
                            .then_inc(s["y_mul"].sem, 1)
                    if e:
                        dve.wait_ge(s["y_mul"].sem, s["y_mul"].now(b, e + 1))
                        dve.tensor_tensor(acc[:, :], acc[:, :], y_one[:, :], ALU.add)\
                            .then_inc(s["y"].sem, 1)
                    if e == 2:
                        prep_vector_stats(dve, s, m, b + 1)
                    if e == 3:
                        prep_vector_xn(dve, s, m, b + 1)
                dve.wait_ge(s["updT"].sem, s["updT"].now(b, 1))
                xb = g["x"][:, bass.ds(b * NB, NB), :]
                dve.tensor_tensor(xb, xb, bank[6][:, :].rearrange("p (i d) -> p i d", i=NB),
                                  ALU.add).then_inc(s["x_new"].sem, 1)

        @block.tensor
        def _(pe):
            prep_tensor(pe, s, m, 0, bank[7])
            pe.wait_ge(w_small, N_SMALL)
            pe.wait_ge(setup, SETUP)
            pe.wait_ge(w_lo, N_SPLIT)
            pe.wait_ge(w_hi, N_PIECES)

            def queries_keys(k, n):
                a, gr = n % 2, n // 2
                if n >= 4:
                    pe.wait_ge(s["qk_lo"].sem, s["qk_lo"].now(k, n - 3))
                elif n < 2:
                    pe.wait_ge(s["y_mul"].sem, s["y_mul"].before(k, E8 - 1 + n))
                elif n == 2:
                    pe.wait_ge(s["c_all"].sem, s["c_all"].before(k, E8))
                else:
                    pe.wait_ge(s["x_new"].sem, s["x_new"].before(k, 1))
                product3(pe, bank[3 + n % 4][:, :], wqk_hi[:, a, gr, :], wqk_lo[:, a, gr, :],
                         m).then_inc(s["qk_ps"].sem, 1)

            def first_queries_keys(k):
                pe.wait_ge(s["xnT_hi"].sem, s["xnT_hi"].now(k, 1))
                pe.wait_ge(s["xnT_lo"].sem, s["xnT_lo"].now(k, 1))
                for n in range(3):
                    queries_keys(k, n)

            first_queries_keys(0)
            with pe.Fori(0, B) as b:
                pe.wait_ge(s["xnT"].sem, s["xnT"].now(b, 1))

                def per_block(w, n, signal):
                    for i in range(NB):
                        last = pe.matmul(bank[7][:, i * n:(i + 1) * n],
                                         m["xnT"][:, i * P:(i + 1) * P], w, start=True, stop=True)
                    last.then_inc(s[signal].sem, 1)

                def max_scores(h):
                    gr = h // 4
                    pe.wait_ge(s["qm"].sem, s["qm"].now(b, h + 1))
                    for k, i in enumerate(reversed(range(NB))):
                        bk, lo, n = MAX_AT[i]
                        n = max(n, 256)
                        if h == 0 and k < 3:
                            pe.wait_ge(s["qk_lo"].sem, s["qk_lo"].now(b, 5 + k))
                        elif k < 3:
                            pe.wait_ge(s["neg_max"].sem,
                                       s["neg_max"].now(b, 4 * (h - 1) + (k + 1 if k < 2 else 4)))
                        if h and h % 4 == 0 and k == 2:
                            pe.wait_ge(s["max_t"].sem, s["max_t"].now(b, h // 4))
                        pe.matmul(bank[bk][:, lo:lo + n], qm[0:96, h % 8, i * P:(i + 1) * P],
                                  k4[0:96, gr, 0:n], start=True, stop=False)
                        last = pe.matmul(bank[bk][:, lo + i * P:lo + (i + 1) * P],
                                         g["ident_bf"][:, :], g["causal_q"][:, :],
                                         start=False, stop=True)
                        last.then_inc(s["max_ps"].sem, 1)

                def transpose_max(gr):
                    pe.wait_ge(s["neg_max"].sem, s["neg_max"].now(b, 16 * gr + 16))
                    for i in range(NB):
                        last = pe.transpose(bank[5][0:112, i * P:(i + 1) * P], neg_max[:, i, :],
                                            g["ident"][:, :])
                    last.then_inc(s["maxT"].sem, 1)

                def scores(h):
                    gr = h // 4
                    pe.wait_ge(s["qm_max"].sem, s["qm_max"].now(b, h + 1))
                    for c, blocks in enumerate([(0,), (1,), (3, 2)]):
                        if h:
                            pe.wait_ge(s["probs"].sem, s["probs"].now(b, 3 * (h - 1) + c + 1))
                        else:
                            pe.wait_ge(s["hid"].sem, s["hid"].before(b, NH))
                        for kb in blocks:
                            lo, n = (0, T - kb * P) if kb < 2 else (256 * (3 - kb), 256)
                            if kb == 3:
                                lo = 0
                            pe.matmul(bank[c][:, lo:lo + n], k4[:, gr, kb * P:(kb + 1) * P],
                                      qm[:, h % 8, T - n:T], start=True, stop=False)
                            if power_law:
                                first = 0 if kb == 3 else P
                                pe.matmul(bank[c][:, lo:lo + n], g["ident_r"][:, :],
                                          g["decay_hi"][:, first:first + n],
                                          start=False, stop=False)
                                last = pe.matmul(bank[c][:, lo:lo + n], g["ident_r"][:, :],
                                                 g["decay_lo"][:, first:first + n],
                                                 start=False, stop=True)
                            else:
                                at = lo + (P if kb == 3 else 0)
                                last = pe.matmul(bank[c][:, at:at + P], g["ident_bf"][:, :],
                                                 g["causal_k"][:, :], start=False, stop=True)
                        last.then_inc(s["s_ps"].sem, 1)

                def times_values(h):
                    gr, par = h // 4, h // 4 % 2
                    if h % 4 == 0:
                        pe.wait_ge(s["vs"].sem, s["vs"].now(b, 2 * gr + 2))
                        if gr == 0:
                            pe.wait_ge(s["qk_lo"].sem, s["qk_lo"].now(b, 8))
                        elif gr == 1:
                            pe.wait_ge(s["route"].sem, s["route"].now(b, 1))
                        else:
                            pe.wait_ge(s["o_t"].sem, s["o_t"].now(b, gr - 1))
                    for k, (kb, q0, at) in enumerate(PV_AT):
                        n = T - q0
                        pe.wait_ge(s["p_lo"].sem, s["p_lo"].now(b, 2 * h + 1 + k // 2))
                        pe.matmul(bank[6 + par][:, q0:T], vs[:, par, kb, h % 4, :],
                                  p_hi[:, h % 2, at:at + n], start=h % 4 == 0 and k == 0,
                                  stop=False)
                        last = pe.matmul(bank[6 + par][:, q0:T], vs[:, par, kb, h % 4, :],
                                         p_lo[:, h % 2, at:at + n], start=False,
                                         stop=h % 4 == 3 and k == 3)
                    last.then_inc(s["pv"].sem, 1)

                per_block(wv[:, :], D, "v_ps")
                for n in range(3, 8):
                    queries_keys(b, n)
                pe.wait_ge(s["v_f"].sem, s["v_f"].now(b, 1))
                per_block(wr[:, :], E8, "lg_ps")
                for h in range(4):
                    max_scores(h)
                transpose_max(0)
                max_scores(4)
                for h in range(H):
                    scores(h)
                    if h + AHEAD_MAX < H:
                        max_scores(h + AHEAD_MAX)
                    if h:
                        times_values(h - 1)
                    if h % 4 == 2 and h + 4 < H:
                        transpose_max(h // 4 + 1)

                def up(n):
                    if n >= 3:
                        pe.wait_ge(s["hid"].sem, s["hid"].now(b, n - 2))
                    else:
                        pe.wait_ge(s["probs"].sem, s["probs"].now(b, 48))
                    c = slice(n * P, (n + 1) * P)
                    product3(pe, bank[n % 3][:, :], wup_hi[:, c], wup_lo[:, c], m)\
                        .then_inc(s["up"].sem, 1)

                AHEAD = 3
                up(0)
                times_values(H - 1)
                for n in range(1, AHEAD):
                    up(n)
                pe.wait_ge(s["o_t"].sem, s["o_t"].now(b, 4))
                pe.matmul(bank[6][:, :], wo[:, 0, :], o_t[:, 0, :], start=True, stop=False)
                pe.matmul(bank[6][:, :], wo[:, 1, :], o_t[:, 1, :], start=False, stop=True)\
                    .then_inc(s["s_ps_out"].sem, 1)
                pe.wait_ge(s["route"].sem, s["route"].now(b, 16))
                for i in range(NB):
                    last = pe.transpose(bank[7][0:E8, i * P:(i + 1) * P], c_tok[:, i, :],
                                        g["ident"][:, :])
                last.then_inc(s["cT_ps"].sem, 1)

                def down(n):
                    e, f = n // FC, n % FC
                    pe.wait_ge(s["hid"].sem, s["hid"].now(b, n + 1))
                    if n == 0:
                        pe.wait_ge(w_down, 16)
                    if f == 0 and e >= 2:
                        pe.wait_ge(s["y_mul"].sem, s["y_mul"].now(b, e - 1))
                    elif n == 0:
                        pe.wait_ge(s["neg_max"].sem, s["neg_max"].now(b, 64))
                    pe.matmul(bank[3 + e % 2][:, :], wdn[:, e, f, :], hid[:, n % 3, :],
                              start=(f == 0), stop=(f == FC - 1)).then_inc(s["dn"].sem, 1)

                def spread(e):
                    if e:
                        pe.wait_ge(s["c_all"].sem, s["c_all"].now(b, e))
                    else:
                        pe.wait_ge(s["c_lo"].sem, s["c_lo"].now(b, 1))
                        pe.wait_ge(s["max_t"].sem, s["max_t"].now(b, 4))
                    pe.matmul(bank[5][:, :], select[:, e, :], c_t[:, :], start=True, stop=True)\
                        .then_inc(s["c_ps"].sem, 1)

                for n in range(NH):
                    if n >= AHEAD:
                        up(n)
                    if n % FC == 3:
                        spread(n // FC)
                    if n >= 2:
                        down(n - 2)
                    if n == 20:
                        prep_tensor(pe, s, m, b + 1, bank[7])
                down(NH - 2)
                down(NH - 1)
                first_queries_keys(b + 1)
                pe.wait_ge(s["upd"].sem, s["upd"].now(b, 1))
                for i in range(NB):
                    last = pe.transpose(bank[6][:, i * P:(i + 1) * P], upd[:, i * P:(i + 1) * P],
                                        g["ident"][:, :])
                last.then_inc(s["updT"].sem, 1)




E16 = 16
NE = E16 + 1
ROUTE_SCALE = 2.826
HW = HD + 1
UW = HW * D
UB = UW // 3
LIN = dict(qkv_ps=NB, e_qk=NB, v_one=NB, e_min=NB, phi=NB, u=NB, u_sum=2, s_ps=NB, w=NB, num=NB,
           den=NB, den_inv=NB, o=NB, oT_ps=1, oT=1, s_ps_out=1, s_t=1, gate=1, upd=1, x_new=1)


def linear_tiles(m, sb):
    m["e_qk"] = sb("e_qk", [P, NB, 2 * D], F32)
    m["phi"] = sb("phi", [P, NB, 2 * D], F32)
    m["v_one"] = sb("v_one", [P, NB, HW, H], F32)
    m["u"] = sb("u", [P, NB, UW], F32)
    m["u_sum"] = sb("u_sum", [P, 2, UW], F32)
    m["w"] = sb("w", [P, UW], F32)
    m["num"] = sb("num", [P, HW, H], F32)
    m["den"] = sb("den", [P, H], F32)
    m["den_inv"] = sb("den_inv", [P, H], F32)
    m["o"] = sb("o", [P, NB, D], F32)
    m["oT"] = sb("oT", [P, T], F32)
    m["s_t"] = sb("s_t", [P, T], F32)
    m["gate"] = sb("gate", [P, T], F32)
    m["upd"] = sb("upd", [P, T], F32)
    m["wqkv"] = sb("wqkv", [P, 3 * D], F32)
    m["wo"] = sb("wo", [P, D], F32)


def qkv_bank(bank, i):
    return bank[3 + i % 2]


def linear_scalar(act, s, m, b, i, bank):
    act.wait_ge(s["qkv_ps"].sem, s["qkv_ps"].now(b, i + 1))
    act.wait_ge(s["phi"].sem, s["phi"].before(b, i + 1))
    act.wait_ge(s["u"].sem, s["u"].before(b, i + 1))
    qkv = qkv_bank(bank, i)
    act.activation(m["e_qk"][:, i, :], qkv[:, 0:2 * D], ACT.Exp).then_inc(s["e_qk"].sem, 1)
    act.activation(m["v_one"][:, i, 0:HD, :].rearrange("p e h -> p h e"),
                   qkv[:, 2 * D:3 * D].rearrange("p (h e) -> p h e", h=H), ACT.Copy)\
        .then_inc(s["v_one"].sem, 1)


def linear_gpsimd_min(pool, s, m, b, i):
    pool.wait_ge(s["e_qk"].sem, s["e_qk"].now(b, i + 1))
    pool.sem_inc(m["passed"], 1)
    e = m["e_qk"][:, i, :]
    pool.tensor_scalar(e, e, 1.0, 0.0, ALU.min, ALU.max).then_inc(s["e_min"].sem, 1)


def linear_gpsimd_sum(pool, s, m, b, i):
    pool.wait_ge(s["u"].sem, s["u"].now(b, i + 1))
    if i == 1:
        pool.wait_ge(s["s_ps"].sem, s["s_ps"].before(b, NB))
    else:
        pool.wait_ge(s["u_sum"].sem, s["u_sum"].now(b, i - 1))
    older = m["u"][:, 0, :] if i == 1 else m["u_sum"][:, i - 2, :]
    pool.tensor_tensor(m["u_sum"][:, i - 1, :], older, m["u"][:, i, :], ALU.add)\
        .then_inc(s["u_sum"].sem, 1)


def linear_vector_phi(dve, s, m, b, i, bank):
    dve.wait_ge(s["e_min"].sem, s["e_min"].now(b, i + 1))
    dve.wait_ge(s["v_one"].sem, s["v_one"].now(b, i + 1))
    dve.wait_ge(s["w"].sem, s["w"].before(b, i + 1))
    dve.scalar_tensor_tensor(out=m["phi"][:, i, :], in0=qkv_bank(bank, i)[:, 0:2 * D],
                             scalar=0.0, in1=m["e_qk"][:, i, :], op0=ALU.max, op1=ALU.add)\
        .then_inc(s["phi"].sem, 1)


def linear_vector_u(dve, s, m, b, i):
    dve.wait_ge(s["phi"].sem, s["phi"].now(b, i + 1))
    dve.wait_ge(s["s_ps"].sem, s["s_ps"].before(b, NB))
    phi_k = m["phi"][:, i, D:2 * D].rearrange("p (h d) -> p h d", h=H)
    shape = [P, HW, H, HD]
    dve.tensor_tensor(m["u"][:, i, :].rearrange("p (e h d) -> p e h d", e=HW, h=H),
                      phi_k.unsqueeze(1).to_broadcast(shape),
                      m["v_one"][:, i, :, :].unsqueeze(3).to_broadcast(shape), ALU.mult)\
        .then_inc(s["u"].sem, 1)


def linear_vector_out(dve, s, m, b, i, psum, eps):
    dve.wait_ge(s["s_ps"].sem, s["s_ps"].now(b, i + 1))
    if i:
        dve.wait_ge(s["num"].sem, s["num"].now(b, i))
    else:
        dve.wait_ge(s["num"].sem, s["num"].before(b, NB))
    phi_q = m["phi"][:, i, 0:D].unsqueeze(1).unsqueeze(1).to_broadcast([P, 3, 3, D])
    dve.tensor_tensor(m["w"][:, :].rearrange("p (k e x) -> p k e x", k=3, e=3),
                      psum[:, 0:3, 0:UB].rearrange("p k (e x) -> p k e x", e=3),
                      phi_q, ALU.mult).then_inc(s["w"].sem, 1)
    dve.wait_ge(s["w"].sem, s["w"].now(b, i + 1))
    dve.tensor_reduce(m["num"][:, :, :],
                      m["w"][:, :].rearrange("p (e h d) -> p e h d", e=HW, h=H), AX.X, ALU.add)\
        .then_inc(s["num"].sem, 1)
    dve.wait_ge(s["num"].sem, s["num"].now(b, i + 1))
    dve.tensor_scalar(m["den"][:, :], m["num"][:, HD, :], eps, None, ALU.add)\
        .then_inc(s["den"].sem, 1)
    dve.wait_ge(s["den"].sem, s["den"].now(b, i + 1))
    dve.reciprocal(m["den_inv"][:, :], m["den"][:, :]).then_inc(s["den_inv"].sem, 1)
    dve.wait_ge(s["den_inv"].sem, s["den_inv"].now(b, i + 1))
    if i == 0:
        dve.wait_ge(s["oT_ps"].sem, s["oT_ps"].before(b, 1))
    dve.tensor_tensor(m["o"][:, i, :].rearrange("p (h e) -> p e h", h=H), m["num"][:, 0:HD, :],
                      m["den_inv"][:, :].unsqueeze(1).to_broadcast([P, HD, H]), ALU.mult)\
        .then_inc(s["o"].sem, 1)


def linear_tensor_qkv(pe, s, m, b, i, bank):
    if i >= 2:
        pe.wait_ge(s["phi"].sem, s["phi"].now(b, i - 1))
    pe.matmul(qkv_bank(bank, i)[:, 0:3 * D], m["xnT"][:, i * P:(i + 1) * P], m["wqkv"][:, :],
              start=True, stop=True).then_inc(s["qkv_ps"].sem, 1)


def linear_tensor_sums(pe, s, m, b, i, bank):
    pe.wait_ge(s["u"].sem, s["u"].now(b, i + 1))
    if i >= 2:
        pe.wait_ge(s["u_sum"].sem, s["u_sum"].now(b, i - 1))
    if i:
        pe.wait_ge(s["w"].sem, s["w"].now(b, i))
    for k in range(3):
        c = slice(UB * k, UB * (k + 1))
        last = pe.matmul(bank[k][:, 0:UB], m["tri"][:, :], m["u"][:, i, c],
                         start=True, stop=i == 0)
        if i:
            older = m["u"][:, 0, c] if i == 1 else m["u_sum"][:, i - 2, c]
            last = pe.matmul(bank[k][:, 0:UB], m["ones"][:, :], older, start=False, stop=True)
    last.then_inc(s["s_ps"].sem, 1)


def linear_tensor_oT(pe, s, m, b, bank):
    pe.wait_ge(s["phi"].sem, s["phi"].now(b, NB))
    for i in range(NB):
        pe.wait_ge(s["o"].sem, s["o"].now(b, i + 1))
        last = pe.transpose(bank[3][:, i * P:(i + 1) * P], m["o"][:, i, :], m["ident"][:, :])
    last.then_inc(s["oT_ps"].sem, 1)


def linear_moe_layer(nc, layer, g, d):
    with ExitStack() as ctx:
        sems = Semaphores(nc, ctx)

        def sb(name, shape, dt):
            return ctx.enter_context(nc.sbuf_tensor(f"{name}_{layer}", shape, dt))

        m = dict(g)
        prep_tiles(m, sb)
        linear_tiles(m, sb)
        bank, psum = g["bank"], g["psum"]
        wup_hi = sb("wup_hi", [P, NE, 2, P], F32R)
        wup_lo = sb("wup_lo", [P, NE, 2, P], F32R)
        wdn = sb("wdn", [P, NE, D], F32)
        stage = sb("stage", [P, 4, 2 * P], F32)
        select_raw = sb("select_raw", [64, E16 * P], F32)
        select = sb("select", [64, E16, P], F32R)
        wr = sb("wr", [P, E16], F32)
        rbias = sb("rbias", [P, E16], F32)
        lg_exp = sb("lg_exp", [P, NB, E16], F32)
        lg_one = sb("lg_one", [P, NB, E16], F32)
        score = sb("score", [P, NB, E16], F32)
        biased = sb("biased", [P, NB, E16], F32)
        top = sb("top", [P, NB, 8], F32)
        rest = sb("rest", [P, NB, E16], F32)
        chosen = sb("chosen", [P, NB, E16], F32)
        c_raw = sb("c_raw", [P, NB, E16], F32)
        c_sum = sb("c_sum", [P, NB], F32)
        c_inv = sb("c_inv", [P, NB], F32)
        c_scaled = sb("c_scaled", [P, NB], F32)
        c_tok = sb("c_tok", [P, NB, E16], F32)
        c_t = sb("c_t", [64, T], F32R)
        silu = sb("silu", [P, 2, T], F32)
        c_all = sb("c_all", [P, 2, T], F32)
        hid_raw = sb("hid_raw", [P, 2, T], F32)
        hid = sb("hid", [P, 2, T], F32)
        s = signals(sems, layer, **PREP, **LIN, lg_ps=1, lg_exp=1, route=16, c_scaled=1, cT_ps=1,
                    c_hi=1, c_lo=1, gate_ps=NE, up=NE, silu=NE, c_ps=E16, c_all=E16, hid_raw=NE,
                    hid=E16, dn=NE, updT=1)
        setup = sems.new(f"setup_{layer}")
        m["passed"] = sems.new(f"passed_{layer}")
        w_small = sems.new(f"w_small_{layer}")
        w_stage = [sems.new(f"w_stage{i}_{layer}") for i in range(4)]
        w_hi = sems.new(f"w_hi_{layer}")
        w_lo = sems.new(f"w_lo_{layer}")
        w_down = sems.new(f"w_down_{layer}")
        small = [(m["wqkv"], d["wqkv"]), (m["wo"], d["wo"]), (wr, d["wr"]), (rbias, d["rbias"]),
                 (select_raw, d["select"])]
        N_SMALL = 16 * len(small)
        OT_AT = 8
        block = ctx.enter_context(nc.Block())

        def halves(w, e):
            return w[:, e, :, :].rearrange("p a c -> p (a c)")

        @block.sync
        def _(sync):
            for x in s.values():
                sync.sem_inc(x.sem, x.per)
            for tile, src in small:
                sync.dma_start(tile[:], src).then_inc(w_small, 16)
            for e in range(NE):
                if e >= 4:
                    sync.wait_ge(w_lo, e - 3)
                sync.dma_start(stage[:, e % 4, :], d["wup"][:, e * 2 * P:(e + 1) * 2 * P])\
                    .then_inc(w_stage[e % 4], 16)
            sync.dma_start(wdn[:], d["wdn"]).then_inc(w_down, 16)

        @block.gpsimd
        def _(pool):
            prep_gpsimd(pool, s, m, 0)
            pool.wait_ge(s["rstd"].sem, s["rstd"].now(0, 1))
            pool.memset(m["v_one"][:, :, :, :], 1.0).then_inc(setup, 1)
            pool.wait_ge(setup, 1)
            pool.memset(c_t[:, :].bitcast(F32), 0.0).then_inc(setup, 1)
            pool.wait_ge(setup, 2)
            with pool.Fori(0, B) as b:
                for i in range(NB):
                    linear_gpsimd_min(pool, s, m, b, i)
                linear_gpsimd_sum(pool, s, m, b, 1)
                linear_gpsimd_sum(pool, s, m, b, 2)
                prep_gpsimd(pool, s, m, b + 1)
                pool.wait_ge(s["gate"].sem, s["gate"].now(b, 1))
                pool.wait_ge(s["s_t"].sem, s["s_t"].now(b, 1))
                pool.wait_ge(s["updT"].sem, s["updT"].before(b, 1))
                pool.tensor_tensor(m["upd"][:, :], m["gate"][:, :], m["s_t"][:, :], ALU.mult)\
                    .then_inc(s["upd"].sem, 1)

        @block.scalar
        def _(act):
            act.preload_act_table_set(EXP_LN)
            prep_scalar(act, s, m, 0, bank[1], "xnT")
            prep_scalar(act, s, m, 0, bank[1], "xnT_hi")
            for e in range(NE):
                act.wait_ge(w_stage[e % 4], 16 * (e // 4 + 1))
                act.activation(halves(wup_hi, e), stage[:, e % 4, :], ACT.Copy).then_inc(w_hi, 1)
            act.wait_ge(setup, 2)

            with act.Fori(0, B) as b:
                def gate_silu(k):
                    act.wait_ge(s["gate_ps"].sem, s["gate_ps"].now(b, k + 1))
                    if k >= 2:
                        act.wait_ge(s["hid_raw"].sem, s["hid_raw"].now(b, k - 1))
                    else:
                        act.wait_ge(s["hid_raw"].sem, s["hid_raw"].before(b, NE - 1 + k))
                    act.activation(silu[:, k % 2, :], bank[5][:, :], ACT.Silu)\
                        .then_inc(s["silu"].sem, 1)

                def weights(k):
                    act.wait_ge(s["c_ps"].sem, s["c_ps"].now(b, k))
                    if k >= 3:
                        act.wait_ge(s["hid"].sem, s["hid"].now(b, k - 2))
                    else:
                        act.wait_ge(s["hid"].sem, s["hid"].before(b, E16 - 2 + k))
                    act.activation(c_all[:, k % 2, :], bank[7][:, :], ACT.Copy)\
                        .then_inc(s["c_all"].sem, 1)

                act.preload_act_table_set(EXP_LN)
                linear_scalar(act, s, m, b, 0, bank)
                act.wait_ge(s["lg_ps"].sem, s["lg_ps"].now(b, 1))
                act.activation(lg_exp[:, :, :],
                               bank[7][:, 0:NB * E16].rearrange("p (i e) -> p i e", i=NB),
                               ACT.Exp, scale=-1.0).then_inc(s["lg_exp"].sem, 1)
                for i in range(1, NB):
                    linear_scalar(act, s, m, b, i, bank)
                for k in range(NE):
                    if k == NE - 1:
                        prep_scalar(act, s, m, b + 1, bank[1], "xnT")
                    gate_silu(k)
                    if k == 0:
                        act.wait_ge(s["cT_ps"].sem, s["cT_ps"].now(b, 1))
                        act.wait_ge(s["c_ps"].sem, s["c_ps"].before(b, E16))
                        act.activation(c_t[0:E16, :], bank[7][0:E16, :], ACT.Copy)\
                            .then_inc(s["c_hi"].sem, 1)
                    else:
                        weights(k)
                    if k == OT_AT:
                        act.wait_ge(s["oT_ps"].sem, s["oT_ps"].now(b, 1))
                        act.activation(m["oT"][:, :], bank[3][:, :], ACT.Copy)\
                            .then_inc(s["oT"].sem, 1)
                    if k == OT_AT + 1:
                        act.wait_ge(s["s_ps_out"].sem, s["s_ps_out"].now(b, 1))
                        act.wait_ge(s["upd"].sem, s["upd"].before(b, 1))
                        act.activation(m["s_t"][:, :], bank[0][:, :], ACT.Copy)\
                            .then_inc(s["s_t"].sem, 1)
                act.wait_ge(s["up"].sem, s["up"].now(b, NE))
                prep_scalar(act, s, m, b + 1, bank[1], "xnT_hi")
                act.wait_ge(s["dn"].sem, s["dn"].now(b, NE))
                act.wait_ge(s["upd"].sem, s["upd"].before(b, 1))
                act.activation(m["gate"][:, :], bank[4][:, :], ACT.Silu)\
                    .then_inc(s["gate"].sem, 1)

        @block.vector
        def _(dve):
            prep_vector_stats(dve, s, m, 0)
            prep_vector_xn(dve, s, m, 0)
            prep_vector_lo(dve, s, m, 0)
            for e in range(NE):
                dve.wait_ge(w_hi, e + 1)
                dve.tensor_tensor(halves(wup_lo, e), stage[:, e % 4, :],
                                  halves(wup_hi, e).bitcast(F32), ALU.subtract).then_inc(w_lo, 1)
            dve.wait_ge(w_small, N_SMALL)
            dve.tensor_copy(select[:, :, :].rearrange("k e p -> k (e p)"), select_raw[:, :])\
                .then_inc(w_lo, 1)
            dve.wait_ge(setup, 2)
            with dve.Fori(0, B) as b:
                def route(n):
                    dve.wait_ge(s["route"].sem, s["route"].now(b, n))

                def done(ins):
                    ins.then_inc(s["route"].sem, 1)

                def router():
                    dve.wait_ge(s["lg_exp"].sem, s["lg_exp"].now(b, 1))
                    done(dve.tensor_scalar(lg_one[:, :, :], lg_exp[:, :, :], 1.0, None, ALU.add))
                    route(1)
                    done(dve.reciprocal(score[:, :, :], lg_one[:, :, :]))
                    route(2)
                    done(dve.tensor_tensor(biased[:, :, :], score[:, :, :],
                                           rbias[:, :].unsqueeze(1).to_broadcast([P, NB, E16]),
                                           ALU.add))
                    route(3)
                    dve.sem_inc(m["passed"], 1)
                    for i in range(NB):
                        done(dve.max(top[:, i, :], biased[:, i, :]))
                    route(7)
                    dve.sem_inc(m["passed"], 1)
                    for i in range(NB):
                        done(dve.match_replace(rest[:, i, :], top[:, i, :], biased[:, i, :], 3e38))
                    route(11)
                    done(dve.tensor_tensor(chosen[:, :, :], rest[:, :, :], biased[:, :, :],
                                           ALU.not_equal))
                    route(12)
                    done(dve.tensor_tensor(c_raw[:, :, :], score[:, :, :], chosen[:, :, :],
                                           ALU.mult))
                    route(13)
                    done(dve.tensor_reduce(c_sum[:, :], c_raw[:, :, :], AX.X, ALU.add))
                    route(14)
                    done(dve.reciprocal(c_inv[:, :], c_sum[:, :]))
                    route(15)
                    dve.tensor_scalar(c_scaled[:, :], c_inv[:, :], ROUTE_SCALE, None, ALU.mult)\
                        .then_inc(s["c_scaled"].sem, 1)
                    dve.wait_ge(s["c_scaled"].sem, s["c_scaled"].now(b, 1))
                    dve.wait_ge(s["cT_ps"].sem, s["cT_ps"].before(b, 1))
                    done(dve.tensor_tensor(c_tok[:, :, :], c_raw[:, :, :],
                                           c_scaled[:, :].unsqueeze(2).to_broadcast([P, NB, E16]),
                                           ALU.mult))

                def weights_lower():
                    dve.wait_ge(s["c_hi"].sem, s["c_hi"].now(b, 1))
                    dve.tensor_tensor(c_t[32:32 + E16, :], bank[7][0:E16, :],
                                      c_t[0:E16, :].bitcast(F32), ALU.subtract)\
                        .then_inc(s["c_lo"].sem, 1)

                def hidden(k):
                    dve.wait_ge(s["silu"].sem, s["silu"].now(b, k + 1))
                    dve.wait_ge(s["up"].sem, s["up"].now(b, k + 1))
                    if k == 0:
                        dve.wait_ge(s["dn"].sem, s["dn"].before(b, NE))
                    elif k < 3:
                        dve.wait_ge(s["hid"].sem, s["hid"].before(b, E16 - 2 + k))
                    else:
                        dve.wait_ge(s["hid"].sem, s["hid"].now(b, k - 2))
                    dve.tensor_tensor((hid_raw if k else hid)[:, k % 2, :], bank[6][:, :],
                                      silu[:, k % 2, :], ALU.mult).then_inc(s["hid_raw"].sem, 1)
                    if k:
                        dve.wait_ge(s["hid_raw"].sem, s["hid_raw"].now(b, k + 1))
                        dve.wait_ge(s["c_all"].sem, s["c_all"].now(b, k))
                        if k >= 2:
                            dve.wait_ge(s["dn"].sem, s["dn"].now(b, k - 1))
                        else:
                            dve.wait_ge(s["dn"].sem, s["dn"].before(b, NE))
                        dve.tensor_tensor(hid[:, k % 2, :], hid_raw[:, k % 2, :],
                                          c_all[:, k % 2, :], ALU.mult)\
                            .then_inc(s["hid"].sem, 1)

                def out(i):
                    linear_vector_out(dve, s, m, b, i, psum, 1e-6)

                linear_vector_phi(dve, s, m, b, 0, bank)
                linear_vector_u(dve, s, m, b, 0)
                linear_vector_phi(dve, s, m, b, 1, bank)
                router()
                linear_vector_phi(dve, s, m, b, 2, bank)
                linear_vector_phi(dve, s, m, b, 3, bank)
                hidden(0)
                linear_vector_u(dve, s, m, b, 1)
                weights_lower()
                out(0)
                hidden(1)
                linear_vector_u(dve, s, m, b, 2)
                linear_vector_u(dve, s, m, b, 3)
                hidden(2)
                out(1)
                hidden(3)
                hidden(4)
                out(2)
                hidden(5)
                hidden(6)
                out(3)
                for k in range(7, NE):
                    hidden(k)
                    if k == 9:
                        prep_vector_stats(dve, s, m, b + 1)
                    if k == 11:
                        prep_vector_xn(dve, s, m, b + 1)
                prep_vector_lo(dve, s, m, b + 1)
                dve.wait_ge(s["updT"].sem, s["updT"].now(b, 1))
                xb = g["x"][:, bass.ds(b * NB, NB), :]
                dve.tensor_tensor(xb, xb, bank[2][:, :].rearrange("p (i d) -> p i d", i=NB),
                                  ALU.add).then_inc(s["x_new"].sem, 1)

        @block.tensor
        def _(pe):
            prep_tensor(pe, s, m, 0, bank[1])
            pe.wait_ge(w_small, N_SMALL)
            pe.wait_ge(setup, 2)
            pe.wait_ge(w_lo, NE + 1)
            pe.wait_ge(w_down, 16)
            pe.wait_ge(s["xnT"].sem, s["xnT"].now(0, 1))
            linear_tensor_qkv(pe, s, m, 0, 0, bank)
            with pe.Fori(0, B) as b:
                def down(k):
                    if k == 0:
                        pe.wait_ge(s["phi"].sem, s["phi"].now(b, NB))
                        pe.wait_ge(s["hid_raw"].sem, s["hid_raw"].now(b, 1))
                    else:
                        pe.wait_ge(s["hid"].sem, s["hid"].now(b, k))
                    pe.matmul(bank[4][:, :], wdn[:, k, :], hid[:, k % 2, :], start=k == 0,
                              stop=k == NE - 1).then_inc(s["dn"].sem, 1)

                def expert(k):
                    if k:
                        pe.wait_ge(s["silu"].sem, s["silu"].now(b, k))
                    else:
                        pe.wait_ge(s["silu"].sem, s["silu"].before(b, NE))
                        pe.wait_ge(s["xnT_lo"].sem, s["xnT_lo"].now(b, 1))
                    product3(pe, bank[5][:, :], wup_hi[:, k, 0, :], wup_lo[:, k, 0, :], m)\
                        .then_inc(s["gate_ps"].sem, 1)
                    if k == 1:
                        pe.wait_ge(s["route"].sem, s["route"].now(b, 16))
                        for i in range(NB):
                            last = pe.transpose(bank[7][0:E16, i * P:(i + 1) * P],
                                                c_tok[:, i, :], g["ident"][:, :])
                        last.then_inc(s["cT_ps"].sem, 1)
                    if k:
                        if k == 1:
                            pe.wait_ge(s["c_lo"].sem, s["c_lo"].now(b, 1))
                        else:
                            pe.wait_ge(s["c_all"].sem, s["c_all"].now(b, k - 1))
                        pe.matmul(bank[7][:, :], select[:, k - 1, :], c_t[:, :], start=True,
                                  stop=True).then_inc(s["c_ps"].sem, 1)
                        pe.wait_ge(s["hid_raw"].sem, s["hid_raw"].now(b, k))
                    else:
                        pe.wait_ge(s["hid_raw"].sem, s["hid_raw"].before(b, NE))
                    product3(pe, bank[6][:, :], wup_hi[:, k, 1, :], wup_lo[:, k, 1, :], m)\
                        .then_inc(s["up"].sem, 1)
                    if k:
                        down(k - 1)

                pe.wait_ge(s["c_all"].sem, s["c_all"].before(b, E16))
                for i in range(NB):
                    last = pe.matmul(bank[7][:, i * E16:(i + 1) * E16],
                                     m["xnT"][:, i * P:(i + 1) * P], wr[:, :],
                                     start=True, stop=True)
                last.then_inc(s["lg_ps"].sem, 1)
                pe.wait_ge(s["gate"].sem, s["gate"].before(b, 1))
                linear_tensor_qkv(pe, s, m, b, 1, bank)
                linear_tensor_qkv(pe, s, m, b, 2, bank)
                expert(0)
                linear_tensor_qkv(pe, s, m, b, 3, bank)
                pe.wait_ge(s["xnT_hi"].sem, s["xnT_hi"].now(b, 1))
                pe.wait_ge(s["s_t"].sem, s["s_t"].before(b, 1))
                pe.wait_ge(s["x_new"].sem, s["x_new"].before(b, 1))
                linear_tensor_sums(pe, s, m, b, 0, bank)
                expert(1)
                linear_tensor_sums(pe, s, m, b, 1, bank)
                expert(2)
                expert(3)
                linear_tensor_sums(pe, s, m, b, 2, bank)
                expert(4)
                expert(5)
                linear_tensor_sums(pe, s, m, b, 3, bank)
                for k in range(6, NE):
                    expert(k)
                    if k == OT_AT:
                        linear_tensor_oT(pe, s, m, b, bank)
                    if k == OT_AT + 1:
                        pe.wait_ge(s["oT"].sem, s["oT"].now(b, 1))
                        pe.wait_ge(s["w"].sem, s["w"].now(b, NB))
                        pe.matmul(bank[0][:, :], m["wo"][:, :], m["oT"][:, :], start=True,
                                  stop=True).then_inc(s["s_ps_out"].sem, 1)
                    if k == 13:
                        prep_tensor(pe, s, m, b + 1, bank[1])
                down(NE - 1)
                pe.wait_ge(s["xnT"].sem, s["xnT"].now(b + 1, 1))
                linear_tensor_qkv(pe, s, m, b + 1, 0, bank)
                pe.wait_ge(s["upd"].sem, s["upd"].now(b, 1))
                for i in range(NB):
                    last = pe.transpose(bank[2][:, i * P:(i + 1) * P],
                                        m["upd"][:, i * P:(i + 1) * P], g["ident"][:, :])
                last.then_inc(s["updT"].sem, 1)


def linear_ternary_layer(nc, layer, g, d):
    with ExitStack() as ctx:
        sems = Semaphores(nc, ctx)

        def sb(name, shape, dt):
            return ctx.enter_context(nc.sbuf_tensor(f"{name}_{layer}", shape, dt))

        m = dict(g)
        prep_tiles(m, sb)
        linear_tiles(m, sb)
        bank, psum = g["bank"], g["psum"]
        bo = sb("bo", [P, D], F32)
        lnw = sb("lnw", [P, 4], F32)
        lnb = sb("lnb", [P, 4], F32)
        wfc_raw = sb("wfc_raw", [P, 4 * P], F32)
        wproj_raw = sb("wproj_raw", [P, 4 * P], F32)
        abs_sum = sb("abs_sum", [P, 2], F32)
        half_gamma = sb("half_gamma", [P, 2], F32)
        minus_half_gamma = sb("minus_half_gamma", [P, 2], F32)
        above = sb("above", [P, 2, 4 * P], F32)
        below = sb("below", [P, 2, 4 * P], F32)
        wfc = sb("wfc", [P, 4, P], F32R)
        wproj = sb("wproj", [P, 4, P], F32)
        lnb_all = sb("lnb_all", [P, 4, P], F32)
        wproj_scaled = sb("wproj_scaled", [P, 4, D], F32)
        ffn_bias = sb("ffn_bias", [P, D], F32)
        mean_w = sb("mean_w", [P, P], F32)
        hid = sb("hid", [P, 4, T], F32)
        cen = sb("cen", [P, 4, T], F32)
        sq = sb("sq", [P, 4, T], F32)
        var_eps_t = sb("var_eps_t", [P, NB], F32)
        rstd_t = sb("rstd_t", [P, NB], F32)
        z = sb("z", [P, NB, D], F32)
        s = signals(sems, layer, **PREP, **LIN, up=4, hid=4, mean_ps=1, cen=4, sq=4, var_ps=1,
                    var_eps_t=1, rstd_t=1, dn=1, z=4)
        setup = sems.new(f"setup_{layer}")
        m["passed"] = sems.new(f"passed_{layer}")
        w_small = sems.new(f"w_small_{layer}")
        ternary = sems.new(f"ternary_{layer}")
        gamma_ps = sems.new(f"gamma_ps_{layer}")
        small = [(m["wqkv"], d["wqkv"]), (m["wo"], d["wo"]), (bo, d["bo"]), (lnw, d["lnw"]),
                 (lnb, d["lnb"]), (wfc_raw, d["wfc"]), (wproj_raw, d["wproj"])]
        N_SMALL = 16 * len(small)
        block = ctx.enter_context(nc.Block())

        @block.sync
        def _(sync):
            for x in s.values():
                sync.sem_inc(x.sem, x.per)
            for tile, src in small:
                sync.dma_start(tile[:], src).then_inc(w_small, 16)

        @block.gpsimd
        def _(pool):
            prep_gpsimd(pool, s, m, 0)
            pool.wait_ge(s["rstd"].sem, s["rstd"].now(0, 1))
            pool.memset(m["v_one"][:, :, :, :], 1.0).then_inc(setup, 1)
            pool.wait_ge(setup, 1)
            pool.memset(mean_w[:, :], 1.0 / (4 * P)).then_inc(setup, 1)
            pool.wait_ge(setup, 2)
            with pool.Fori(0, B) as b:
                for i in range(NB):
                    linear_gpsimd_min(pool, s, m, b, i)
                linear_gpsimd_sum(pool, s, m, b, 1)
                linear_gpsimd_sum(pool, s, m, b, 2)
                prep_gpsimd(pool, s, m, b + 1)
                pool.wait_ge(s["var_eps_t"].sem, s["var_eps_t"].now(b, 1))
                pool.wait_ge(s["z"].sem, s["z"].before(b, 4))
                pool.tensor_tensor(rstd_t[:, :], var_eps_t[:, :], m["minus_half"][:, :],
                                   ALU.pow).then_inc(s["rstd_t"].sem, 1)
                pool.wait_ge(s["gate"].sem, s["gate"].now(b, 1))
                pool.wait_ge(s["s_t"].sem, s["s_t"].now(b, 1))
                pool.wait_ge(s["x_new"].sem, s["x_new"].before(b, 1))
                pool.tensor_tensor(m["upd"][:, :], m["gate"][:, :], m["s_t"][:, :], ALU.mult)\
                    .then_inc(s["upd"].sem, 1)

        @block.scalar
        def _(act):
            act.preload_act_table_set(EXP_LN)
            prep_scalar(act, s, m, 0, bank[6], "xnT")
            prep_scalar(act, s, m, 0, bank[6], "xnT_hi")
            act.wait_ge(setup, 2)
            with act.Fori(0, B) as b:
                for c in range(4):
                    act.wait_ge(s["up"].sem, s["up"].now(b, c + 1))
                    if c == 0:
                        act.wait_ge(s["cen"].sem, s["cen"].before(b, 4))
                    act.activation(hid[:, c, :], bank[4 + c][:, :], ACT.Gelu)\
                        .then_inc(s["hid"].sem, 1)
                act.preload_act_table_set(EXP_LN)
                for i in range(NB):
                    linear_scalar(act, s, m, b, i, bank)
                for c in range(4):
                    act.wait_ge(s["cen"].sem, s["cen"].now(b, c + 1))
                    if c == 0:
                        act.wait_ge(s["var_ps"].sem, s["var_ps"].before(b, 1))
                    act.activation(sq[:, c, :], cen[:, c, :], ACT.Square)\
                        .then_inc(s["sq"].sem, 1)
                prep_scalar(act, s, m, b + 1, bank[6], "xnT")
                prep_scalar(act, s, m, b + 1, bank[6], "xnT_hi")
                act.wait_ge(s["oT_ps"].sem, s["oT_ps"].now(b, 1))
                act.activation(m["oT"][:, :], bank[3][:, :], ACT.Copy).then_inc(s["oT"].sem, 1)
                act.wait_ge(s["upd"].sem, s["upd"].before(b, 1))
                act.wait_ge(s["z"].sem, s["z"].now(b, 4))
                act.activation(m["gate"][:, :], z[:, :, :].rearrange("p i d -> p (i d)"),
                               ACT.Silu).then_inc(s["gate"].sem, 1)

        def ternary_weights(dve):
            for n, w in enumerate((wfc_raw, wproj_raw)):
                dve.tensor_reduce(abs_sum[:, n:n + 1], w[:, :], AX.X, ALU.add,
                                  apply_absolute_value=True).then_inc(ternary, 1)
            dve.wait_ge(gamma_ps, 1)
            size = float(4 * P * D)
            dve.tensor_scalar(half_gamma[:, :], bank[0][:, 0:2], 0.5 / size, 0.5e-6, ALU.mult,
                              ALU.add).then_inc(ternary, 1)
            dve.wait_ge(ternary, 3)
            dve.tensor_scalar(minus_half_gamma[:, :], half_gamma[:, :], -1.0, None, ALU.mult)\
                .then_inc(ternary, 1)
            dve.wait_ge(ternary, 4)
            for n, w in enumerate((wfc_raw, wproj_raw)):
                dve.tensor_scalar(above[:, n, :], w[:, :], half_gamma[:, n:n + 1], None,
                                  ALU.is_gt).then_inc(ternary, 1)
                dve.tensor_scalar(below[:, n, :], w[:, :], minus_half_gamma[:, n:n + 1], None,
                                  ALU.is_lt).then_inc(ternary, 1)
            dve.wait_ge(ternary, 8)
            for n, w in enumerate((wfc, wproj)):
                dve.tensor_tensor(w[:, :, :].rearrange("p c f -> p (c f)"), above[:, n, :],
                                  below[:, n, :], ALU.subtract).then_inc(ternary, 1)
            dve.tensor_copy(lnb_all[:, :, :], lnb[:, :].unsqueeze(2).to_broadcast([P, 4, P]))\
                .then_inc(ternary, 1)
            dve.wait_ge(ternary, 10)
            for c in range(4):
                dve.tensor_scalar(wproj_scaled[:, c, :], wproj[:, c, :], lnw[:, c:c + 1], None,
                                  ALU.mult).then_inc(ternary, 1)
            dve.wait_ge(gamma_ps, 2)
            dve.tensor_copy(ffn_bias[:, :], bank[1][:, 0:D]).then_inc(ternary, 1)

        @block.vector
        def _(dve):
            prep_vector_stats(dve, s, m, 0)
            prep_vector_xn(dve, s, m, 0)
            prep_vector_lo(dve, s, m, 0)
            dve.wait_ge(w_small, N_SMALL)
            dve.wait_ge(setup, 2)
            ternary_weights(dve)
            with dve.Fori(0, B) as b:
                def centre():
                    dve.wait_ge(s["mean_ps"].sem, s["mean_ps"].now(b, 1))
                    dve.wait_ge(s["dn"].sem, s["dn"].before(b, 1))
                    dve.wait_ge(s["sq"].sem, s["sq"].before(b, 4))
                    for c in range(4):
                        dve.tensor_tensor(cen[:, c, :], hid[:, c, :], bank[7][:, :],
                                          ALU.subtract).then_inc(s["cen"].sem, 1)

                def ffn_out():
                    dve.wait_ge(s["dn"].sem, s["dn"].now(b, 1))
                    dve.wait_ge(s["rstd_t"].sem, s["rstd_t"].now(b, 1))
                    dve.wait_ge(s["gate"].sem, s["gate"].before(b, 1))
                    for i in range(NB):
                        dve.scalar_tensor_tensor(out=z[:, i, :],
                                                 in0=bank[4][:, i * P:(i + 1) * P],
                                                 scalar=rstd_t[:, i:i + 1], in1=ffn_bias[:, :],
                                                 op0=ALU.mult, op1=ALU.add)\
                            .then_inc(s["z"].sem, 1)

                linear_vector_phi(dve, s, m, b, 0, bank)
                linear_vector_u(dve, s, m, b, 0)
                linear_vector_phi(dve, s, m, b, 1, bank)
                linear_vector_u(dve, s, m, b, 1)
                linear_vector_phi(dve, s, m, b, 2, bank)
                linear_vector_phi(dve, s, m, b, 3, bank)
                linear_vector_u(dve, s, m, b, 2)
                linear_vector_out(dve, s, m, b, 0, psum, 1e-5)
                linear_vector_u(dve, s, m, b, 3)
                centre()
                prep_vector_stats(dve, s, m, b + 1)
                linear_vector_out(dve, s, m, b, 1, psum, 1e-5)
                prep_vector_xn(dve, s, m, b + 1)
                linear_vector_out(dve, s, m, b, 2, psum, 1e-5)
                dve.wait_ge(s["var_ps"].sem, s["var_ps"].now(b, 1))
                dve.wait_ge(s["rstd_t"].sem, s["rstd_t"].before(b, 1))
                dve.tensor_scalar(var_eps_t[:, :], bank[5][:, 0:NB], LN_EPS, None, ALU.add)\
                    .then_inc(s["var_eps_t"].sem, 1)
                linear_vector_out(dve, s, m, b, 3, psum, 1e-5)
                ffn_out()
                prep_vector_lo(dve, s, m, b + 1)
                dve.wait_ge(s["s_ps_out"].sem, s["s_ps_out"].now(b, 1))
                dve.wait_ge(s["upd"].sem, s["upd"].before(b, 1))
                dve.tensor_tensor(m["s_t"][:, :].rearrange("p (i d) -> p i d", i=NB),
                                  bank[0][:, :].rearrange("p (i d) -> p i d", i=NB),
                                  bo[:, :].unsqueeze(1).to_broadcast([P, NB, D]), ALU.add)\
                    .then_inc(s["s_t"].sem, 1)
                dve.wait_ge(s["upd"].sem, s["upd"].now(b, 1))
                xb = g["x"][:, bass.ds(b * NB, NB), :]
                dve.tensor_tensor(xb, xb, m["upd"][:, :].rearrange("p (i d) -> p i d", i=NB),
                                  ALU.add).then_inc(s["x_new"].sem, 1)

        @block.tensor
        def _(pe):
            prep_tensor(pe, s, m, 0, bank[6])
            pe.wait_ge(w_small, N_SMALL)
            pe.wait_ge(setup, 2)
            pe.wait_ge(ternary, 2)
            pe.matmul(bank[0][:, 0:2], g["ones"][:, :], abs_sum[:, :], start=True, stop=True)\
                .then_inc(gamma_ps, 1)
            pe.wait_ge(ternary, 11)
            for c in range(4):
                last = pe.matmul(bank[1][:, 0:D], lnb_all[:, c, :], wproj[:, c, :],
                                 start=c == 0, stop=c == 3)
            last.then_inc(gamma_ps, 1)
            pe.wait_ge(ternary, 16)
            with pe.Fori(0, B) as b:
                pe.wait_ge(s["xnT"].sem, s["xnT"].now(b, 1))
                pe.wait_ge(s["oT"].sem, s["oT"].before(b, 1))
                linear_tensor_qkv(pe, s, m, b, 0, bank)
                pe.wait_ge(s["xnT_lo"].sem, s["xnT_lo"].now(b, 1))
                for c in range(4):
                    if c == 0:
                        pe.wait_ge(s["z"].sem, s["z"].before(b, 4))
                    pe.matmul(bank[4 + c][:, :], wfc[:, c, :], m["xnT_hi"][:, :], start=True,
                              stop=False)
                    pe.matmul(bank[4 + c][:, :], wfc[:, c, :], m["xnT_lo"][:, :], start=False,
                              stop=True).then_inc(s["up"].sem, 1)
                pe.wait_ge(s["hid"].sem, s["hid"].now(b, 1))
                linear_tensor_qkv(pe, s, m, b, 1, bank)
                pe.wait_ge(s["s_t"].sem, s["s_t"].before(b, 1))
                pe.wait_ge(s["hid"].sem, s["hid"].now(b, 4))
                for c in range(4):
                    last = pe.matmul(bank[7][:, :], mean_w[:, :], hid[:, c, :],
                                     start=c == 0, stop=c == 3)
                last.then_inc(s["mean_ps"].sem, 1)
                linear_tensor_qkv(pe, s, m, b, 2, bank)
                linear_tensor_sums(pe, s, m, b, 0, bank)
                linear_tensor_qkv(pe, s, m, b, 3, bank)
                linear_tensor_sums(pe, s, m, b, 1, bank)
                pe.wait_ge(s["phi"].sem, s["phi"].now(b, NB))
                pe.wait_ge(s["cen"].sem, s["cen"].now(b, 4))
                for i in range(NB):
                    for c in range(4):
                        last = pe.matmul(bank[4][:, i * P:(i + 1) * P],
                                         cen[:, c, i * P:(i + 1) * P], wproj_scaled[:, c, :],
                                         start=c == 0, stop=c == 3)
                last.then_inc(s["dn"].sem, 1)
                linear_tensor_sums(pe, s, m, b, 2, bank)
                pe.wait_ge(s["sq"].sem, s["sq"].now(b, 4))
                for i in range(NB):
                    for c in range(4):
                        last = pe.matmul(bank[5][:, i:i + 1], sq[:, c, i * P:(i + 1) * P],
                                         mean_w[:, 0:1], start=c == 0, stop=c == 3)
                last.then_inc(s["var_ps"].sem, 1)
                prep_tensor(pe, s, m, b + 1, bank[6])
                linear_tensor_sums(pe, s, m, b, 3, bank)
                linear_tensor_oT(pe, s, m, b, bank)
                pe.wait_ge(s["oT"].sem, s["oT"].now(b, 1))
                pe.wait_ge(s["w"].sem, s["w"].now(b, NB))
                for i in range(NB):
                    c = slice(i * P, (i + 1) * P)
                    last = pe.matmul(bank[0][:, c], m["oT"][:, c], m["wo"][:, :], start=True,
                                     stop=True)
                last.then_inc(s["s_ps_out"].sem, 1)




def decay_table():
    k, q = np.arange(P)[:, None], np.arange(T)[None, :]
    delta = (q - k).astype(np.float64)
    t = np.where(delta > 0, -0.25 * np.log(np.maximum(delta, 1.0)) * np.sqrt(HD), 0.0)
    t = np.where(delta < 0, NEG, t)
    return np.concatenate([np.zeros((P, P)), t], 1).astype(np.float32)


def constants():
    p = np.arange(P)
    head = np.zeros((P, H), np.float32)
    for h in range(H):
        head[:96, h] = (p[:96] % 32) // HD == h % 4
        head[96 + h, h] = 1
    select = np.zeros((64, 16, P), np.float32)
    for e in range(16):
        select[e, e] = select[32 + e, e] = 1
    return {
        "c_ident": np.eye(P, dtype=np.float32),
        "c_causal_q": np.where(p[None, :] > p[:, None], NEG, 0).astype(np.float32),
        "c_causal_k": np.where(p[:, None] > p[None, :], NEG, 0).astype(np.float32),
        "c_head_mask": head,
        "l0_select": select.reshape(64, -1),
        "l1_select": select[:, :E8].reshape(64, -1),
        "l3_select": select[:, :E8].reshape(64, -1),
        "c_decay": decay_table(),
        "c_tri": (p[:, None] <= p[None, :]).astype(np.float32),
    }


def load_constants(nc, ctx, dram):
    def sb(name, shape, dt):
        return ctx.enter_context(nc.sbuf_tensor(name, shape, dt))

    psum = ctx.enter_context(nc.psum_tensor("psum", [P, 8, 512], F32))
    g = {"psum": psum, "bank": [psum[:, i, :] for i in range(8)]}
    g["x"] = sb("x_res", [P, (B + 1) * NB, D], F32)
    g["ident"] = sb("ident", [P, P], F32)
    g["ident_r"] = sb("ident_r", [P, P], F32R)
    g["ident_bf"] = sb("ident_bf", [P, P], BF16)
    g["causal_q"] = sb("causal_q", [P, P], BF16)
    g["causal_k"] = sb("causal_k", [P, P], BF16)
    g["head_mask"] = sb("head_mask", [P, H], F32)
    g["tri"] = sb("tri", [P, P], F32)
    g["ones"] = sb("ones", [P, P], F32)
    g["minus_half"] = sb("minus_half", [P, NB], F32)
    if 3 in LAYERS:
        g["decay_hi"] = sb("decay_hi", [P, P + T], F32R)
        g["decay_lo"] = sb("decay_lo", [P, P + T], F32R)
    with ExitStack() as tmp:
        raw = tmp.enter_context(nc.sbuf_tensor("raw_mask", [P, 2, P], F32))
        raw_dec = tmp.enter_context(nc.sbuf_tensor("raw_decay", [P, P + T], F32))
        consts = nc.alloc_semaphore(name="consts")
        x_in = nc.alloc_semaphore(name="x_in")
        narrowed = nc.alloc_semaphore(name="narrowed")
        block = tmp.enter_context(nc.Block())
        loads = [(g["ident"][:, :], dram["c_ident"]), (raw[:, 0, :], dram["c_causal_q"]),
                 (raw[:, 1, :], dram["c_causal_k"]), (g["head_mask"][:, :], dram["c_head_mask"]),
                 (raw_dec[:, :], dram["c_decay"]), (g["tri"][:, :], dram["c_tri"])]

        @block.sync
        def _(sync):
            for tile, src in loads:
                sync.dma_start(tile, src).then_inc(consts, 16)
            sync.wait_ge(consts, 16 * len(loads))
            sync.wait_ge(x_in, 16 * B)

        @block.scalar
        def _(act):
            x_blocks = dram["L0_attn_x"].rearrange("(t p) d -> p t d", p=P)
            for b in range(B):
                act.dma_start(g["x"][:, b * NB:(b + 1) * NB, :],
                              x_blocks[:, b * NB:(b + 1) * NB, :]).then_inc(x_in, 16)

        @block.gpsimd
        def _(pool):
            pool.memset(g["ones"][:, :], 1.0)
            pool.memset(g["minus_half"][:, :], -0.5)
            pool.memset(g["x"][:, B * NB:(B + 1) * NB, :], 0.0)

        @block.vector
        def _(dve):
            dve.wait_ge(consts, 16 * len(loads))
            dve.tensor_copy(g["ident_bf"][:, :], g["ident"][:, :])
            dve.tensor_copy(g["ident_r"][:, :], g["ident"][:, :])
            dve.tensor_copy(g["causal_q"][:, :], raw[:, 0, :])
            dve.tensor_copy(g["causal_k"][:, :], raw[:, 1, :])
            if 3 in LAYERS:
                dve.tensor_copy(g["decay_hi"][:, :], raw_dec[:, :]).then_inc(narrowed, 1)
                dve.wait_ge(narrowed, 1)
                dve.tensor_tensor(g["decay_lo"][:, :], raw_dec[:, :],
                                  g["decay_hi"][:, :].bitcast(F32), ALU.subtract)
    return g


def store_x(nc, g, out):
    with ExitStack() as ctx:
        stored = nc.alloc_semaphore(name="stored")
        block = ctx.enter_context(nc.Block())

        @block.sync
        def _(sync):
            blocks = out.rearrange("(t p) d -> p t d", p=P)
            for b in range(B):
                sync.dma_start(blocks[:, b * NB:(b + 1) * NB, :],
                               g["x"][:, b * NB:(b + 1) * NB, :]).then_inc(stored, 16)
            sync.wait_ge(stored, 16 * B)


LAYERS = (0, 1, 2, 3)
LAYER = {0: linear_moe_layer, 1: softmax_layer, 2: linear_ternary_layer, 3: softmax_layer}


def build(nc, dram, out):
    with ExitStack() as ctx:
        g = load_constants(nc, ctx, dram)
        for layer in LAYERS:
            ops = {k.split("_", 1)[1]: v for k, v in dram.items() if k.startswith(f"l{layer}_")}
            LAYER[layer](nc, layer, g, ops)
        store_x(nc, g, out)


def lay_out(a):
    c = np.ascontiguousarray
    r = {"L0_attn_x": a["L0_attn_x"].reshape(B * T, D)}

    def four(w):
        return np.tile(w.reshape(D, 4, 1, 32), (1, 1, 4, 1)).reshape(D, 4, P)

    def out_rows(w):
        return np.tile(w.reshape(2, 8, 1, HD, D), (1, 1, 2, 1, 1)).reshape(2, P, D)\
            .transpose(1, 0, 2)

    def rows(v):
        return c(np.broadcast_to(v[None, :], (P, v.shape[0])))

    r["l0_wqkv"] = c(a["L0_attn_w_attn"].T)
    r["l0_wo"] = c(a["L0_attn_w_proj"].T)
    r["l0_wr"] = c(a["L0_ffn_gate_w"].T)
    r["l0_rbias"] = rows(a["L0_ffn_expert_bias"])
    gate = np.concatenate([a["L0_ffn_shared_gate_w"][None], a["L0_ffn_w_gate"]])
    up = np.concatenate([a["L0_ffn_shared_up_w"][None], a["L0_ffn_w_up"]])
    down = np.concatenate([a["L0_ffn_shared_down_w"][None], a["L0_ffn_w_down"]])
    r["l0_wup"] = c(np.stack([gate, up], 1).transpose(3, 0, 1, 2).reshape(D, -1))
    r["l0_wdn"] = c(down.transpose(2, 0, 1))
    qkv, bias = a["L1_attn_qkv_w"], a["L1_attn_qkv_b"]
    r["l1_wqk"] = c(np.stack([four(qkv[:, :D]), four(qkv[:, D:2 * D])], 1).reshape(D, -1))
    r["l1_bqk"] = c(np.stack([four(np.broadcast_to(v, (D, D)))[0].T
                              for v in (bias[:D], bias[D:2 * D])], 1))
    r["l1_wv"] = c(qkv[:, 2 * D:])
    r["l1_bv"] = rows(bias[2 * D:])
    r["l1_wo"], r["l1_bo"] = out_rows(a["L1_attn_out_w"]), c(a["L1_attn_out_b"][:, None])
    r["l1_wr"] = c(a["L1_ffn_Wg"].T)
    r["l1_wup"] = c(a["L1_ffn_W1"].transpose(1, 0, 2).reshape(D, -1))
    r["l1_wdn"] = c(a["L1_ffn_W2"].reshape(E8, FC, P, D).transpose(2, 0, 1, 3))
    r["l2_wqkv"] = c(np.concatenate([a[f"L2_attn_W{n}"].T for n in "qkv"], 1))
    r["l2_wo"], r["l2_bo"] = c(a["L2_attn_Wo"].T), rows(a["L2_attn_bo"])
    r["l2_wfc"] = c(a["L2_ffn_W_fc"].T)
    r["l2_wproj"] = c(a["L2_ffn_W_proj"].reshape(D, 4, P).transpose(2, 1, 0).reshape(P, -1))
    r["l2_lnw"] = c(a["L2_ffn_ln_w"].reshape(4, P).T)
    r["l2_lnb"] = c(a["L2_ffn_ln_b"].reshape(4, P).T)
    r["l3_wqk"] = c(np.stack([four(a["L3_attn_Wq"]), four(a["L3_attn_Wk"])], 1).reshape(D, -1))
    r["l3_bqk"] = c(np.stack([four(np.broadcast_to(v, (D, D)))[0].T
                              for v in (a["L3_attn_bq"], a["L3_attn_bk"])], 1))
    r["l3_wv"], r["l3_bv"] = a["L3_attn_Wv"], rows(a["L3_attn_bv"])
    r["l3_wo"], r["l3_bo"] = out_rows(a["L3_attn_Wo"]), c(a["L3_attn_bo"][:, None])
    r["l3_wr"] = c(a["L3_ffn_router_w"].T)
    r["l3_wup"] = c(a["L3_ffn_w1"].transpose(2, 0, 1).reshape(D, -1))
    r["l3_b1"] = c(a["L3_ffn_b1"].reshape(E8, FC, P).transpose(2, 0, 1))
    r["l3_wdn"] = c(a["L3_ffn_w2"].transpose(2, 0, 1).reshape(FC, P, E8, D).transpose(1, 2, 0, 3))
    r["l3_b2"] = c(a["L3_ffn_b2"].T)
    return {k: c(v) for k, v in {**r, **constants()}.items()}


def kernel(**inputs):
    import concourse.bacc as bacc
    from concourse.bass_utils import run_bass_kernel_spmd

    arrays = lay_out({k: np.asarray(v) for k, v in inputs.items()})
    nc = bacc.Bacc("TRN2", target_bir_lowering=False, num_devices=1)
    dram = {k: nc.dram_tensor(k, v.shape, mybir.dt.from_np(v.dtype), kind="ExternalInput").ap()
            for k, v in arrays.items()}
    out = nc.dram_tensor("x_out", (B * T, D), F32, kind="ExternalOutput").ap()
    build(nc, dram, out)
    r = run_bass_kernel_spmd(nc, [arrays], core_ids=[0])
    return r.results[0]["x_out"].reshape(B, T, D)
```
